# Optimizing a Trainium2 kernel written in Bass

```python
import numpy as np
import jax
import jax.numpy as jnp

def _softmax(x, axis=-1):
    return jax.nn.softmax(x, axis=axis)

def _gelu(x):
    return jax.nn.gelu(x, approximate=True)

def _silu(x):
    return jax.nn.silu(x)

def _sigmoid(x):
    return jax.nn.sigmoid(x)

def _layernorm(x, axis=-1, eps=1e-05):
    m = jnp.mean(x, axis=axis, keepdims=True)
    v = jnp.var(x, axis=axis, keepdims=True)
    return (x - m) / jnp.sqrt(v + eps)

def _scatter_add(tgt, idx, src, axis=0):
    return tgt.at[idx].add(src)

def _segment_sum(src, seg, n):
    return jax.ops.segment_sum(src, seg, n)
kernel_name = 'mk_adaln_ffn_d2_seqx_r8_821225'

def setup_inputs(seed: int=0):
    np.random.seed(seed)
    _w = jnp.asarray

    def _rec_inputs():
        import jax
        import jax.numpy as jnp
        _rk = jax.random.key(seed)
        x = -0.0002928 + 1 * jax.random.normal(jax.random.fold_in(_rk, 1), (2, 512, 128), jnp.float32)
        _lenS = 512 - jax.random.randint(jax.random.fold_in(_rk, 7), (2,), 0, max(1, 512 // 4) + 1, jnp.int32)
        _lenS2 = 512 - jax.random.randint(jax.random.fold_in(_rk, 8), (2,), 0, max(1, 512 // 4) + 1, jnp.int32)
        cond_256 = -0.106481 + 1.03144 * jax.random.normal(jax.random.fold_in(_rk, 11), (2, 32), jnp.float32)
        return (x, cond_256)
    x, cond_256 = _rec_inputs()

    def _L0_cond_setup():
        import jax, jax.numpy as jnp
        import numpy as np
        TOP_K = 2
        EPS = 1e-06
        B, S, H, G, E, M = (2, 256, 128, 32, 8, 256)
        key = jax.random.key(seed)
        ks = jax.random.split(key, 16)
        s_h = 1.0 / np.sqrt(H)
        s_g = 1.0 / np.sqrt(G)
        s_m = 1.0 / np.sqrt(M)
        return {'x': jax.random.normal(ks[0], (B, S, H), jnp.float32), 'genre_embed': jax.random.normal(ks[1], (B, 1, G), jnp.float32), 'rms_w': jnp.ones((H,), jnp.float32), 'wg_W': jax.random.normal(ks[2], (H, E), jnp.float32) * s_h, 'wg_b': jnp.zeros((E,), jnp.float32), 'gg_W': jax.random.normal(ks[3], (G, E), jnp.float32) * s_g, 'gg_b': jnp.zeros((E,), jnp.float32), 'W1': jax.random.normal(ks[4], (E, H, M), jnp.float32) * s_h, 'b1': jnp.zeros((E, M), jnp.float32), 'W2': jax.random.normal(ks[5], (E, M, M), jnp.float32) * s_m, 'b2': jnp.zeros((E, M), jnp.float32), 'W3': jax.random.normal(ks[6], (E, M, H), jnp.float32) * s_m, 'b3': jnp.zeros((E, H), jnp.float32)}
    _L0_cond_all = _L0_cond_setup()
    _L0_cond_in = {k: v for k, v in _L0_cond_all.items() if k in ('rms_w', 'wg_W', 'wg_b', 'gg_W', 'gg_b', 'W1', 'b1', 'W2', 'b2', 'W3', 'b3')}
    del _L0_cond_all

    def _L0_ffn_setup():
        import jax, jax.numpy as jnp
        import numpy as np
        import math
        D = 128
        H = 16
        E = 8
        TOPK = 2
        LAT = D // 2
        KPH = LAT // H
        HD = D // H

        def _forward(hs, q_w, q_b, k_w, k_b, v_w, v_b, o_w, o_b, router_w, router_b, w1, b1, w2, b2):
            B, S, _ = hs.shape
            Q = (hs @ q_w + q_b).reshape(B, S, H, HD).transpose(0, 2, 1, 3)
            K = (hs @ k_w + k_b).reshape(B, S, H, KPH).transpose(0, 2, 1, 3)
            V = (hs @ v_w + v_b).reshape(B, S, H, KPH).transpose(0, 2, 1, 3)
            scores = jnp.einsum('bhsk,bhtk->bhst', Q[..., :KPH], K) / math.sqrt(KPH)
            attn = jax.nn.softmax(scores, axis=-1)
            ao = jnp.einsum('bhst,bhtv->bhsv', attn, V)
            ao = ao.transpose(0, 2, 1, 3).reshape(B, S, H * KPH)
            ao = jnp.concatenate([ao, jnp.zeros((B, S, D - LAT), ao.dtype)], axis=-1)
            mla_out = ao @ o_w + o_b
            probs = jax.nn.softmax(mla_out @ router_w + router_b, axis=-1)
            topw, topi = jax.lax.top_k(probs, TOPK)
            topw = topw / (topw.sum(-1, keepdims=True) + 1e-08)
            combine = jnp.sum(jax.nn.one_hot(topi, E, dtype=probs.dtype) * topw[..., None], axis=-2)
            h1 = jnp.einsum('bsd,edf->ebsf', mla_out, w1) + b1[:, None, None, :]
            h1 = jax.nn.gelu(h1, approximate=False)
            h2 = jnp.einsum('ebsf,efd->ebsd', h1, w2) + b2[:, None, None, :]
            moe_out = jnp.einsum('bse,ebsd->bsd', combine, h2)
            return hs + 0.3 * moe_out
        key = jax.random.key(seed)
        ks = jax.random.split(key, 16)
        s = 0.02
        inp = {'hidden_states': jax.random.normal(ks[0], (2, 256, D), jnp.float32), 'q_w': jax.random.normal(ks[1], (D, D), jnp.float32) * s, 'q_b': jnp.zeros((D,), jnp.float32), 'k_w': jax.random.normal(ks[2], (D, LAT), jnp.float32) * s, 'k_b': jnp.zeros((LAT,), jnp.float32), 'v_w': jax.random.normal(ks[3], (D, LAT), jnp.float32) * s, 'v_b': jnp.zeros((LAT,), jnp.float32), 'o_w': jax.random.normal(ks[4], (D, D), jnp.float32) * s, 'o_b': jnp.zeros((D,), jnp.float32), 'router_w': jax.random.normal(ks[5], (D, E), jnp.float32) * s, 'router_b': jnp.zeros((E,), jnp.float32), 'w1': jax.random.normal(ks[6], (E, D, 2 * D), jnp.float32) * s, 'b1': jnp.zeros((E, 2 * D), jnp.float32), 'w2': jax.random.normal(ks[7], (E, 2 * D, D), jnp.float32) * s, 'b2': jnp.zeros((E, D), jnp.float32)}
        return inp
    _L0_ffn_all = _L0_ffn_setup()
    _L0_ffn_in = {k: v for k, v in _L0_ffn_all.items() if k in ('q_w', 'q_b', 'k_w', 'k_b', 'v_w', 'v_b', 'o_w', 'o_b', 'router_w', 'router_b', 'w1', 'b1', 'w2', 'b2')}
    del _L0_ffn_all

    def _L1_cond_setup():
        import jax, jax.numpy as jnp
        import numpy as np
        B, S, E, H, CD = (4, 128, 128, 16, 32)
        HD = E // H
        FIELD_COHERENCE = 0.7
        COH_THRESHOLD = 0.5
        FIELD_COUPLING = 0.3

        def _layernorm(x, g, b, eps=1e-05):
            mu = x.mean(-1, keepdims=True)
            var = ((x - mu) ** 2).mean(-1, keepdims=True)
            return (x - mu) * jax.lax.rsqrt(var + eps) * g + b
        key = jax.random.key(seed)
        ks = jax.random.split(key, 10)
        s = 0.02
        f32 = jnp.float32
        return {'x': jax.random.normal(ks[0], (B, S, E), f32), 'consciousness_state': jax.random.normal(ks[1], (B, CD), f32), 'Wqkv': jax.random.normal(ks[2], (3 * E, E), f32) * s, 'bqkv': jnp.zeros((3 * E,), f32), 'Wout': jax.random.normal(ks[3], (E, E), f32) * s, 'bout': jnp.zeros((E,), f32), 'Wc1': jax.random.normal(ks[4], (E, E + CD), f32) * s, 'bc1': jnp.zeros((E,), f32), 'Wc2': jax.random.normal(ks[5], (H, E), f32) * s, 'bc2': jnp.zeros((H,), f32), 'We1': jax.random.normal(ks[6], (E, CD), f32) * s, 'be1': jnp.zeros((E,), f32), 'We2': jax.random.normal(ks[7], (E, E), f32) * s, 'be2': jnp.zeros((E,), f32), 'ln_g': jnp.ones((E,), f32), 'ln_b': jnp.zeros((E,), f32)}
    _L1_cond_all = _L1_cond_setup()
    _L1_cond_in = {k: v for k, v in _L1_cond_all.items() if k in ('Wqkv', 'bqkv', 'Wout', 'bout', 'Wc1', 'bc1', 'Wc2', 'bc2', 'We1', 'be1', 'We2', 'be2', 'ln_g', 'ln_b')}
    del _L1_cond_all

    def _L1_ffn_setup():
        import math
        import jax, jax.numpy as jnp
        import numpy as np
        NUM_EXPERTS = 16
        TOP_K = 2
        CAPACITY_FACTOR = 1.25
        key = jax.random.key(seed)
        k1, k2, k3, k4 = jax.random.split(key, 4)
        d, dff, E = (128, 512, NUM_EXPERTS)
        x = jax.random.normal(k1, (4, 256, d), dtype=jnp.float32)
        router_w = jax.random.normal(k2, (E, d), dtype=jnp.float32) * d ** (-0.5)
        router_b = jnp.zeros((E,), dtype=jnp.float32)
        w1 = jax.random.normal(k3, (E, d, dff), dtype=jnp.float32) * 0.02
        b1 = jnp.zeros((E, dff), dtype=jnp.float32)
        w2 = jax.random.normal(k4, (E, dff, d), dtype=jnp.float32) * 0.02
        b2 = jnp.zeros((E, d), dtype=jnp.float32)
        return {'x': x, 'router_w': router_w, 'router_b': router_b, 'w1': w1, 'b1': b1, 'w2': w2, 'b2': b2}
    _L1_ffn_all = _L1_ffn_setup()
    _L1_ffn_in = {k: v for k, v in _L1_ffn_all.items() if k in ('router_w', 'router_b', 'w1', 'b1', 'w2', 'b2')}
    del _L1_ffn_all
    return {'x': x, 'cond_256': cond_256, 'L0_cond_rms_w': _L0_cond_in['rms_w'], 'L0_cond_wg_W': _L0_cond_in['wg_W'], 'L0_cond_wg_b': _L0_cond_in['wg_b'], 'L0_cond_gg_W': _L0_cond_in['gg_W'], 'L0_cond_gg_b': _L0_cond_in['gg_b'], 'L0_cond_W1': _L0_cond_in['W1'], 'L0_cond_b1': _L0_cond_in['b1'], 'L0_cond_W2': _L0_cond_in['W2'], 'L0_cond_b2': _L0_cond_in['b2'], 'L0_cond_W3': _L0_cond_in['W3'], 'L0_cond_b3': _L0_cond_in['b3'], 'L0_ffn_q_w': _L0_ffn_in['q_w'], 'L0_ffn_q_b': _L0_ffn_in['q_b'], 'L0_ffn_k_w': _L0_ffn_in['k_w'], 'L0_ffn_k_b': _L0_ffn_in['k_b'], 'L0_ffn_v_w': _L0_ffn_in['v_w'], 'L0_ffn_v_b': _L0_ffn_in['v_b'], 'L0_ffn_o_w': _L0_ffn_in['o_w'], 'L0_ffn_o_b': _L0_ffn_in['o_b'], 'L0_ffn_router_w': _L0_ffn_in['router_w'], 'L0_ffn_router_b': _L0_ffn_in['router_b'], 'L0_ffn_w1': _L0_ffn_in['w1'], 'L0_ffn_b1': _L0_ffn_in['b1'], 'L0_ffn_w2': _L0_ffn_in['w2'], 'L0_ffn_b2': _L0_ffn_in['b2'], 'L1_cond_Wqkv': _L1_cond_in['Wqkv'], 'L1_cond_bqkv': _L1_cond_in['bqkv'], 'L1_cond_Wout': _L1_cond_in['Wout'], 'L1_cond_bout': _L1_cond_in['bout'], 'L1_cond_Wc1': _L1_cond_in['Wc1'], 'L1_cond_bc1': _L1_cond_in['bc1'], 'L1_cond_Wc2': _L1_cond_in['Wc2'], 'L1_cond_bc2': _L1_cond_in['bc2'], 'L1_cond_We1': _L1_cond_in['We1'], 'L1_cond_be1': _L1_cond_in['be1'], 'L1_cond_We2': _L1_cond_in['We2'], 'L1_cond_be2': _L1_cond_in['be2'], 'L1_cond_ln_g': _L1_cond_in['ln_g'], 'L1_cond_ln_b': _L1_cond_in['ln_b'], 'L1_ffn_router_w': _L1_ffn_in['router_w'], 'L1_ffn_router_b': _L1_ffn_in['router_b'], 'L1_ffn_w1': _L1_ffn_in['w1'], 'L1_ffn_b1': _L1_ffn_in['b1'], 'L1_ffn_w2': _L1_ffn_in['w2'], 'L1_ffn_b2': _L1_ffn_in['b2']}

def reference(x, cond_256, L0_cond_rms_w, L0_cond_wg_W, L0_cond_wg_b, L0_cond_gg_W, L0_cond_gg_b, L0_cond_W1, L0_cond_b1, L0_cond_W2, L0_cond_b2, L0_cond_W3, L0_cond_b3, L0_ffn_q_w, L0_ffn_q_b, L0_ffn_k_w, L0_ffn_k_b, L0_ffn_v_w, L0_ffn_v_b, L0_ffn_o_w, L0_ffn_o_b, L0_ffn_router_w, L0_ffn_router_b, L0_ffn_w1, L0_ffn_b1, L0_ffn_w2, L0_ffn_b2, L1_cond_Wqkv, L1_cond_bqkv, L1_cond_Wout, L1_cond_bout, L1_cond_Wc1, L1_cond_bc1, L1_cond_Wc2, L1_cond_bc2, L1_cond_We1, L1_cond_be1, L1_cond_We2, L1_cond_be2, L1_cond_ln_g, L1_cond_ln_b, L1_ffn_router_w, L1_ffn_router_b, L1_ffn_w1, L1_ffn_b1, L1_ffn_w2, L1_ffn_b2):
    import jax
    import jax.numpy as jnp

    def _L0_cond_ref(x, genre_embed, rms_w, wg_W, wg_b, gg_W, gg_b, W1, b1, W2, b2, W3, b3):
        import jax, jax.numpy as jnp
        import numpy as np
        TOP_K = 2
        EPS = 1e-06
        E = W1.shape[0]
        var = jnp.mean(x * x, axis=-1, keepdims=True)
        xn = rms_w * (x * jax.lax.rsqrt(var + EPS))
        gate = xn @ wg_W + wg_b + (genre_embed @ gg_W + gg_b)
        gate_w = jax.nn.softmax(gate, axis=-1)
        topk_w, topk_i = jax.lax.top_k(gate_w, TOP_K)
        cw = jnp.sum(jax.nn.one_hot(topk_i, E, dtype=x.dtype) * topk_w[..., None], axis=-2)
        h1 = jax.nn.relu(jnp.einsum('bsh,ehm->bsem', x, W1) + b1)
        h2 = jax.nn.relu(jnp.einsum('bsem,emn->bsen', h1, W2) + b2)
        out_e = jnp.einsum('bsen,enh->bseh', h2, W3) + b3
        return jnp.einsum('bseh,bse->bsh', out_e, cw)

    def _L0_ffn_ref(hidden_states, q_w, q_b, k_w, k_b, v_w, v_b, o_w, o_b, router_w, router_b, w1, b1, w2, b2):
        import jax, jax.numpy as jnp
        import numpy as np
        import math
        D = 128
        H = 16
        E = 8
        TOPK = 2
        LAT = D // 2
        KPH = LAT // H
        HD = D // H

        def _forward(hs, q_w, q_b, k_w, k_b, v_w, v_b, o_w, o_b, router_w, router_b, w1, b1, w2, b2):
            B, S, _ = hs.shape
            Q = (hs @ q_w + q_b).reshape(B, S, H, HD).transpose(0, 2, 1, 3)
            K = (hs @ k_w + k_b).reshape(B, S, H, KPH).transpose(0, 2, 1, 3)
            V = (hs @ v_w + v_b).reshape(B, S, H, KPH).transpose(0, 2, 1, 3)
            scores = jnp.einsum('bhsk,bhtk->bhst', Q[..., :KPH], K) / math.sqrt(KPH)
            attn = jax.nn.softmax(scores, axis=-1)
            ao = jnp.einsum('bhst,bhtv->bhsv', attn, V)
            ao = ao.transpose(0, 2, 1, 3).reshape(B, S, H * KPH)
            ao = jnp.concatenate([ao, jnp.zeros((B, S, D - LAT), ao.dtype)], axis=-1)
            mla_out = ao @ o_w + o_b
            probs = jax.nn.softmax(mla_out @ router_w + router_b, axis=-1)
            topw, topi = jax.lax.top_k(probs, TOPK)
            topw = topw / (topw.sum(-1, keepdims=True) + 1e-08)
            combine = jnp.sum(jax.nn.one_hot(topi, E, dtype=probs.dtype) * topw[..., None], axis=-2)
            h1 = jnp.einsum('bsd,edf->ebsf', mla_out, w1) + b1[:, None, None, :]
            h1 = jax.nn.gelu(h1, approximate=False)
            h2 = jnp.einsum('ebsf,efd->ebsd', h1, w2) + b2[:, None, None, :]
            moe_out = jnp.einsum('bse,ebsd->bsd', combine, h2)
            return hs + 0.3 * moe_out
        return _forward(hidden_states, q_w, q_b, k_w, k_b, v_w, v_b, o_w, o_b, router_w, router_b, w1, b1, w2, b2)

    def _L1_cond_ref(x, consciousness_state, Wqkv, bqkv, Wout, bout, Wc1, bc1, Wc2, bc2, We1, be1, We2, be2, ln_g, ln_b):
        import jax, jax.numpy as jnp
        import numpy as np
        B, S, E, H, CD = (4, 128, 128, 16, 32)
        HD = E // H
        FIELD_COHERENCE = 0.7
        COH_THRESHOLD = 0.5
        FIELD_COUPLING = 0.3

        def _layernorm(x, g, b, eps=1e-05):
            mu = x.mean(-1, keepdims=True)
            var = ((x - mu) ** 2).mean(-1, keepdims=True)
            return (x - mu) * jax.lax.rsqrt(var + eps) * g + b
        Bb, Ss, Ee = x.shape
        qkv = (x @ Wqkv.T + bqkv).reshape(Bb, Ss, 3, H, HD).transpose(2, 0, 3, 1, 4)
        q, k, v = (qkv[0], qkv[1], qkv[2])
        attn = jax.nn.softmax(jnp.einsum('bhid,bhjd->bhij', q, k) / jnp.sqrt(jnp.float32(HD)), axis=-1)
        cs_exp = jnp.broadcast_to(consciousness_state[:, None, :], (Bb, Ss, CD))
        comb = jnp.concatenate([x, cs_exp], axis=-1)
        coh = jax.nn.sigmoid(jnp.tanh(comb @ Wc1.T + bc1) @ Wc2.T + bc2).transpose(0, 2, 1)
        mod = attn * coh[..., None]
        mod = mod / (mod.sum(-1, keepdims=True) + 1e-08)
        fp = _layernorm(jax.nn.relu(consciousness_state @ We1.T + be1) @ We2.T + be2, ln_g, ln_b)
        pos = jnp.arange(Ss, dtype=jnp.float32)
        inv = 10000.0 ** jnp.repeat(jnp.arange(0, Ee, 2, dtype=jnp.float32) / Ee, 2)
        pe = jnp.sin(pos[:, None] / inv[None, :])
        fa = jax.nn.softmax(jnp.einsum('be,se->bs', fp, pe), axis=-1)
        fi = FIELD_COUPLING * FIELD_COHERENCE
        mod = (1.0 - fi) * mod + fi * fa[:, None, :, None]
        out = jnp.einsum('bhij,bhjd->bhid', mod, v).transpose(0, 2, 1, 3).reshape(Bb, Ss, Ee)
        return out @ Wout.T + bout

    def _L1_ffn_ref(x, router_w, router_b, w1, b1, w2, b2):
        import math
        import jax, jax.numpy as jnp
        import numpy as np
        NUM_EXPERTS = 16
        TOP_K = 2
        CAPACITY_FACTOR = 1.25
        E, k = (NUM_EXPERTS, TOP_K)
        B, S, d = x.shape
        tokens = B * S
        capacity = max(1, int(math.ceil(CAPACITY_FACTOR * tokens * k / E)))
        x2d = x.reshape(tokens, d)
        logits = x2d @ router_w.T + router_b
        vals, idx = jax.lax.top_k(logits, k)
        gates = jax.nn.softmax(vals, axis=-1)
        flat_e = idx.reshape(-1)
        oh = (flat_e[:, None] == jnp.arange(E)[None, :]).astype(jnp.int32)
        pos = jnp.take_along_axis(jnp.cumsum(oh, axis=0) - 1, flat_e[:, None], axis=1)[:, 0]
        kept = pos < capacity
        kept2 = kept.reshape(tokens, k)
        denom = jnp.sum(gates * kept2, axis=-1, keepdims=True)
        gates = jnp.where(kept2, gates / (denom + 1e-09), 0.0)
        slot = flat_e * capacity + pos
        slot_safe = jnp.where(kept, slot, E * capacity)
        x_rep = jnp.repeat(x2d, k, axis=0)
        buf = jnp.zeros((E * capacity + 1, d), x.dtype).at[slot_safe].set(x_rep)
        packed = buf[:E * capacity].reshape(E, capacity, d)
        h = jax.nn.gelu(jnp.einsum('ecd,edf->ecf', packed, w1) + b1[:, None, :], approximate=False)
        expert_out = jnp.einsum('ecf,efd->ecd', h, w2) + b2[:, None, :]
        eflat = expert_out.reshape(E * capacity, d)
        gathered = eflat[jnp.clip(slot, 0, E * capacity - 1)]
        w = (gates.reshape(-1) * kept.astype(x.dtype))[:, None]
        out = (gathered * w).reshape(tokens, k, d).sum(axis=1)
        return out.reshape(B, S, d)
    x = x + _L0_ffn_ref(_L0_cond_ref(x, cond_256[:, None, :], L0_cond_rms_w, L0_cond_wg_W, L0_cond_wg_b, L0_cond_gg_W, L0_cond_gg_b, L0_cond_W1, L0_cond_b1, L0_cond_W2, L0_cond_b2, L0_cond_W3, L0_cond_b3), L0_ffn_q_w, L0_ffn_q_b, L0_ffn_k_w, L0_ffn_k_b, L0_ffn_v_w, L0_ffn_v_b, L0_ffn_o_w, L0_ffn_o_b, L0_ffn_router_w, L0_ffn_router_b, L0_ffn_w1, L0_ffn_b1, L0_ffn_w2, L0_ffn_b2)
    x = x + _L1_ffn_ref(_L1_cond_ref(x, cond_256, L1_cond_Wqkv, L1_cond_bqkv, L1_cond_Wout, L1_cond_bout, L1_cond_Wc1, L1_cond_bc1, L1_cond_Wc2, L1_cond_bc2, L1_cond_We1, L1_cond_be1, L1_cond_We2, L1_cond_be2, L1_cond_ln_g, L1_cond_ln_b), L1_ffn_router_w, L1_ffn_router_b, L1_ffn_w1, L1_ffn_b1, L1_ffn_w2, L1_ffn_b2)
    return x

_drawn_inputs = setup_inputs


def setup_inputs(seed=0):
    import zlib

    import numpy as np

    out = dict(_drawn_inputs(seed))
    spreads = {'L0_cond_rms_w': (1.0, 0.2),
     'L0_cond_wg_b': (0.0, 0.1),
     'L0_cond_gg_b': (0.0, 0.1),
     'L0_cond_b1': (0.0, 0.345),
     'L0_cond_b2': (0.0, 0.1),
     'L0_cond_b3': (0.0, 0.1),
     'L0_ffn_q_b': (0.0, 0.8),
     'L0_ffn_k_b': (0.0, 2.0),
     'L0_ffn_v_b': (0.0, 0.8),
     'L0_ffn_o_b': (0.0, 0.371),
     'L0_ffn_router_b': (0.0, 0.403),
     'L0_ffn_b1': (0.0, 0.8),
     'L0_ffn_b2': (0.0, 0.414),
     'L1_cond_bqkv': (0.0, 0.522),
     'L1_cond_bout': (0.0, 0.1),
     'L1_cond_bc1': (0.0, 2.0),
     'L1_cond_bc2': (0.0, 2.0),
     'L1_cond_be1': (0.0, 0.763),
     'L1_cond_be2': (0.0, 0.422),
     'L1_cond_ln_g': (1.0, 0.6),
     'L1_cond_ln_b': (0.0, 0.8),
     'L1_ffn_router_b': (0.0, 0.1),
     'L1_ffn_b1': (0.0, 0.8),
     'L1_ffn_b2': (0.0, 0.1)}
    factors = {'L0_ffn_q_w': 8.0,
     'L0_ffn_k_w': 8.0,
     'L0_ffn_v_w': 8.0,
     'L0_ffn_o_w': 8.0,
     'L0_ffn_router_w': 3.66,
     'L0_ffn_w1': 8.0,
     'L0_ffn_w2': 8.0,
     'L1_cond_Wqkv': 8.0,
     'L1_cond_Wc1': 64.0,
     'L1_cond_Wc2': 64.0,
     'L1_cond_We1': 5.954,
     'L1_cond_We2': 4.396,
     'L1_ffn_w1': 8.0,
     'L1_ffn_w2': 6.778}
    for name, (base, spread) in spreads.items():
        noise = np.random.default_rng([zlib.crc32(name.encode()), seed]).standard_normal(out[name].shape)
        drawn = base * np.exp(spread * noise) if base else spread * noise
        out[name] = jnp.asarray(drawn.astype(out[name].dtype))
    for name, factor in factors.items():
        out[name] = (out[name] * factor).astype(out[name].dtype)
    return out
```

```python
import concourse.bass as bass
from concourse import mybir
from contextlib import ExitStack

P = 128
B, S, D = 2, 512, 128
TPB = S // P
NT = B * TPB
EA, MA = 8, 256
EB, MB = 8, 256
EC, MC = 16, 512
CAP = 160
NSLOT = EC * CAP
NST = NSLOT // P
H = 16
HPG = 4
NG = H // HPG
SL = 32
VW = 16
HD = (4, 8)
FC = MC // P
CD = 32
FI = 0.3 * 0.7

EARLY = [("wg", EA), ("rms", 1), ("gg", EA), ("cond_rep", B * P), ("wg_b", EA), ("gg_b", EA),
         ("b1a", 2 * EA), ("b2a", 2 * EA), ("b3a", P), ("cond", B), ("iota", EC), ("ident", P)]
LATE = [("wqk0", P), ("bqk0", 1), ("wv0", H * HD[0]), ("bv0", H * HD[0]), ("wo0", P), ("bo0", 1),
        ("rb_w", EB), ("rb_b", EB), ("b1b", 2 * EB), ("b2b", P),
        ("wq1", P), ("wk1", P), ("wv1", P), ("bq1", 1), ("bk1", 1), ("bv1", P),
        ("wc1x", P), ("wc1c", P), ("bc1", 1), ("wc2", H), ("bc2", H),
        ("we1", P), ("be1", 1), ("we2", P), ("be2", P), ("ln_g", P), ("ln_b", P), ("pe", S),
        ("wout", P), ("bout_col", 1), ("bout", P), ("rc_w", EC), ("rc_b", EC),
        ("b1c", EC * FC), ("b2c", EC), ("before", P), ("ones", P), ("minus", 1)]


def places(fields):
    at, out = 0, {}
    for name, n in fields:
        out[name] = (at, at + n)
        at += n
    return out, at


EARLY_AT, EARLY_N = places(EARLY)
LATE_AT, LATE_N = places(LATE)


def build(nc, x_tok_d, xT_d, early_d, late_d, sel_d, wa_d, wb_d, wc_d, out_d):
    F32, F32R, BF16, U32 = mybir.dt.float32, mybir.dt.float32r, mybir.dt.bfloat16, mybir.dt.uint32
    ALU, ACT, AX = mybir.AluOpType, mybir.ActivationFunctionType, mybir.AxisListType
    ctx = ExitStack()
    with ctx:
        def sb(name, shape, dt=F32):
            return ctx.enter_context(nc.sbuf_tensor(name, shape, dt))

        def sem(name):
            return ctx.enter_context(nc.semaphore(name))

        packed_d = nc.dram_tensor("packed_rows", [NSLOT, D], F32, kind="Internal").ap()
        expert_d = nc.dram_tensor("expert_rows", [NSLOT, D], F32, kind="Internal").ap()

        x_tok = sb("x_tok", [P, NT, D])
        xT_yT = sb("xT_yT", [P, 2, B * S])
        xT, yT = xT_yT[:, 0, :], xT_yT[:, 1, :]
        mlaT = xT
        early = sb("early", [P, EARLY_N])
        late = sb("late", [P, LATE_N])
        sel = sb("sel", [P, NG, 4, P], F32R)
        wa = sb("wa", [P, EA, 4 * MA])
        wb = sb("wb", [P, EB, 2 * MB])
        wc_late = sb("wc_late", [P, EC // 2, 2 * MC])
        wc = [wa[:, e, :] if e < EC // 2 else wc_late[:, e - EC // 2, :] for e in range(EC)]
        ident_r = sb("ident_r", [P, P], F32R)
        wgs = sb("wgs", [P, EA])
        gbias = sb("gbias", [P, B, EA])
        ssq = sb("ssq", [P, NT])
        rstd = sb("rstd", [P, NT])
        lg = sb("lg", [P, NT, EC])
        pr = sb("pr", [P, NT, EC])
        rmx = sb("rmx", [P, NT])
        rsm = sb("rsm", [P, NT])
        top8 = sb("top8", [P, NT, 8])
        idx8 = sb("idx8", [P, NT, 8], U32)
        idxf = sb("idxf", [P, NT, 2])
        oh = sb("oh", [P, 2, NT, EC])
        cw = sb("cw", [P, NT, EA])
        c0 = sb("c0", [P, NT, D])
        y = c0
        work = sb("work", [P, 4608])
        moe = work[:, 0:NT * D].rearrange("p (t d) -> p t d", d=D)
        h1 = work[:, 1024:2048].rearrange("p (c s) -> p c s", c=2)
        h2 = work[:, 2048:3072].rearrange("p (c s) -> p c s", c=2)
        cwT = work[0:EA, 3072:4096]
        OT, aoT, tT = work[:, 3072:3584], work[:, 3584:4096], work[:, 4096:4608]
        cT = sb("cT", [P, S])
        qH = sb("qH", [P, S], F32R)
        qL = sb("qL", [P, S], F32R)
        kH = sb("kH", [P, S], F32R)
        kL = sb("kL", [P, S], F32R)
        vaug = sb("vaug", [P, 2, TPB, H, VW])
        Kp = sb("Kp", [P, 2, HPG, S], F32R)
        Qs = sb("Qs", [P, 2, S], F32R)
        Qm = sb("Qm", [P, 2, S], F32R)
        mx = sb("mx", [P, TPB, HPG])
        MP = sb("MP", [P, TPB, HPG, SL], F32R)
        E4 = sb("E4", [P, 4, 2, S])
        rden = sb("rden", [P, TPB, HPG])
        ao = sb("ao", [P, TPB, P])
        x1 = x_tok
        rT = sb("rT", [P, B])
        bc1c = sb("bc1c", [P, B])
        fz = sb("fz", [B, D])
        fst = sb("fst", [B, 6])
        fag = sb("fag", [B, 2])
        fsd = sb("fsd", [B, 4])
        fpT = sb("fpT", [P, B])
        fe = sb("fe", [B, S])
        faT = sb("faT", [P, TPB, B])
        coh = sb("coh", [P, TPB, H])
        coh2 = sb("coh2", [P, B, TPB, H])
        vsum = sb("vsum", [P, B, P])
        ohb = sb("ohb", [P, NT, EC], BF16)
        before_b = sb("before_b", [P, P], BF16)
        ones_b = sb("ones_b", [P, P], BF16)
        pos = sb("pos", [P, 2, NT])
        slot = sb("slot", [P, 2, NT])
        kept = sb("kept", [P, 2, NT])
        gate = sb("gate", [P, 2, NT])
        gden = sb("gden", [P, NT])
        put_at = sb("put_at", [P, 2, NT], U32)
        get_at = sb("get_at", [P, 2, NT], U32)
        flat = E4[:, :, :, :].rearrange("p a b c -> p (a b c)")
        pk_tok = flat[:, 0:NST * D].rearrange("p (t d) -> p t d", d=D)
        eoT = flat[:, 0:NSLOT]
        pkT = work[:, 0:NSLOT]
        hC = work[:, NSLOT:NSLOT + 2 * FC * CAP].rearrange("p (a c n) -> p a c n", a=2, c=FC)
        eo_tok = wb[:, :, :].rearrange("p e n -> p (e n)")[:, 0:NST * D].rearrange("p (t d) -> p t d", d=D)
        got = xT_yT[:, :, :].rearrange("p k (t d) -> p k t d", d=D)

        PS = ctx.enter_context(nc.psum_tensor("PS", [P, 8, 512], F32))
        SLOTS = {"m0": (0, 1), "m1": (1, 2), "s0": (2, 4), "s1": (4, 6), "pv": (6, 7), "mi": (7, 8)}
        full = {s: sem("full_" + s) for s in SLOTS}
        taken = {s: sem("taken_" + s) for s in SLOTS}

        def ps(s):
            a, b = SLOTS[s]
            return PS[:, a, :] if b == a + 1 else PS[:, a:b, :]

        x_in, xT_in, early_in, late_in, sel_in = (sem(n) for n in ("x_in", "xT_in", "early_in", "late_in", "sel_in"))
        wa_in = [sem(f"wa_in{e}") for e in range(EA)]
        wb_in = sem("wb_in")
        wc_in = [sem(f"wc_in{q}") for q in range(4)]
        ssq_done, var_done, sd_done = sem("ssq_done"), sem("var_done"), sem("sd_done")
        gate_w_ready = sem("gate_w_ready")
        shifted, expd = sem("logits_shifted"), sem("logits_expd")
        cw_ready, cwT_ready, c0_set = sem("cw_ready"), sem("cwT_ready"), sem("c0_set")
        c0_done = sem("c0_done")
        dve_chain = sem("dve_chain")
        field_rT, field_var, field_sd, field_fp = sem("field_rT"), sem("field_var"), sem("field_sd"), sem("field_fp")
        field_mx, field_exp, field_fa = sem("field_mx"), sem("field_exp"), sem("field_fa")
        H_done, L_done = sem("high_parts"), sem("low_parts")
        V_ready = sem("V_ready")
        stack_ready = sem("stack_ready")
        MP_ready, Qm_ready = sem("maxima_placed"), sem("Qm_ready")
        pv_read = sem("exps_used")
        ao_ready = sem("ao_ready")
        mla_ready = sem("mla_ready")
        moe_set, x1_ready = sem("moe_set"), sem("x1_ready")
        coh_z, coh_e = sem("coh_shifted"), sem("coh_expd")
        y_ready = sem("y_ready")
        consts_r, consts_b, clear0 = sem("ident_r_ready"), sem("bf16_consts"), sem("cleared")
        ohb_ready = sem("ohb_ready")
        gdiff, gexp = sem("gate_difference"), sem("gate_exp")
        put_ready, get_ready = sem("put_ready"), sem("get_ready")
        zeroed, putted, pk_in = sem("packed_zeroed"), sem("rows_put"), sem("packed_in")
        eo_ready, eo_out, got_in = sem("eo_ready"), sem("eo_out"), sem("rows_got")
        out_ready, out_done = sem("out_ready"), sem("out_done")
        zero_ready = sem("zero_ready")

        def ea(name):
            a, b = EARLY_AT[name]
            return early[:, a:b]

        def la(name):
            a, b = LATE_AT[name]
            return late[:, a:b]

        ident = ea("ident")

        filled_at = {}

        def wait_full(eng, key):
            s, n = filled_at[key]
            eng.wait_ge(full[s], n)
            return ps(s)

        def wait_taken(eng, key):
            s, n = filled_at[key]
            eng.wait_ge(taken[s], n)

        NAB = B * EA

        block = ctx.enter_context(nc.Block())

        @block.tensor
        def _(pe):
            fills = {s: 0 for s in SLOTS}
            mm = nc.tensor.matmul

            def claim(key, s):
                if fills[s]:
                    pe.wait_ge(taken[s], fills[s])
                fills[s] += 1
                filled_at[key] = (s, fills[s])
                return ps(s)

            def filled(last, key):
                last.then_inc(full[filled_at[key][0]], 1)

            def transposes(key, s, tiles, n=P, k=P):
                p = claim(key, s)
                for i, t in enumerate(tiles):
                    last = nc.tensor.transpose(p[0:n, i * P:i * P + k] if k == P else p[0:n, i * k:(i + 1) * k],
                                               t, ident[0:k, 0:k])
                filled(last, key)

            def field(step):
                if step == 0:
                    pe.wait_ge(late_in, 16)
                    p = claim("field0", "mi")
                    mm(p[:, 0:B], la("we1"), ea("cond"), start=True, stop=True)
                    filled(mm(p[:, B:2 * B], la("wc1c"), ea("cond"), start=True, stop=True), "field0")
                elif step == 1:
                    pe.wait_ge(field_rT, 1)
                    p = claim("field1", "mi")
                    filled(mm(p[0:B, 0:P], rT[:, :], la("we2"), start=True, stop=True), "field1")
                elif step == 2:
                    pe.wait_ge(field_fp, 1)
                    p = claim("field2", "mi")
                    filled(nc.tensor.transpose(p[:, 0:B], fz[:, :], ident[0:B, 0:B]), "field2")
                elif step == 3:
                    wait_taken(pe, "field2")
                    p = claim("field3", "mi")
                    filled(mm(p[0:B, :], fpT[:, :], la("pe"), start=True, stop=True), "field3")
                elif step == 4:
                    wait_taken(pe, "field3")
                    p = claim("field4", "mi")
                    for st in range(TPB):
                        last = nc.tensor.transpose(p[:, st * B:(st + 1) * B], fe[:, st * P:(st + 1) * P], ident[0:B, 0:B])
                    filled(last, "field4")

            pe.wait_ge(early_in, 16)
            p = claim("gb", "mi")
            for b in range(B):
                a0 = EARLY_AT["cond_rep"][0] + b * P
                last = mm(p[:, b * EA:(b + 1) * EA], early[:, a0:a0 + P], ea("gg"), start=True, stop=True)
            filled(last, "gb")
            pe.wait_ge(xT_in, 16)
            pe.wait_ge(gate_w_ready, 1)
            p = claim("gl", "m0")
            for t in range(NT):
                last = mm(p[:, t * EA:(t + 1) * EA], xT[:, t * P:(t + 1) * P], wgs[:, :], start=True, stop=True)
            filled(last, "gl")

            def a_h1(n):
                b, e = divmod(n, EA)
                if b == 0:
                    pe.wait_ge(wa_in[e], 16)
                p = claim(("a1", n), "s0")
                for c in range(2):
                    last = mm(p[:, c, :], wa[:, e, c * P:(c + 1) * P], xT[:, b * S:(b + 1) * S], start=True, stop=True)
                filled(last, ("a1", n))

            def a_h2(n):
                e = n % EA
                wait_taken(pe, ("a1", n))
                p = claim(("a2", n), "s1")
                for c in range(2):
                    for k in range(2):
                        o = MA + k * MA + c * P
                        last = mm(p[:, c, :], wa[:, e, o:o + P], h1[:, k, :], start=(k == 0), stop=(k == 1))
                filled(last, ("a2", n))

            def a_out(n):
                e = n % EA
                wait_taken(pe, ("a2", n))
                p = claim(("a3", n), "m1" if n % 2 else "m0")
                for t in range(TPB):
                    for k in range(2):
                        o = 3 * MA + k * P
                        last = mm(p[:, t * P:(t + 1) * P], h2[:, k, t * P:(t + 1) * P], wa[:, e, o:o + P],
                                  start=(k == 0), stop=(k == 1))
                filled(last, ("a3", n))

            def row_weights_bias(kind, rows):
                pe.wait_ge(cw_ready, 1 if kind == "a" else 2)
                p = claim((kind, "cwT"), "pv")
                for t in range(TPB):
                    last = nc.tensor.transpose(p[0:EA, t * P:(t + 1) * P], cw[:, t, :], ident)
                filled(last, (kind, "cwT"))
                p = claim((kind, "cwT2"), "mi")
                for t in range(TPB):
                    last = nc.tensor.transpose(p[0:EA, t * P:(t + 1) * P], cw[:, TPB + t, :], ident)
                filled(last, (kind, "cwT2"))
                for b, (key, s) in enumerate((("cwT", "pv"), ("cwT2", "mi"))):
                    wait_taken(pe, (kind, key))
                    p = claim((kind, "bias", b), s)
                    for t in range(TPB):
                        o = (b * TPB + t) * P
                        last = mm(p[:, t * P:(t + 1) * P], cwT[:, o:o + P], rows[0:EA, :], start=True, stop=True)
                    filled(last, (kind, "bias", b))

            a_h1(0)
            a_h2(0)
            row_weights_bias("a", ea("b3a"))
            for n in range(1, NAB):
                a_h1(n)
                a_out(n - 1)
                a_h2(n)
                if 3 <= n < 8:
                    field(n - 3)
            a_out(NAB - 1)

            def attention(L):
                hd = HD[L]
                src = c0 if L == 0 else x1

                def prep(b):
                    if L == 0:
                        wait_taken(pe, ("a3", (b + 1) * EA - 1))
                    else:
                        pe.wait_ge(x1_ready, 1)
                    transposes((L, "cT", b), "mi", [src[:, b * TPB + t, :] for t in range(TPB)])
                    wait_taken(pe, (L, "cT", b))
                    for i, w in enumerate([la("wqk0")] if L == 0 else [la("wq1"), la("wk1")]):
                        p = claim((L, "qk", b, i), "mi")
                        filled(mm(p, w, cT[:, :], start=True, stop=True), (L, "qk", b, i))
                    p = claim((L, "v", b), "mi")
                    for t in range(TPB):
                        last = mm(p[:, t * P:t * P + H * hd], cT[:, t * P:(t + 1) * P], la("wv0" if L == 0 else "wv1"),
                                  start=True, stop=True)
                    filled(last, (L, "v", b))
                    if L == 1:
                        p = claim(("tanh", b), "mi")
                        filled(mm(p, la("wc1x"), cT[:, :], start=True, stop=True), ("tanh", b))
                        wait_taken(pe, ("tanh", b))
                        p = claim(("coh", b), "mi")
                        for t in range(TPB):
                            last = mm(p[:, t * H:(t + 1) * H], tT[:, t * P:(t + 1) * P], la("wc2"), start=True, stop=True)
                        filled(last, ("coh", b))
                        wait_taken(pe, (L, "v", b))
                        p = claim(("vsum", b), "mi")
                        for t in range(TPB):
                            last = mm(p[:, 0:P], la("ones"), vaug[:, b, t, :, 0:hd], start=(t == 0), stop=(t == TPB - 1))
                        filled(last, ("vsum", b))

                def stacks(G):
                    b, g = divmod(G, NG)
                    wait_taken(pe, (L, "qk", b, L))
                    for i, (hi, lo) in enumerate(((kH, kL), (qH, qL)) if L else ((qH, qL), (qH, qL))):
                        w = 2 if i == 0 else 0
                        key = (L, "stack", G, i)
                        p = claim(key, "mi")
                        mm(p, sel[:, g, w, :], hi[:, :], start=True, stop=False)
                        filled(mm(p, sel[:, g, w + 1, :], lo[:, :], start=False, stop=True), key)

                def maxima(G, qt):
                    if qt == 0:
                        wait_taken(pe, (L, "stack", G, 1))
                    for j in range(HPG):
                        s = "m1" if j % 2 else "m0"
                        p = claim((L, "max", G, qt, j), s)
                        filled(mm(p, Qs[:, G % 2, qt * P:(qt + 1) * P], Kp[:, G % 2, j, :], start=True, stop=True),
                               (L, "max", G, qt, j))

                def place_maxima(G):
                    pe.wait_ge(MP_ready, L * B * NG + G + 1)
                    p = claim((L, "mT", G), "mi")
                    for qt in range(TPB):
                        last = mm(p[:, qt * P:(qt + 1) * P], MP[:, qt, :, :].rearrange("p j s -> p (j s)"), ident_r[:, :],
                                  start=True, stop=True)
                    filled(last, (L, "mT", G))

                def scores(G, kt):
                    if kt == 0:
                        wait_taken(pe, (L, "mT", G))
                    for jp in range(2):
                        s = f"s{jp}"
                        p = claim((L, "s", G, kt, jp), s)
                        for j in range(2):
                            last = mm(p[:, j, :], Kp[:, G % 2, 2 * jp + j, kt * P:(kt + 1) * P], Qm[:, G % 2, :],
                                      start=True, stop=True)
                        filled(last, (L, "s", G, kt, jp))

                def values(G, kt):
                    b, g = divmod(G, NG)
                    if kt == 0:
                        claim((L, "pv", G), "pv")
                        wait_taken(pe, (L, "v", b))
                    p = ps("pv")
                    for jp in range(2):
                        wait_taken(pe, (L, "s", G, kt, jp))
                    for j in range(HPG):
                        r = 2 * (kt % 2) + j // 2
                        last = mm(p[SL * j:SL * j + VW, :], vaug[:, b, kt, g * HPG + j, :], E4[:, r, j % 2, :],
                                  start=(kt == 0), stop=(kt == TPB - 1), tile_position=(0, SL * j))
                    if kt < TPB - 1:
                        last.then_inc(pv_read, 1)
                    else:
                        filled(last, (L, "pv", G))

                def turn(G):
                    wait_taken(pe, (L, "pv", G))
                    transposes((L, "o", G), "mi", [OT[:, q * P:(q + 1) * P] for q in range(TPB)])

                def post(b):
                    if L == 0:
                        wait_taken(pe, (L, "o", (b + 1) * NG - 1))
                    else:
                        pe.wait_ge(ao_ready, b + 1)
                    transposes((L, "aoT", b), "mi", [ao[:, q, :] for q in range(TPB)])
                    wait_taken(pe, (L, "aoT", b))
                    if L == 0:
                        p = claim(("mla", b), "mi")
                        filled(mm(p, la("wo0"), aoT[:, :], start=True, stop=True), ("mla", b))
                    else:
                        p = claim(("yT", b), "mi")
                        filled(mm(p, la("wout"), aoT[:, :], start=True, stop=True), ("yT", b))
                        p = claim(("y", b), "mi")
                        for t in range(TPB):
                            last = mm(p[:, t * P:(t + 1) * P], aoT[:, t * P:(t + 1) * P], la("wout"), start=True, stop=True)
                        filled(last, ("y", b))

                NGB = B * NG
                prep(0)
                pe.wait_ge(sel_in, 16 * (L + 1))
                stacks(0)
                for qt in range(TPB):
                    maxima(0, qt)
                for G in range(NGB):
                    if G + 1 < NGB:
                        if (G + 1) % NG == 0:
                            prep((G + 1) // NG)
                        stacks(G + 1)
                    place_maxima(G)
                    if G:
                        turn(G - 1)
                        if G % NG == 0:
                            post(G // NG - 1)
                    for kt in range(TPB):
                        scores(G, kt)
                        if kt:
                            values(G, kt - 1)
                        if G + 1 < NGB:
                            maxima(G + 1, kt)
                    values(G, TPB - 1)
                turn(NGB - 1)
                post(B - 1)

            pe.wait_ge(consts_r, 1)
            attention(0)

            wait_taken(pe, ("mla", B - 1))
            p = claim("bl", "m0")
            for t in range(NT):
                last = mm(p[:, t * EB:(t + 1) * EB], mlaT[:, t * P:(t + 1) * P], la("rb_w"), start=True, stop=True)
            filled(last, "bl")
            pe.wait_ge(wb_in, 16)

            def b_h1(n):
                b, e = divmod(n, EB)
                p = claim(("b1", n), f"s{n % 2}")
                for c in range(2):
                    last = mm(p[:, c, :], wb[:, e, c * P:(c + 1) * P], mlaT[:, b * S:(b + 1) * S], start=True, stop=True)
                filled(last, ("b1", n))

            def b_out(n):
                e = n % EB
                wait_taken(pe, ("b1", n))
                hb = h1 if n % 2 == 0 else h2
                p = claim(("b2", n), "m1" if n % 2 else "m0")
                for t in range(TPB):
                    for k in range(2):
                        o = MB + k * P
                        last = mm(p[:, t * P:(t + 1) * P], hb[:, k, t * P:(t + 1) * P], wb[:, e, o:o + P],
                                  start=(k == 0), stop=(k == 1))
                filled(last, ("b2", n))

            b_h1(0)
            b_h1(1)
            row_weights_bias("b", la("b2b"))
            for n in range(NAB):
                b_out(n)
                if n + 2 < NAB:
                    b_h1(n + 2)

            attention(1)

            wait_taken(pe, ("yT", B - 1))
            p = claim("cl", "m0")
            for t in range(NT):
                last = mm(p[:, t * EC:(t + 1) * EC], yT[:, t * P:(t + 1) * P], la("rc_w"), start=True, stop=True)
            filled(last, "cl")
            pe.wait_ge(ohb_ready, 1)
            pe.wait_ge(consts_b, 2)
            p = claim("count", "m1")
            for t in range(NT):
                for u in range(t + 1):
                    last = mm(p[:, t * EC:(t + 1) * EC], before_b[:, :] if u == t else ones_b[:, :], ohb[:, u, :],
                              start=(u == 0), stop=(u == t))
            filled(last, "count")
            pe.wait_ge(pk_in, 16)
            CT = ("m0", "m1", "pv", "mi")
            for q in range(NST // 4):
                transposes(("pk", q), CT[q % 4], [pk_tok[:, 4 * q + i, :] for i in range(4)])
            for q in range(NST // 4):
                wait_taken(pe, ("pk", q))

            def c_h1(e):
                if e % 4 == 0:
                    pe.wait_ge(wc_in[e // 4], 16)
                p = claim(("c1", e), f"s{e % 2}")
                for c in range(FC):
                    last = mm(p[:, c // 2, (c % 2) * CAP:(c % 2 + 1) * CAP], wc[e][:, c * P:(c + 1) * P],
                              pkT[:, e * CAP:(e + 1) * CAP], start=True, stop=True)
                filled(last, ("c1", e))

            def c_out(e):
                wait_taken(pe, ("c1", e))
                p = claim(("c2", e), "m1" if e % 2 else "m0")
                for c in range(FC):
                    o = MC + c * P
                    last = mm(p[:, 0:CAP], wc[e][:, o:o + P], hC[:, e % 2, c, :], start=(c == 0), stop=(c == FC - 1))
                filled(last, ("c2", e))

            c_h1(0)
            for e in range(EC):
                if e + 1 < EC:
                    c_h1(e + 1)
                c_out(e)
            wait_taken(pe, ("c2", EC - 1))
            wait_taken(pe, ("c2", EC - 2))
            for q in range(NST // 4):
                transposes(("eo", q), CT[q % 4], [eoT[:, (4 * q + i) * P:(4 * q + i + 1) * P] for i in range(4)])

        @block.scalar
        def _(act):
            A = nc.scalar.activation

            def field(step):
                if step == 0:
                    p = wait_full(act, "field0")
                    A(rT[:, :], p[:, 0:B], ACT.Relu, bias=la("be1")).then_inc(field_rT, 1)
                    A(bc1c[:, :], p[:, B:2 * B], ACT.Identity, bias=la("bc1")).then_inc(taken["mi"], 1)
                elif step == 1:
                    act.wait_ge(field_var, 1)
                    A(fsd[:, 1:2], fsd[:, 0:1], ACT.Sqrt).then_inc(field_sd, 1)
                elif step == 3:
                    act.wait_ge(field_mx, 1)
                    p = wait_full(act, "field3")
                    A(fe[:, :], p[0:B, :], ACT.Exp, bias=fsd[:, 2:3], accum_out=fsd[:, 3:4]).then_inc(field_exp, 1)

            act.wait_ge(x_in, 16)
            for t in range(NT):
                last = A(moe[:, t, :], x_tok[:, t, :], ACT.Square, accum_out=ssq[:, t:t + 1])
            last.then_inc(ssq_done, 1)
            act.wait_ge(var_done, 1)
            A(rstd[:, :], ssq[:, :], ACT.Sqrt).then_inc(sd_done, 1)
            act.wait_ge(shifted, 1)
            A(pr[:, :, 0:EA], lg[:, :, 0:EA], ACT.Exp).then_inc(expd, 1)
            for n in range(NAB):
                p = wait_full(act, ("a1", n))
                e = n % EA
                for c in range(2):
                    o = EARLY_AT["b1a"][0] + 2 * e + c
                    last = A(h1[:, c, :], p[:, c, :], ACT.Relu, bias=early[:, o:o + 1])
                last.then_inc(taken["s0"], 1)
                if 3 <= n < 8:
                    field(n - 3)

            def attention(L):
                def prep(b):
                    p = wait_full(act, (L, "cT", b))
                    A(cT[:, :], p, ACT.Copy).then_inc(taken["mi"], 1)
                    for i in range(1 + L):
                        p = wait_full(act, (L, "qk", b, i))
                        hi = kH if i else qH
                        A(hi[:, :], p, ACT.Identity, bias=la(("bqk0",) [0] if L == 0 else ("bq1", "bk1")[i])).then_inc(H_done, 1)
                    if L == 1:
                        p = wait_full(act, ("tanh", b))
                        A(tT[:, :], p, ACT.Tanh, bias=bc1c[:, b:b + 1]).then_inc(taken["mi"], 1)
                        wait_taken(act, ("coh", b))
                        A(coh[:, :, :], coh2[:, b, :, :], ACT.Exp, scale=-1.0).then_inc(coh_e, 1)

                def stacks(G):
                    p = wait_full(act, (L, "stack", G, 0))
                    for j in range(HPG):
                        r = slice(SL * j, SL * (j + 1))
                        last = A(Kp[r, G % 2, j, :], p[r, :], ACT.Identity, bias=la("minus")[r, :])
                    last.then_inc(taken["mi"], 1)
                    p = wait_full(act, (L, "stack", G, 1))
                    A(Qs[:, G % 2, :], p, ACT.Copy).then_inc(taken["mi"], 1)

                def exps(G, kt):
                    if kt >= 2:
                        act.wait_ge(pv_read, (L * B * NG + G) * (TPB - 1) + kt - 1)
                    for jp in range(2):
                        p = wait_full(act, (L, "s", G, kt, jp))
                        A(E4[:, 2 * (kt % 2) + jp, :, :], p, ACT.Exp, scale=float(HD[L]) ** -0.5).then_inc(taken[f"s{jp}"], 1)

                NGB = B * NG
                prep(0)
                if L == 0:
                    act.wait_ge(clear0, 1)
                stacks(0)
                for G in range(NGB):
                    if G + 1 < NGB:
                        if (G + 1) % NG == 0:
                            prep((G + 1) // NG)
                        stacks(G + 1)
                    if G and G % NG == 0:
                        post(L, G // NG - 1)
                    for kt in range(TPB):
                        exps(G, kt)
                    p = wait_full(act, (L, "pv", G))
                    A(OT[:, :], p, ACT.Copy).then_inc(taken["pv"], 1)
                post(L, B - 1)

            def post(L, b):
                p = wait_full(act, (L, "aoT", b))
                A(aoT[:, :], p, ACT.Copy).then_inc(taken["mi"], 1)
                if L == 0:
                    p = wait_full(act, ("mla", b))
                    A(mlaT[:, b * S:(b + 1) * S], p, ACT.Identity, bias=la("bo0")).then_inc(taken["mi"], 1)
                else:
                    p = wait_full(act, ("yT", b))
                    A(yT[:, b * S:(b + 1) * S], p, ACT.Identity, bias=la("bout_col")).then_inc(taken["mi"], 1)

            attention(0)
            act.wait_ge(shifted, 2)
            A(pr[:, :, 0:EB], lg[:, :, 0:EB], ACT.Exp).then_inc(expd, 1)
            for n in range(NAB):
                p = wait_full(act, ("b1", n))
                e = n % EB
                if n >= 2:
                    wait_full(act, ("b2", n - 2))
                hb = h1 if n % 2 == 0 else h2
                for c in range(2):
                    o = LATE_AT["b1b"][0] + 2 * e + c
                    last = A(hb[:, c, :], p[:, c, :], ACT.Gelu, bias=late[:, o:o + 1])
                last.then_inc(taken[f"s{n % 2}"], 1)
            attention(1)
            act.wait_ge(gdiff, 1)
            A(gate[:, 1, :], gden[:, :], ACT.Exp).then_inc(gexp, 1)
            for q in range(1, NST // 4, 2):
                p = wait_full(act, ("pk", q))
                A(pkT[:, q * 512:(q + 1) * 512], p, ACT.Copy).then_inc(taken[filled_at[("pk", q)][0]], 1)
            for e in range(EC):
                p = wait_full(act, ("c1", e))
                if e >= 2:
                    wait_full(act, ("c2", e - 2))
                for c in range(FC):
                    o = LATE_AT["b1c"][0] + FC * e + c
                    last = A(hC[:, e % 2, c, :], p[:, c // 2, (c % 2) * CAP:(c % 2 + 1) * CAP], ACT.Gelu,
                             bias=late[:, o:o + 1])
                last.then_inc(taken[f"s{e % 2}"], 1)
            for q in range(1, NST // 4, 2):
                p = wait_full(act, ("eo", q))
                A(eo_tok[:, 4 * q:4 * q + 4, :].rearrange("p t d -> p (t d)"), p, ACT.Copy).then_inc(
                    taken[filled_at[("eo", q)][0]], 1)

        @block.vector
        def _(dve):
            V = nc.vector
            links = [0]

            def link(ins):
                links[0] += 1
                ins.then_inc(dve_chain, 1)
                dve.wait_ge(dve_chain, links[0])

            def wide(ap, n):
                return ap.unsqueeze(2).to_broadcast([ap.shape[0], ap.shape[1], n])

            def top2(E, p_or_l):
                for t in range(NT):
                    last = V.max(top8[:, t, :], p_or_l[:, t, 0:E])
                link(last)
                for t in range(NT):
                    last = V.max_index(idx8[:, t, :], top8[:, t, :], p_or_l[:, t, 0:E])
                link(last)
                link(V.tensor_copy(idxf[:, :, :], idx8[:, :, 0:2]))
                io = ea("iota")[:, 0:E].unsqueeze(1).to_broadcast([P, NT, E])
                for k in range(2):
                    last = V.tensor_tensor(oh[:, k, :, 0:E], io, wide(idxf[:, :, k], E), ALU.is_equal)
                link(last)

            def softmax8(nth):
                link(V.reduce_max(rmx[:, :], lg[:, :, 0:8], AX.X))
                V.tensor_tensor(lg[:, :, 0:8], lg[:, :, 0:8], wide(rmx[:, :], 8), ALU.subtract).then_inc(shifted, 1)
                dve.wait_ge(expd, nth)
                link(V.reduce_sum(rsm[:, :], pr[:, :, 0:8], AX.X))
                link(V.reciprocal(rsm[:, :], rsm[:, :]))
                link(V.tensor_tensor(pr[:, :, 0:8], pr[:, :, 0:8], wide(rsm[:, :], 8), ALU.mult))

            V.memset(Kp[:, :, :, :].rearrange("p a j s -> p (a j s)").bitcast(F32), 0.0).then_inc(clear0, 1)
            V.memset(MP[:, :, :, :].rearrange("p a j s -> p (a j s)").bitcast(F32), 0.0)
            V.memset(ao[:, :, :], 0.0).then_inc(zero_ready, 1)
            link(V.memset(vaug[:, :, :, :, :], 0.0))
            link(V.memset(vaug[:, :, :, :, HD[0]:HD[0] + 1], 1.0))
            dve.wait_ge(early_in, 16)
            V.tensor_copy(ident_r[:, :], ident).then_inc(consts_r, 1)
            V.tensor_scalar(wgs[:, :], ea("wg"), ea("rms"), None, ALU.mult).then_inc(gate_w_ready, 1)
            dve.wait_ge(ssq_done, 1)
            V.tensor_scalar(ssq[:, :], ssq[:, :], 1.0 / D, 1e-6, ALU.mult, ALU.add).then_inc(var_done, 1)
            p = wait_full(dve, "gb")
            pv = p[:, 0:B * EA].rearrange("p (b e) -> p b e", b=B)
            V.tensor_tensor(gbias[:, :, :], pv, ea("gg_b").unsqueeze(1).to_broadcast([P, B, EA]), ALU.add).then_inc(taken["mi"], 1)
            dve.wait_ge(taken["mi"], 1)
            link(V.tensor_tensor(gbias[:, :, :], gbias[:, :, :], ea("wg_b").unsqueeze(1).to_broadcast([P, B, EA]), ALU.add))
            dve.wait_ge(sd_done, 1)
            link(V.reciprocal(rstd[:, :], rstd[:, :]))
            p = wait_full(dve, "gl")
            pv = p[:, 0:NT * EA].rearrange("p (t e) -> p t e", e=EA)
            V.tensor_tensor(lg[:, :, 0:EA], pv, wide(rstd[:, :], EA), ALU.mult).then_inc(taken["m0"], 1)
            dve.wait_ge(taken["m0"], 1)
            for b in range(B):
                last = V.tensor_tensor(lg[:, b * TPB:(b + 1) * TPB, 0:EA], lg[:, b * TPB:(b + 1) * TPB, 0:EA],
                                       gbias[:, b, :].unsqueeze(1).to_broadcast([P, TPB, EA]), ALU.add)
            link(last)
            softmax8(1)
            top2(EA, pr)
            link(V.tensor_tensor(cw[:, :, :], oh[:, 0, :, 0:EA], oh[:, 1, :, 0:EA], ALU.add))
            V.tensor_tensor(cw[:, :, :], cw[:, :, :], pr[:, :, 0:EA], ALU.mult).then_inc(cw_ready, 1)

            def h2_out(n):
                p = wait_full(dve, ("a2", n))
                e = n % EA
                for c in range(2):
                    o = EARLY_AT["b2a"][0] + 2 * e + c
                    last = V.tensor_scalar(h2[:, c, :], p[:, c, :], early[:, o:o + 1], 0.0, ALU.add, ALU.max)
                last.then_inc(taken["s1"], 1)

            acc_at = {}

            def combine(kind, n, acc):
                b, e = divmod(n, 8)
                key = ("a3" if kind == "a" else "b2", n)
                p = wait_full(dve, key)
                if e:
                    dve.wait_ge(*acc_at[kind, n - 1])
                for t in range(TPB):
                    T = b * TPB + t
                    last = V.scalar_tensor_tensor(acc[:, T, :], p[:, t * P:(t + 1) * P], cw[:, T, e:e + 1], acc[:, T, :],
                                                  ALU.mult, ALU.add)
                last.then_inc(taken[filled_at[key][0]], 1)
                s, k = filled_at[key]
                acc_at[kind, n] = (taken[s], k)

            def bias_rows(kind, acc, done):
                p = wait_full(dve, (kind, "cwT"))
                V.tensor_copy(cwT[:, 0:S], p[0:EA, :]).then_inc(taken["pv"], 1)
                p = wait_full(dve, (kind, "cwT2"))
                V.tensor_copy(cwT[:, S:2 * S], p[0:EA, :]).then_inc(taken["mi"], 1)
                for b, s in enumerate(("pv", "mi")):
                    p = wait_full(dve, (kind, "bias", b))
                    V.tensor_copy(acc[:, b * TPB:(b + 1) * TPB, :].rearrange("p t d -> p (t d)"), p).then_inc(taken[s], 1)
                    dve.wait_ge(taken[s], filled_at[(kind, "bias", b)][1])

            def field(step):
                if step == 1:
                    p = wait_full(dve, "field1")
                    V.tensor_tensor(fz[:, :], p[0:B, 0:P], la("be2")[0:B, :], ALU.add).then_inc(taken["mi"], 1)
                    wait_taken(dve, "field1")
                    link(V.bn_stats(fst[:, :], fz[:, :]))
                    link(V.bn_aggr(fag[:, :], fst[:, :]))
                    V.tensor_scalar(fsd[:, 0:1], fag[:, 1:2], 1e-5, None, ALU.add).then_inc(field_var, 1)
                elif step == 2:
                    dve.wait_ge(field_sd, 1)
                    link(V.reciprocal(fsd[:, 2:3], fsd[:, 1:2]))
                    link(V.tensor_scalar(fz[:, :], fz[:, :], fag[:, 0:1], fsd[:, 2:3], ALU.subtract, ALU.mult))
                    link(V.tensor_tensor(fz[:, :], fz[:, :], la("ln_g")[0:B, :], ALU.mult))
                    V.tensor_tensor(fz[:, :], fz[:, :], la("ln_b")[0:B, :], ALU.add).then_inc(field_fp, 1)
                    p = wait_full(dve, "field2")
                    V.tensor_copy(fpT[:, :], p[:, 0:B]).then_inc(taken["mi"], 1)
                elif step == 3:
                    p = wait_full(dve, "field3")
                    V.tensor_reduce(fsd[:, 2:3], p[0:B, :], AX.X, ALU.max, negate=True).then_inc(field_mx, 1)
                    dve.wait_ge(field_exp, 1)
                    link(V.reciprocal(fsd[:, 3:4], fsd[:, 3:4]))
                    V.tensor_scalar(fe[:, :], fe[:, :], fsd[:, 3:4], FI, ALU.mult, ALU.mult).then_inc(taken["mi"], 1)
                elif step == 4:
                    p = wait_full(dve, "field4")
                    V.tensor_copy(faT[:, :, :], p[:, 0:TPB * B].rearrange("p (t b) -> p t b", b=B)).then_inc(taken["mi"], 1)

            h2_out(0)
            bias_rows("a", c0, c0_set)
            for n in range(1, NAB):
                combine("a", n - 1, c0)
                if n == EA + 1:
                    pass
                h2_out(n)
                if 3 <= n < 8:
                    field(n - 3)
            combine("a", NAB - 1, c0)
            dve.wait_ge(late_in, 16)
            V.tensor_copy(before_b[:, :], la("before")).then_inc(consts_b, 1)
            V.tensor_copy(ones_b[:, :], la("ones")).then_inc(consts_b, 1)

            def attention(L):
                hd = HD[L]

                def prep(b):
                    for i in range(1 + L):
                        p = wait_full(dve, (L, "qk", b, i))
                        dve.wait_ge(H_done, (b + 1) if L == 0 else B + 2 * b + i + 1)
                        hi, lo = (kH, kL) if i else (qH, qL)
                        bias = la("bqk0" if L == 0 else ("bq1", "bk1")[i])
                        V.scalar_tensor_tensor(lo[:, :], p, bias, hi[:, :], ALU.add, ALU.subtract).then_inc(taken["mi"], 1)
                        wait_taken(dve, (L, "qk", b, i))
                    p = wait_full(dve, (L, "v", b))
                    pvv = p.rearrange("p (t c) -> p t c", t=TPB)[:, :, 0:H * hd]
                    for t in range(TPB):
                        last = V.tensor_tensor(vaug[:, b, t, :, 0:hd], pvv[:, t, :].rearrange("p (h d) -> p h d", d=hd),
                                               la("bv0" if L == 0 else "bv1").rearrange("p (h d) -> p h d", d=hd), ALU.add)
                    last.then_inc(taken["mi"], 1)
                    wait_taken(dve, (L, "v", b))
                    if L == 1:
                        p = wait_full(dve, ("coh", b))
                        V.tensor_tensor(coh2[:, b, :, :], p[:, 0:TPB * H].rearrange("p (t h) -> p t h", h=H),
                                        la("bc2").unsqueeze(1).to_broadcast([P, TPB, H]), ALU.add).then_inc(taken["mi"], 1)
                        wait_taken(dve, ("coh", b))
                        p = wait_full(dve, ("vsum", b))
                        V.tensor_copy(vsum[:, b, :], p[:, 0:P]).then_inc(taken["mi"], 1)
                        dve.wait_ge(coh_e, b + 1)
                        link(V.tensor_scalar(coh[:, :, :], coh[:, :, :], 1.0, None, ALU.add))
                        link(V.reciprocal(coh[:, :, :], coh[:, :, :]))
                        link(V.tensor_scalar(coh2[:, b, :, :], coh[:, :, :], 1e-8, None, ALU.add))
                        link(V.reciprocal(coh2[:, b, :, :], coh2[:, b, :, :]))
                        link(V.scalar_tensor_tensor(coh2[:, b, :, :], coh[:, :, :], 1.0 - FI, coh2[:, b, :, :], ALU.mult, ALU.mult))

                def maxima(G, qt):
                    for j in range(HPG):
                        p = wait_full(dve, (L, "max", G, qt, j))
                        V.reduce_max(mx[:, qt, j:j + 1], p, AX.X).then_inc(taken[filled_at[(L, "max", G, qt, j)][0]], 1)

                def place(G):
                    for j in (HPG - 2, HPG - 1):
                        wait_taken(dve, (L, "max", G, TPB - 1, j))
                    link(V.tensor_copy(MP[:, :, :, 0], mx[:, :, :]))
                    V.tensor_tensor(MP[:, :, :, 1], mx[:, :, :], MP[:, :, :, 0], ALU.subtract).then_inc(MP_ready, 1)

                def put_maxima(G):
                    p = wait_full(dve, (L, "mT", G))
                    V.tensor_tensor(Qm[:, G % 2, :], p, Qs[:, G % 2, :], ALU.add).then_inc(taken["mi"], 1)
                    wait_taken(dve, (L, "mT", G))

                def norm(G):
                    b, g = divmod(G, NG)
                    p = wait_full(dve, (L, "o", G))
                    o = p.rearrange("p (t j s) -> p t j s", t=TPB, j=HPG)
                    link(V.reciprocal(rden[:, :, :], o[:, :, :, hd]))
                    if L == 1:
                        link(V.tensor_tensor(rden[:, :, :], rden[:, :, :], coh2[:, b, :, g * HPG:(g + 1) * HPG], ALU.mult))
                    if L == 0 and G == 0:
                        dve.wait_ge(zeroed, 16)
                    a = ao[:, :, :].rearrange("p t (h d) -> p t h d", d=hd)
                    for t in range(TPB):
                        last = V.tensor_tensor(a[:, t, g * HPG:(g + 1) * HPG, :], o[:, t, :, 0:hd], wide(rden[:, t, :], hd),
                                               ALU.mult)
                    last.then_inc(taken["mi"], 1)
                    wait_taken(dve, (L, "o", G))

                def post(b):
                    if L == 1:
                        for t in range(TPB):
                            last = V.scalar_tensor_tensor(ao[:, t, :], vsum[:, b, :], faT[:, t, b:b + 1], ao[:, t, :],
                                                          ALU.mult, ALU.add)
                        last.then_inc(ao_ready, 1)
                        p = wait_full(dve, ("y", b))
                        V.tensor_tensor(y[:, b * TPB:(b + 1) * TPB, :], p.rearrange("p (t d) -> p t d", t=TPB),
                                        la("bout").unsqueeze(1).to_broadcast([P, TPB, D]), ALU.add).then_inc(taken["mi"], 1)

                NGB = B * NG
                prep(0)
                for qt in range(TPB):
                    maxima(0, qt)
                place(0)
                for G in range(NGB):
                    if G + 1 < NGB and (G + 1) % NG == 0:
                        prep1 = (G + 1) // NG
                        if L == 0:
                            prep(prep1)
                        else:
                            prep(prep1)
                    put_maxima(G)
                    if G:
                        norm(G - 1)
                        if G % NG == 0:
                            post(G // NG - 1)
                    if G + 1 < NGB:
                        for kt in range(TPB):
                            maxima(G + 1, kt)
                        place(G + 1)
                norm(NGB - 1)
                post(B - 1)

            attention(0)
            p = wait_full(dve, "bl")
            V.tensor_tensor(lg[:, :, 0:EB], p[:, 0:NT * EB].rearrange("p (t e) -> p t e", e=EB),
                            la("rb_b").unsqueeze(1).to_broadcast([P, NT, EB]), ALU.add).then_inc(taken["m0"], 1)
            wait_taken(dve, "bl")
            softmax8(2)
            top2(EB, pr)
            link(V.tensor_tensor(rsm[:, :], top8[:, :, 0], top8[:, :, 1], ALU.add))
            link(V.tensor_scalar(rsm[:, :], rsm[:, :], 1e-8, None, ALU.add))
            link(V.reciprocal(rsm[:, :], rsm[:, :]))
            link(V.tensor_tensor(cw[:, :, :], oh[:, 0, :, 0:EB], oh[:, 1, :, 0:EB], ALU.add))
            link(V.tensor_tensor(cw[:, :, :], cw[:, :, :], pr[:, :, 0:EB], ALU.mult))
            V.tensor_tensor(cw[:, :, :], cw[:, :, :], wide(rsm[:, :], EB), ALU.mult).then_inc(cw_ready, 1)
            bias_rows("b", moe, moe_set)
            for n in range(NAB):
                combine("b", n, moe)
            for n in (EB - 1, NAB - 1):
                dve.wait_ge(*acc_at["b", n])
            link(V.scalar_tensor_tensor(moe[:, :, :], moe[:, :, :], 0.3, c0[:, :, :], ALU.mult, ALU.add))
            V.tensor_tensor(x1[:, :, :], moe[:, :, :], x_tok[:, :, :], ALU.add).then_inc(x1_ready, 1)
            V.memset(vaug[:, :, :, :, HD[1]:HD[1] + 1], 1.0)
            attention(1)

            p = wait_full(dve, "cl")
            V.tensor_tensor(lg[:, :, :], p[:, 0:NT * EC].rearrange("p (t e) -> p t e", e=EC),
                            la("rc_b").unsqueeze(1).to_broadcast([P, NT, EC]), ALU.add).then_inc(taken["m0"], 1)
            wait_taken(dve, "cl")
            top2(EC, lg)
            V.tensor_tensor(ohb[:, :, :], oh[:, 0, :, :], oh[:, 1, :, :], ALU.add).then_inc(ohb_ready, 1)
            V.tensor_tensor(gden[:, :], top8[:, :, 1], top8[:, :, 0], ALU.subtract).then_inc(gdiff, 1)
            p = wait_full(dve, "count").rearrange("p (t e) -> p t e", e=EC)[:, 0:NT, :]
            link(V.tensor_tensor(lg[:, :, :], oh[:, 0, :, :], p, ALU.mult))
            V.tensor_tensor(pr[:, :, :], oh[:, 1, :, :], p, ALU.mult).then_inc(taken["m1"], 1)
            wait_taken(dve, "count")
            V.reduce_sum(pos[:, 0, :], lg[:, :, :], AX.X)
            link(V.reduce_sum(pos[:, 1, :], pr[:, :, :], AX.X))
            for k in range(2):
                last = V.scalar_tensor_tensor(slot[:, k, :], idxf[:, :, k], float(CAP), pos[:, k, :], ALU.mult, ALU.add)
            link(last)
            link(V.tensor_scalar(kept[:, :, :], pos[:, :, :], float(CAP), None, ALU.is_lt))
            link(V.tensor_scalar(pos[:, :, :], kept[:, :, :], -2.0 * NSLOT, 2.0 * NSLOT, ALU.mult, ALU.add))
            link(V.tensor_tensor(pos[:, :, :], pos[:, :, :], slot[:, :, :], ALU.add))
            V.tensor_copy(put_at[:, :, :], pos[:, :, :]).then_inc(put_ready, 1)
            link(V.tensor_scalar(slot[:, :, :], slot[:, :, :], float(NSLOT - 1), None, ALU.min))
            V.tensor_copy(get_at[:, :, :], slot[:, :, :]).then_inc(get_ready, 1)
            dve.wait_ge(gexp, 1)
            link(V.tensor_scalar(gden[:, :], gate[:, 1, :], 1.0, None, ALU.add))
            link(V.reciprocal(gate[:, 0, :], gden[:, :]))
            link(V.tensor_tensor(gate[:, 1, :], gate[:, 1, :], gate[:, 0, :], ALU.mult))
            link(V.tensor_tensor(gate[:, :, :], gate[:, :, :], kept[:, :, :], ALU.mult))
            link(V.tensor_tensor(gden[:, :], gate[:, 0, :], gate[:, 1, :], ALU.add))
            link(V.tensor_scalar(gden[:, :], gden[:, :], 1e-9, None, ALU.add))
            link(V.reciprocal(gden[:, :], gden[:, :]))
            for k in range(2):
                last = V.tensor_tensor(gate[:, k, :], gate[:, k, :], gden[:, :], ALU.mult)
            link(last)
            for q in range(0, NST // 4, 2):
                p = wait_full(dve, ("pk", q))
                V.tensor_copy(pkT[:, q * 512:(q + 1) * 512], p).then_inc(taken[filled_at[("pk", q)][0]], 1)
            for e in range(EC):
                p = wait_full(dve, ("c2", e))
                o = LATE_AT["b2c"][0] + e
                V.tensor_scalar(eoT[:, e * CAP:(e + 1) * CAP], p[:, 0:CAP], late[:, o:o + 1], None, ALU.add).then_inc(
                    taken[filled_at[("c2", e)][0]], 1)
            for q in range(0, NST // 4, 2):
                p = wait_full(dve, ("eo", q))
                V.tensor_copy(eo_tok[:, 4 * q:4 * q + 4, :].rearrange("p t d -> p (t d)"), p).then_inc(
                    taken[filled_at[("eo", q)][0]], 1)
            for t in range(NT):
                dve.wait_ge(got_in, 16 * 2 * NT) if t == 0 else None
                link(V.scalar_tensor_tensor(x1[:, t, :], got[:, 0, t, :], gate[:, 0, t:t + 1], x1[:, t, :], ALU.mult, ALU.add))
                last = V.scalar_tensor_tensor(x1[:, t, :], got[:, 1, t, :], gate[:, 1, t:t + 1], x1[:, t, :], ALU.mult, ALU.add)
            last.then_inc(out_ready, 1)

        @block.sync
        def _(sp):
            sp.dma_start(early[:, :], early_d).then_inc(early_in, 16)
            sp.dma_start(x_tok[:, :, :], x_tok_d).then_inc(x_in, 16)
            sp.dma_start(xT[:, :], xT_d).then_inc(xT_in, 16)
            for e in range(EA):
                sp.dma_start(wa[:, e, :], wa_d[:, e, :]).then_inc(wa_in[e], 16)
            sp.dma_start(late[:, :], late_d).then_inc(late_in, 16)
            sp.wait_ge(zero_ready, 1)
            sp.dma_start(packed_d.rearrange("(p r) d -> p (r d)", p=P).rearrange("p (a n) -> p a n", n=512),
                         ao[:, :, :].rearrange("p t d -> p (t d)").unsqueeze(1).to_broadcast([P, NSLOT // P * D // 512, 512])).then_inc(zeroed, 16)
            sp.dma_start(wb[:, :, :], wb_d).then_inc(wb_in, 16)
            for q in (2, 3):
                sp.dma_start(wc_late[:, 4 * q - 8:4 * q - 4, :], wc_d[:, 4 * q:4 * q + 4, :]).then_inc(wc_in[q], 16)
            wait_taken(sp, ("a3", NAB - 1))
            for q in (0, 1):
                sp.dma_start(wa[:, 4 * q:4 * q + 4, :], wc_d[:, 4 * q:4 * q + 4, :]).then_inc(wc_in[q], 16)
            sp.wait_ge(putted, 16 * 2 * NT)
            sp.dma_start(pk_tok, packed_d.rearrange("(t p) d -> p t d", p=P)).then_inc(pk_in, 16)
            for q in range(NST // 4):
                wait_taken(sp, ("eo", q))
            sp.dma_start(expert_d.rearrange("(t p) d -> p t d", p=P), eo_tok).then_inc(eo_out, 16)
            sp.wait_ge(out_ready, 1)
            sp.dma_start(out_d, x1[:, :, :]).then_inc(out_done, 16)
            sp.wait_ge(out_done, 16)

        @block.gpsimd
        def _(pool):
            pool.dma_start(sel[:, :, :, :].rearrange("p g w s -> p (g w s)"), sel_d[:, 0, :]).then_inc(sel_in, 16)
            wait_full(pool, (0, "stack", B * NG - 1, 1))
            pool.dma_start(sel[:, :, :, :].rearrange("p g w s -> p (g w s)"), sel_d[:, 1, :]).then_inc(sel_in, 16)
            pool.wait_ge(zeroed, 16)
            pool.wait_ge(put_ready, 1)
            for t in range(NT):
                for k in range(2):
                    pool.indirect_dma_start(out=packed_d, out_offset=bass.IndirectOffsetOnAxis(ap=put_at[:, k, t:t + 1], axis=0),
                                            in_=y[:, t, :], in_offset=None, bounds_check=NSLOT - 1,
                                            oob_is_err=False).then_inc(putted, 16)
            pool.wait_ge(get_ready, 1)
            pool.wait_ge(eo_out, 16)
            for t in range(NT):
                for k in range(2):
                    pool.indirect_dma_start(out=got[:, k, t, :], out_offset=None, in_=expert_d,
                                            in_offset=bass.IndirectOffsetOnAxis(ap=get_at[:, k, t:t + 1], axis=0)
                                            ).then_inc(got_in, 16)


def kernel(**inputs):
    import numpy as np
    import concourse.bacc as bacc
    from concourse.bass_utils import run_bass_kernel_spmd

    a = {k: np.asarray(v) for k, v in inputs.items()}
    f4 = np.float32

    def rows(m):
        m = np.asarray(m, f4)
        out = np.zeros((P, m.shape[1]), f4)
        out[:m.shape[0]] = m
        return out

    def rep(v):
        return np.broadcast_to(np.asarray(v, f4).reshape(1, -1), (P, v.size))

    def cols(v):
        return np.asarray(v, f4).reshape(-1, P).T

    x = a["x"].reshape(B * S, D)
    cond = a["cond_256"]
    q_w = a["L0_ffn_q_w"].reshape(D, H, D // H)[:, :, :HD[0]].reshape(D, H * HD[0])
    q_b = a["L0_ffn_q_b"].reshape(H, D // H)[:, :HD[0]].reshape(-1)
    wqkv, bqkv = a["L1_cond_Wqkv"], a["L1_cond_bqkv"]
    wc1 = a["L1_cond_Wc1"]
    s_, e_ = np.arange(S, dtype=f4), np.arange(0, D, 2, dtype=f4)
    inv = f4(10000.0) ** np.repeat(e_ / f4(D), 2)
    early = {
        "wg": a["L0_cond_wg_W"], "rms": cols(a["L0_cond_rms_w"]), "gg": rows(a["L0_cond_gg_W"]),
        "cond_rep": rows(np.repeat(cond.T[:, :, None], P, axis=2).reshape(CD, B * P)),
        "wg_b": rep(a["L0_cond_wg_b"]), "gg_b": rep(a["L0_cond_gg_b"]),
        "b1a": cols(a["L0_cond_b1"]), "b2a": cols(a["L0_cond_b2"]), "b3a": rows(a["L0_cond_b3"]),
        "cond": rows(cond.T), "iota": rep(np.arange(EC, dtype=f4)), "ident": np.eye(P, dtype=f4),
    }
    minus = np.zeros((P, 1), f4)
    for j in range(HPG):
        minus[SL * j:SL * j + 2] = -1.0
    late = {
        "wqk0": np.concatenate([q_w, a["L0_ffn_k_w"]], 1), "bqk0": cols(np.concatenate([q_b, a["L0_ffn_k_b"]])),
        "wv0": a["L0_ffn_v_w"], "bv0": rep(a["L0_ffn_v_b"]), "wo0": a["L0_ffn_o_w"], "bo0": cols(a["L0_ffn_o_b"]),
        "rb_w": a["L0_ffn_router_w"], "rb_b": rep(a["L0_ffn_router_b"]), "b1b": cols(a["L0_ffn_b1"]),
        "b2b": rows(a["L0_ffn_b2"]),
        "wq1": wqkv[0:D].T, "wk1": wqkv[D:2 * D].T, "wv1": wqkv[2 * D:3 * D].T,
        "bq1": cols(bqkv[0:D]), "bk1": cols(bqkv[D:2 * D]), "bv1": rep(bqkv[2 * D:3 * D]),
        "wc1x": wc1[:, :D].T, "wc1c": rows(wc1[:, D:].T), "bc1": cols(a["L1_cond_bc1"]),
        "wc2": a["L1_cond_Wc2"].T, "bc2": rep(a["L1_cond_bc2"]),
        "we1": rows(a["L1_cond_We1"].T), "be1": cols(a["L1_cond_be1"]), "we2": a["L1_cond_We2"].T,
        "be2": rep(a["L1_cond_be2"]), "ln_g": rep(a["L1_cond_ln_g"]), "ln_b": rep(a["L1_cond_ln_b"]),
        "pe": np.sin(s_[:, None] / inv[None, :]).T,
        "wout": a["L1_cond_Wout"].T, "bout_col": cols(a["L1_cond_bout"]), "bout": rep(a["L1_cond_bout"]),
        "rc_w": a["L1_ffn_router_w"].T, "rc_b": rep(a["L1_ffn_router_b"]),
        "b1c": cols(a["L1_ffn_b1"]), "b2c": cols(a["L1_ffn_b2"]),
        "before": np.triu(np.ones((P, P), f4), 1), "ones": np.ones((P, P), f4), "minus": minus,
    }
    sel = np.zeros((P, 2, NG, 4, P), f4)
    for L in range(2):
        for g in range(NG):
            for j in range(HPG):
                for d in range(HD[L]):
                    q = (g * HPG + j) * HD[L] + d
                    k = q + (H * HD[0] if L == 0 else 0)
                    s0, s1, s2 = (SL * j + 2 + i * HD[L] + d for i in range(3))
                    sel[q, L, g, 0, [s0, s1]] = 1
                    sel[q, L, g, 1, s2] = 1
                    sel[k, L, g, 2, [s0, s2]] = 1
                    sel[k, L, g, 3, s1] = 1

    def chunks(w):
        e, k, n = w.shape
        return w.reshape(e, k // P, P, n).transpose(2, 0, 1, 3).reshape(P, e, -1)

    arrays = {
        "x_tok": x.reshape(NT, P, D).transpose(1, 0, 2), "xT": x.T,
        "early": np.concatenate([early[n] for n, _ in EARLY], 1),
        "late": np.concatenate([late[n] for n, _ in LATE], 1),
        "sel": sel.reshape(P, 2, -1),
        "wa": np.concatenate([chunks(a[f"L0_cond_W{i}"]) for i in (1, 2, 3)], 2),
        "wb": np.concatenate([chunks(a[f"L0_ffn_w{i}"]) for i in (1, 2)], 2),
        "wc": np.concatenate([chunks(a[f"L1_ffn_w{i}"]) for i in (1, 2)], 2),
    }
    arrays = {k + "_dram": np.ascontiguousarray(v) for k, v in arrays.items()}
    nc = bacc.Bacc("TRN2", target_bir_lowering=False, num_devices=1)
    args = [nc.dram_tensor(k, v.shape, mybir.dt.from_np(v.dtype), kind="ExternalInput").ap() for k, v in arrays.items()]
    out = nc.dram_tensor("out_dram", (P, NT, D), mybir.dt.float32, kind="ExternalOutput").ap()
    build(nc, *args, out)
    r = run_bass_kernel_spmd(nc, [arrays], core_ids=[0])
    got = r.results[0]["out_dram"]
    return np.ascontiguousarray(got.transpose(1, 0, 2)).reshape(B, S, D)
```

```python
import concourse.bass as bass
from concourse import mybir
from contextlib import ExitStack

P = 128
B, S, D = 2, 512, 128
TPB = S // P
NT = B * TPB
EA, MA = 8, 256
EB, MB = 8, 256
EC, MC = 16, 512
CAP = 160
NSLOT = EC * CAP
NST = NSLOT // P
H = 16
HPG = 4
NG = H // HPG
SL = 32
VW = 16
HD = (4, 8)
FC = MC // P
CD = 32
FI = 0.3 * 0.7

EARLY = [("wg", EA), ("rms", 1), ("gg", EA), ("cond_rep", B * P), ("wg_b", EA), ("gg_b", EA),
         ("b1a", 2 * EA), ("b2a", 2 * EA), ("b3a", P), ("cond", B), ("iota", EC), ("ident", P)]
LATE = [("wqk0", P), ("bqk0", 1), ("wv0", H * HD[0]), ("bv0", H * HD[0]), ("wo0", P), ("bo0", 1),
        ("rb_w", EB), ("rb_b", EB), ("b1b", 2 * EB), ("b2b", P),
        ("wq1", P), ("wk1", P), ("wv1", P), ("bq1", 1), ("bk1", 1), ("bv1", P),
        ("wc1x", P), ("wc1c", P), ("bc1", 1), ("wc2", H), ("bc2", H),
        ("we1", P), ("be1", 1), ("we2", P), ("be2", P), ("ln_g", P), ("ln_b", P), ("pe", S),
        ("wout", P), ("bout_col", 1), ("bout", P), ("rc_w", EC), ("rc_b", EC),
        ("b1c", EC * FC), ("b2c", EC), ("before", P), ("ones", P), ("minus", 1)]


def places(fields):
    at, out = 0, {}
    for name, n in fields:
        out[name] = (at, at + n)
        at += n
    return out, at


EARLY_AT, EARLY_N = places(EARLY)
LATE_AT, LATE_N = places(LATE)


def build(nc, x_tok_d, xT_d, early_d, late_d, sel_d, wa_d, wb_d, wc_d, out_d):
    F32, F32R, BF16, U32 = mybir.dt.float32, mybir.dt.float32r, mybir.dt.bfloat16, mybir.dt.uint32
    ALU, ACT, AX = mybir.AluOpType, mybir.ActivationFunctionType, mybir.AxisListType
    ctx = ExitStack()
    with ctx:
        def sb(name, shape, dt=F32):
            return ctx.enter_context(nc.sbuf_tensor(name, shape, dt))

        def sem(name):
            return ctx.enter_context(nc.semaphore(name))

        packed_d = nc.dram_tensor("packed_rows", [NSLOT, D], F32, kind="Internal").ap()
        expert_d = nc.dram_tensor("expert_rows", [NSLOT, D], F32, kind="Internal").ap()

        x_tok = sb("x_tok", [P, NT, D])
        xT_yT = sb("xT_yT", [P, 2, B * S])
        xT, yT = xT_yT[:, 0, :], xT_yT[:, 1, :]
        mlaT = xT
        early = sb("early", [P, EARLY_N])
        late = sb("late", [P, LATE_N])
        sel = sb("sel", [P, NG, 4, P], F32R)
        wa = sb("wa", [P, EA, 4 * MA])
        wb = sb("wb", [P, EB, 2 * MB])
        wc_late = sb("wc_late", [P, EC // 2, 2 * MC])
        wc = [wa[:, e, :] if e < EC // 2 else wc_late[:, e - EC // 2, :] for e in range(EC)]
        ident_r = sb("ident_r", [P, P], F32R)
        wgs = sb("wgs", [P, EA])
        gbias = sb("gbias", [P, B, EA])
        ssq = sb("ssq", [P, NT])
        rstd = sb("rstd", [P, NT])
        lg = sb("lg", [P, NT, EC])
        pr = sb("pr", [P, NT, EC])
        rmx = sb("rmx", [P, NT])
        rsm = sb("rsm", [P, NT])
        top8 = sb("top8", [P, NT, 8])
        idx8 = sb("idx8", [P, NT, 8], U32)
        idxf = sb("idxf", [P, NT, 2])
        oh = sb("oh", [P, 2, NT, EC])
        cw = sb("cw", [P, NT, EA])
        c0 = sb("c0", [P, NT, D])
        y = c0
        work = sb("work", [P, 4608])
        moe = work[:, 0:NT * D].rearrange("p (t d) -> p t d", d=D)
        h1 = work[:, 1024:2048].rearrange("p (c s) -> p c s", c=2)
        h2 = work[:, 2048:3072].rearrange("p (c s) -> p c s", c=2)
        cwT = work[0:EA, 3072:4096]
        OT, aoT, tT = work[:, 3072:3584], work[:, 3584:4096], work[:, 4096:4608]
        qH = sb("qH", [P, S], F32R)
        qL = sb("qL", [P, S], F32R)
        kH = sb("kH", [P, S], F32R)
        kL = sb("kL", [P, S], F32R)
        NV = B * TPB * H * VW
        v_c = sb("v_c", [P, NV + S])
        vaug = v_c[:, 0:NV].rearrange("p (b t h v) -> p b t h v", b=B, t=TPB, h=H)
        cT = v_c[:, NV:NV + S]
        Kp = sb("Kp", [P, 3, HPG, S], F32R)
        Qs = sb("Qs", [P, 3, S], F32R)
        Qm = sb("Qm", [P, 2, S], F32R)
        mx = sb("mx", [P, 2, TPB, HPG])
        MP = sb("MP", [P, TPB, HPG, SL], F32R)
        E4 = wc_late[:, 0:4, :].rearrange("p a (b c) -> p a b c", b=2)
        rden = sb("rden", [P, TPB, HPG])
        ao = sb("ao", [P, TPB, P])
        x1 = x_tok
        rT = sb("rT", [P, B])
        bc1c = sb("bc1c", [P, B])
        fz = sb("fz", [B, D])
        fst = sb("fst", [B, 6])
        fag = sb("fag", [B, 2])
        fsd = sb("fsd", [B, 4])
        fpT = sb("fpT", [P, B])
        fe = sb("fe", [B, S])
        faT = sb("faT", [P, TPB, B])
        coh = sb("coh", [P, TPB, H])
        coh2 = sb("coh2", [P, B, TPB, H])
        vsum = sb("vsum", [P, B, P])
        ohb = sb("ohb", [P, NT, EC], BF16)
        before_b = sb("before_b", [P, P], BF16)
        ones_b = sb("ones_b", [P, P], BF16)
        pos = sb("pos", [P, 2, NT])
        slot = sb("slot", [P, 2, NT])
        kept = sb("kept", [P, 2, NT])
        gate = sb("gate", [P, 2, NT])
        gden = sb("gden", [P, NT])
        put_at = sb("put_at", [P, 2, NT], U32)
        get_at = sb("get_at", [P, 2, NT], U32)
        pk_tok = wb[:, :, :].rearrange("p e n -> p (e n)")[:, 0:NST * D].rearrange("p (t d) -> p t d", d=D)
        eoT = v_c[:, :]
        pkT = work[:, 0:NSLOT]
        hC = work[:, NSLOT:NSLOT + 2 * FC * CAP].rearrange("p (a c n) -> p a c n", a=2, c=FC)
        eo_tok = wb[:, :, :].rearrange("p e n -> p (e n)")[:, 0:NST * D].rearrange("p (t d) -> p t d", d=D)
        got = xT_yT[:, :, :].rearrange("p k (t d) -> p k t d", d=D)

        PS = ctx.enter_context(nc.psum_tensor("PS", [P, 8, 512], F32))
        SLOTS = {"m0": (0, 1), "m1": (1, 2), "s0": (2, 4), "s1": (4, 6), "pv": (6, 7), "mi": (7, 8)}
        full = {s: sem("full_" + s) for s in SLOTS}
        taken = {s: sem("taken_" + s) for s in SLOTS}

        def ps(s):
            a, b = SLOTS[s]
            return PS[:, a, :] if b == a + 1 else PS[:, a:b, :]

        x_in, xT_in, early_in, late_in, sel_in = (sem(n) for n in ("x_in", "xT_in", "early_in", "late_in", "sel_in"))
        wa_in = [sem(f"wa_in{e}") for e in range(EA)]
        wb_in = sem("wb_in")
        wc_in = [sem(f"wc_in{q}") for q in range(4)]
        ssq_done, var_done, sd_done = sem("ssq_done"), sem("var_done"), sem("sd_done")
        gate_w_ready = sem("gate_w_ready")
        shifted, expd = sem("logits_shifted"), sem("logits_expd")
        cw_ready, cwT_ready, c0_set = sem("cw_ready"), sem("cwT_ready"), sem("c0_set")
        c0_done = sem("c0_done")
        dve_chain = sem("dve_chain")
        field_rT, field_var, field_sd, field_fp = sem("field_rT"), sem("field_var"), sem("field_sd"), sem("field_fp")
        field_mx, field_exp, field_fa = sem("field_mx"), sem("field_exp"), sem("field_fa")
        H_done, L_done = sem("high_parts"), sem("low_parts")
        V_ready = sem("V_ready")
        stack_ready = sem("stack_ready")
        MP_ready, Qm_ready = sem("maxima_placed"), sem("Qm_ready")
        pv_read = sem("exps_used")
        ao_ready = sem("ao_ready")
        mla_ready = sem("mla_ready")
        moe_set, x1_ready = sem("moe_set"), sem("x1_ready")
        coh_z, coh_e = sem("coh_shifted"), sem("coh_expd")
        y_ready = sem("y_ready")
        consts_r, consts_b, clear0 = sem("ident_r_ready"), sem("bf16_consts"), sem("cleared")
        ohb_ready = sem("ohb_ready")
        gdiff, gexp = sem("gate_difference"), sem("gate_exp")
        put_ready, get_ready = sem("put_ready"), sem("get_ready")
        zeroed, putted, pk_in = sem("packed_zeroed"), sem("rows_put"), sem("packed_in")
        eo_ready, eo_out, got_in = sem("eo_ready"), sem("eo_out"), sem("rows_got")
        out_ready, out_done = sem("out_ready"), sem("out_done")
        zero_ready = sem("zero_ready")

        def ea(name):
            a, b = EARLY_AT[name]
            return early[:, a:b]

        def la(name):
            a, b = LATE_AT[name]
            return late[:, a:b]

        ident = ea("ident")

        filled_at = {}

        def wait_full(eng, key):
            s, n = filled_at[key]
            eng.wait_ge(full[s], n)
            return ps(s)

        def wait_taken(eng, key):
            s, n = filled_at[key]
            eng.wait_ge(taken[s], n)

        NAB = B * EA
        NGB = B * NG
        STEPS = NGB * TPB

        def jobs(L, i):
            G, kt = divmod(i, TPB)
            out = []
            if kt == 0 and G + 2 < NGB:
                out += [("stackK", G + 2)]
            if kt == 1 and G + 2 < NGB:
                out += [("stackK2", G + 2)]
            if kt == 2:
                out += [("turn", G - 1)] * (G > 0) + [("stackQ", G + 2)] * (G + 2 < NGB)
            if kt == 3 and G + 1 < NGB:
                out += [("maxT", G + 1)]
            extra = {2: [("cT", 1)], 3: [("v", 1)], 6: [("qk", 1, 0)]}, \
                {1: [("cT", 1)], 2: [("v", 1)], 3: [("tanh", 1)], 5: [("coh", 1)],
                 6: [("vsum", 1), ("qk", 1, 0)], 7: [("qk", 1, 1)]}
            out += extra[L].get(i, [])
            after = NG * TPB + 3
            if i == after:
                out += [("aoT", 0)]
            if i == after + 3:
                out += [("proj", 0)]
            return out

        def first_jobs(L):
            return [("cT", 0)] + [("qk", 0, k) for k in range(1 + L)] + [("v", 0)] + \
                [("tanh", 0), ("coh", 0), ("vsum", 0)] * L + \
                [(k, G) for G in range(2) for k in ("stackK", "stackK2", "stackQ")]

        block = ctx.enter_context(nc.Block())

        @block.tensor
        def _(pe):
            fills = {s: 0 for s in SLOTS}
            mm = nc.tensor.matmul

            def claim(key, s):
                if fills[s]:
                    pe.wait_ge(taken[s], fills[s])
                fills[s] += 1
                filled_at[key] = (s, fills[s])
                return ps(s)

            def filled(last, key):
                last.then_inc(full[filled_at[key][0]], 1)

            def transposes(key, s, tiles, n=P, k=P):
                p = claim(key, s)
                for i, t in enumerate(tiles):
                    last = nc.tensor.transpose(p[0:n, i * P:i * P + k] if k == P else p[0:n, i * k:(i + 1) * k],
                                               t, ident[0:k, 0:k])
                filled(last, key)

            def field(step):
                if step == 0:
                    pe.wait_ge(late_in, 16)
                    p = claim("field0", "mi")
                    mm(p[:, 0:B], la("we1"), ea("cond"), start=True, stop=True)
                    filled(mm(p[:, B:2 * B], la("wc1c"), ea("cond"), start=True, stop=True), "field0")
                elif step == 1:
                    pe.wait_ge(field_rT, 1)
                    p = claim("field1", "mi")
                    filled(mm(p[0:B, 0:P], rT[:, :], la("we2"), start=True, stop=True), "field1")
                elif step == 2:
                    pe.wait_ge(field_fp, 1)
                    p = claim("field2", "mi")
                    filled(nc.tensor.transpose(p[:, 0:B], fz[:, :], ident[0:B, 0:B]), "field2")
                elif step == 3:
                    wait_taken(pe, "field2")
                    p = claim("field3", "mi")
                    filled(mm(p[0:B, :], fpT[:, :], la("pe"), start=True, stop=True), "field3")
                elif step == 4:
                    wait_taken(pe, "field3")
                    p = claim("field4", "mi")
                    for st in range(TPB):
                        last = nc.tensor.transpose(p[:, st * B:(st + 1) * B], fe[:, st * P:(st + 1) * P], ident[0:B, 0:B])
                    filled(last, "field4")

            pe.wait_ge(early_in, 16)
            p = claim("gb", "mi")
            for b in range(B):
                a0 = EARLY_AT["cond_rep"][0] + b * P
                last = mm(p[:, b * EA:(b + 1) * EA], early[:, a0:a0 + P], ea("gg"), start=True, stop=True)
            filled(last, "gb")
            pe.wait_ge(xT_in, 16)
            pe.wait_ge(gate_w_ready, 1)
            p = claim("gl", "m0")
            for t in range(NT):
                last = mm(p[:, t * EA:(t + 1) * EA], xT[:, t * P:(t + 1) * P], wgs[:, :], start=True, stop=True)
            filled(last, "gl")

            def a_h1(n):
                b, e = divmod(n, EA)
                if b == 0:
                    pe.wait_ge(wa_in[e], 16)
                p = claim(("a1", n), "s0")
                for c in range(2):
                    last = mm(p[:, c, :], wa[:, e, c * P:(c + 1) * P], xT[:, b * S:(b + 1) * S], start=True, stop=True)
                filled(last, ("a1", n))

            def a_h2(n):
                e = n % EA
                wait_taken(pe, ("a1", n))
                p = claim(("a2", n), "s1")
                for c in range(2):
                    for k in range(2):
                        o = MA + k * MA + c * P
                        last = mm(p[:, c, :], wa[:, e, o:o + P], h1[:, k, :], start=(k == 0), stop=(k == 1))
                filled(last, ("a2", n))

            def a_out(n):
                e = n % EA
                wait_taken(pe, ("a2", n))
                p = claim(("a3", n), "m1" if n % 2 else "m0")
                for t in range(TPB):
                    for k in range(2):
                        o = 3 * MA + k * P
                        last = mm(p[:, t * P:(t + 1) * P], h2[:, k, t * P:(t + 1) * P], wa[:, e, o:o + P],
                                  start=(k == 0), stop=(k == 1))
                filled(last, ("a3", n))

            def row_weights_bias(kind, rows):
                pe.wait_ge(cw_ready, 1 if kind == "a" else 2)
                p = claim((kind, "cwT"), "pv")
                for t in range(TPB):
                    last = nc.tensor.transpose(p[0:EA, t * P:(t + 1) * P], cw[:, t, :], ident)
                filled(last, (kind, "cwT"))
                p = claim((kind, "cwT2"), "mi")
                for t in range(TPB):
                    last = nc.tensor.transpose(p[0:EA, t * P:(t + 1) * P], cw[:, TPB + t, :], ident)
                filled(last, (kind, "cwT2"))
                for b, (key, s) in enumerate((("cwT", "pv"), ("cwT2", "mi"))):
                    wait_taken(pe, (kind, key))
                    p = claim((kind, "bias", b), s)
                    for t in range(TPB):
                        o = (b * TPB + t) * P
                        last = mm(p[:, t * P:(t + 1) * P], cwT[:, o:o + P], rows[0:EA, :], start=True, stop=True)
                    filled(last, (kind, "bias", b))

            a_h1(0)
            a_h2(0)
            row_weights_bias("a", ea("b3a"))
            for n in range(1, NAB):
                a_h1(n)
                a_out(n - 1)
                a_h2(n)
                if 3 <= n < 8:
                    field(n - 3)
            a_out(NAB - 1)

            def attention(L):
                hd = HD[L]
                src = c0 if L == 0 else x1

                def cT_(b):
                    if L == 0:
                        wait_taken(pe, ("a3", (b + 1) * EA - 1))
                    else:
                        pe.wait_ge(x1_ready, 1)
                    transposes((L, "cT", b), "mi", [src[:, b * TPB + t, :] for t in range(TPB)])

                def qk(b, i):
                    wait_taken(pe, (L, "cT", b))
                    w = la("wqk0") if L == 0 else la(("wq1", "wk1")[i])
                    filled(mm(claim((L, "qk", b, i), "mi"), w, cT, start=True, stop=True), (L, "qk", b, i))

                def v(b):
                    wait_taken(pe, (L, "cT", b))
                    p = claim((L, "v", b), "mi")
                    for t in range(TPB):
                        last = mm(p[:, t * P:t * P + H * hd], cT[:, t * P:(t + 1) * P], la("wv0" if L == 0 else "wv1"),
                                  start=True, stop=True)
                    filled(last, (L, "v", b))

                def tanh(b):
                    filled(mm(claim(("tanh", b), "mi"), la("wc1x"), cT, start=True, stop=True), ("tanh", b))

                def coh_(b):
                    wait_taken(pe, ("tanh", b))
                    p = claim(("coh", b), "mi")
                    for t in range(TPB):
                        last = mm(p[:, t * H:(t + 1) * H], tT[:, t * P:(t + 1) * P], la("wc2"), start=True, stop=True)
                    filled(last, ("coh", b))

                def vsum_(b):
                    wait_taken(pe, (L, "v", b))
                    p = claim(("vsum", b), "mi")
                    for t in range(TPB):
                        last = mm(p[:, 0:P], la("ones"), vaug[:, b, t, :, 0:hd], start=(t == 0), stop=(t == TPB - 1))
                    filled(last, ("vsum", b))

                def stack(G, i):
                    b, g = divmod(G, NG)
                    wait_taken(pe, (L, "qk", b, L))
                    hi, lo = ((kH, kL), (qH, qL))[i] if L else (qH, qL)
                    w = (2, 0)[i]
                    key = (L, "stack", G, i)
                    p = claim(key, "mi")
                    mm(p, sel[:, g, w, :], hi[:, :], start=True, stop=False)
                    filled(mm(p, sel[:, g, w + 1, :], lo[:, :], start=False, stop=True), key)

                def maxima(m, half):
                    G, qt = divmod(m, TPB)
                    if G >= NGB:
                        return
                    if qt == 0 and half == 0:
                        wait_taken(pe, (L, "stack", G, 1))
                    for j in (2 * half, 2 * half + 1):
                        p = claim((L, "max", G, qt, j), "m1" if j % 2 else "m0")
                        filled(mm(p, Qs[:, G % 3, qt * P:(qt + 1) * P], Kp[:, G % 3, j, :], start=True, stop=True),
                               (L, "max", G, qt, j))

                def place_maxima(G):
                    pe.wait_ge(MP_ready, L * NGB + G + 1)
                    p = claim((L, "mT", G), "mi")
                    for qt in range(TPB):
                        last = mm(p[:, qt * P:(qt + 1) * P], MP[:, qt, :, :].rearrange("p j s -> p (j s)"), ident_r[:, :],
                                  start=True, stop=True)
                    filled(last, (L, "mT", G))

                def scores(i, jp):
                    G, kt = divmod(i, TPB)
                    if kt == 0 and jp == 0:
                        wait_taken(pe, (L, "mT", G))
                    p = claim((L, "s", i, jp), f"s{jp}")
                    for j in range(2):
                        last = mm(p[:, j, :], Kp[:, G % 3, 2 * jp + j, kt * P:(kt + 1) * P], Qm[:, G % 2, :],
                                  start=True, stop=True)
                    filled(last, (L, "s", i, jp))

                def values(i):
                    G, kt = divmod(i, TPB)
                    b, g = divmod(G, NG)
                    if kt == 0:
                        claim((L, "pv", G), "pv")
                        wait_taken(pe, (L, "v", b))
                    p = ps("pv")
                    for jp in range(2):
                        wait_taken(pe, (L, "s", i, jp))
                    for j in range(HPG):
                        r = 2 * (i % 2) + j // 2
                        last = mm(p[SL * j:SL * j + VW, :], vaug[:, b, kt, g * HPG + j, :], E4[:, r, j % 2, :],
                                  start=(kt == 0), stop=(kt == TPB - 1), tile_position=(0, SL * j))
                    if kt < TPB - 1:
                        last.then_inc(pv_read, 1)
                    else:
                        filled(last, (L, "pv", G))

                def turn(G):
                    wait_taken(pe, (L, "pv", G))
                    transposes((L, "o", G), "mi", [OT[:, q * P:(q + 1) * P] for q in range(TPB)])

                def aoT_(b):
                    if L == 0:
                        wait_taken(pe, (L, "o", (b + 1) * NG - 1))
                    else:
                        pe.wait_ge(ao_ready, b + 1)
                    transposes((L, "aoT", b), "mi", [ao[:, q, :] for q in range(TPB)])

                def proj(b):
                    wait_taken(pe, (L, "aoT", b))
                    if L == 0:
                        filled(mm(claim(("mla", b), "mi"), la("wo0"), aoT, start=True, stop=True), ("mla", b))
                    else:
                        filled(mm(claim(("yT", b), "mi"), la("wout"), aoT, start=True, stop=True), ("yT", b))
                        p = claim(("y", b), "mi")
                        for t in range(TPB):
                            last = mm(p[:, t * P:(t + 1) * P], aoT[:, t * P:(t + 1) * P], la("wout"), start=True, stop=True)
                        filled(last, ("y", b))

                def job(name, *at):
                    if name == "stackK":
                        stack(at[0], 0)
                    elif name == "stackQ":
                        stack(at[0], 1)
                    elif name != "stackK2":
                        {"cT": cT_, "qk": qk, "v": v, "tanh": tanh, "coh": coh_, "vsum": vsum_, "turn": turn,
                         "maxT": place_maxima, "aoT": aoT_, "proj": proj}[name](*at)

                for k in first_jobs(L):
                    if k[0] == "stackK" and k[1] == 0:
                        pe.wait_ge(sel_in, 16 * (L + 1))
                    job(*k)
                for m in range(TPB + 1):
                    maxima(m, 0)
                    if m == TPB:
                        job("maxT", 0)
                    maxima(m, 1)
                for i in range(STEPS):
                    scores(i, 0)
                    scores(i, 1)
                    maxima(i + TPB + 1, 0)
                    for k in jobs(L, i):
                        job(*k)
                    if i:
                        values(i - 1)
                    maxima(i + TPB + 1, 1)
                values(STEPS - 1)
                turn(NGB - 1)
                aoT_(B - 1)
                proj(B - 1)

            pe.wait_ge(consts_r, 1)
            attention(0)

            wait_taken(pe, ("mla", B - 1))
            p = claim("bl", "m0")
            for t in range(NT):
                last = mm(p[:, t * EB:(t + 1) * EB], mlaT[:, t * P:(t + 1) * P], la("rb_w"), start=True, stop=True)
            filled(last, "bl")
            pe.wait_ge(wb_in, 16)

            def b_h1(n):
                b, e = divmod(n, EB)
                p = claim(("b1", n), f"s{n % 2}")
                for c in range(2):
                    last = mm(p[:, c, :], wb[:, e, c * P:(c + 1) * P], mlaT[:, b * S:(b + 1) * S], start=True, stop=True)
                filled(last, ("b1", n))

            def b_out(n):
                e = n % EB
                wait_taken(pe, ("b1", n))
                hb = h1 if n % 2 == 0 else h2
                p = claim(("b2", n), "m1" if n % 2 else "m0")
                for t in range(TPB):
                    for k in range(2):
                        o = MB + k * P
                        last = mm(p[:, t * P:(t + 1) * P], hb[:, k, t * P:(t + 1) * P], wb[:, e, o:o + P],
                                  start=(k == 0), stop=(k == 1))
                filled(last, ("b2", n))

            b_h1(0)
            b_h1(1)
            row_weights_bias("b", la("b2b"))
            for n in range(NAB):
                b_out(n)
                if n + 2 < NAB:
                    b_h1(n + 2)

            attention(1)

            wait_taken(pe, ("yT", B - 1))
            p = claim("cl", "m0")
            for t in range(NT):
                last = mm(p[:, t * EC:(t + 1) * EC], yT[:, t * P:(t + 1) * P], la("rc_w"), start=True, stop=True)
            filled(last, "cl")
            pe.wait_ge(ohb_ready, 1)
            pe.wait_ge(consts_b, 2)
            p = claim("count", "m1")
            for t in range(NT):
                for u in range(t + 1):
                    last = mm(p[:, t * EC:(t + 1) * EC], before_b[:, :] if u == t else ones_b[:, :], ohb[:, u, :],
                              start=(u == 0), stop=(u == t))
            filled(last, "count")
            pe.wait_ge(pk_in, 16)
            CT = ("m0", "m1", "pv", "mi")
            for q in range(NST // 4):
                transposes(("pk", q), CT[q % 4], [pk_tok[:, 4 * q + i, :] for i in range(4)])
            for q in range(NST // 4):
                wait_taken(pe, ("pk", q))

            def c_h1(e):
                if e % 4 == 0:
                    pe.wait_ge(wc_in[e // 4], 16)
                p = claim(("c1", e), f"s{e % 2}")
                for c in range(FC):
                    last = mm(p[:, c // 2, (c % 2) * CAP:(c % 2 + 1) * CAP], wc[e][:, c * P:(c + 1) * P],
                              pkT[:, e * CAP:(e + 1) * CAP], start=True, stop=True)
                filled(last, ("c1", e))

            def c_out(e):
                wait_taken(pe, ("c1", e))
                p = claim(("c2", e), "m1" if e % 2 else "m0")
                for c in range(FC):
                    o = MC + c * P
                    last = mm(p[:, 0:CAP], wc[e][:, o:o + P], hC[:, e % 2, c, :], start=(c == 0), stop=(c == FC - 1))
                filled(last, ("c2", e))

            c_h1(0)
            for e in range(EC):
                if e + 1 < EC:
                    c_h1(e + 1)
                c_out(e)
            wait_taken(pe, ("c2", EC - 1))
            wait_taken(pe, ("c2", EC - 2))
            for q in range(NST // 4):
                transposes(("eo", q), CT[q % 4], [eoT[:, (4 * q + i) * P:(4 * q + i + 1) * P] for i in range(4)])

        @block.scalar
        def _(act):
            A = nc.scalar.activation

            def field(step):
                if step == 0:
                    p = wait_full(act, "field0")
                    A(rT[:, :], p[:, 0:B], ACT.Relu, bias=la("be1")).then_inc(field_rT, 1)
                    A(bc1c[:, :], p[:, B:2 * B], ACT.Identity, bias=la("bc1")).then_inc(taken["mi"], 1)
                elif step == 1:
                    act.wait_ge(field_var, 1)
                    A(fsd[:, 1:2], fsd[:, 0:1], ACT.Sqrt).then_inc(field_sd, 1)
                elif step == 3:
                    act.wait_ge(field_mx, 1)
                    p = wait_full(act, "field3")
                    A(fe[:, :], p[0:B, :], ACT.Exp, bias=fsd[:, 2:3], accum_out=fsd[:, 3:4]).then_inc(field_exp, 1)

            act.wait_ge(x_in, 16)
            for t in range(NT):
                last = A(moe[:, t, :], x_tok[:, t, :], ACT.Square, accum_out=ssq[:, t:t + 1])
            last.then_inc(ssq_done, 1)
            act.wait_ge(var_done, 1)
            A(rstd[:, :], ssq[:, :], ACT.Sqrt).then_inc(sd_done, 1)
            act.wait_ge(shifted, 1)
            A(pr[:, :, 0:EA], lg[:, :, 0:EA], ACT.Exp).then_inc(expd, 1)
            for n in range(NAB):
                p = wait_full(act, ("a1", n))
                e = n % EA
                for c in range(2):
                    o = EARLY_AT["b1a"][0] + 2 * e + c
                    last = A(h1[:, c, :], p[:, c, :], ACT.Relu, bias=early[:, o:o + 1])
                last.then_inc(taken["s0"], 1)
                if 3 <= n < 8:
                    field(n - 3)

            def attention(L):
                def cT_(b):
                    p = wait_full(act, (L, "cT", b))
                    A(cT, p, ACT.Copy).then_inc(taken["mi"], 1)

                def qk(b, i):
                    p = wait_full(act, (L, "qk", b, i))
                    hi = kH if i else qH
                    A(hi[:, :], p, ACT.Identity, bias=la("bqk0" if L == 0 else ("bq1", "bk1")[i])).then_inc(H_done, 1)

                def tanh(b):
                    p = wait_full(act, ("tanh", b))
                    A(tT, p, ACT.Tanh, bias=bc1c[:, b:b + 1]).then_inc(taken["mi"], 1)

                def coh_(b):
                    wait_taken(act, ("coh", b))
                    A(coh[:, :, :], coh2[:, b, :, :], ACT.Exp, scale=-1.0).then_inc(coh_e, 1)

                def stackK(G, half):
                    p = wait_full(act, (L, "stack", G, 0))
                    for j in (2 * half, 2 * half + 1):
                        r = slice(SL * j, SL * (j + 1))
                        last = A(Kp[r, G % 3, j, :], p[r, :], ACT.Identity, bias=la("minus")[r, :])
                    if half:
                        last.then_inc(taken["mi"], 1)

                def stackQ(G):
                    p = wait_full(act, (L, "stack", G, 1))
                    A(Qs[:, G % 3, :], p, ACT.Copy).then_inc(taken["mi"], 1)

                def exps(i, jp):
                    G, kt = divmod(i, TPB)
                    if jp == 0 and kt != 1 and i:
                        Gu, ku = divmod(i - 2, TPB)
                        act.wait_ge(pv_read, (L * NGB + Gu) * (TPB - 1) + ku + 1)
                    p = wait_full(act, (L, "s", i, jp))
                    A(E4[:, 2 * (i % 2) + jp, :, :], p, ACT.Exp, scale=float(HD[L]) ** -0.5).then_inc(taken[f"s{jp}"], 1)

                def take_values(G):
                    p = wait_full(act, (L, "pv", G))
                    A(OT, p, ACT.Copy).then_inc(taken["pv"], 1)

                def aoT_(b):
                    p = wait_full(act, (L, "aoT", b))
                    A(aoT, p, ACT.Copy).then_inc(taken["mi"], 1)

                def proj(b):
                    if L == 0:
                        p = wait_full(act, ("mla", b))
                        A(mlaT[:, b * S:(b + 1) * S], p, ACT.Identity, bias=la("bo0")).then_inc(taken["mi"], 1)
                    else:
                        p = wait_full(act, ("yT", b))
                        A(yT[:, b * S:(b + 1) * S], p, ACT.Identity, bias=la("bout_col")).then_inc(taken["mi"], 1)

                def job(name, *at):
                    if name in ("stackK", "stackK2"):
                        stackK(at[0], int(name == "stackK2"))
                    elif name in ("cT", "qk", "tanh", "coh", "stackQ", "aoT", "proj"):
                        {"cT": cT_, "qk": qk, "tanh": tanh, "coh": coh_, "stackQ": stackQ, "aoT": aoT_,
                         "proj": proj}[name](*at)

                if L == 0:
                    act.wait_ge(clear0, 1)
                for k in first_jobs(L):
                    job(*k)
                for i in range(STEPS):
                    exps(i, 0)
                    exps(i, 1)
                    if i and i % TPB == 0:
                        take_values(i // TPB - 1)
                    for k in jobs(L, i):
                        job(*k)
                take_values(NGB - 1)
                aoT_(B - 1)
                proj(B - 1)

            attention(0)
            act.wait_ge(shifted, 2)
            A(pr[:, :, 0:EB], lg[:, :, 0:EB], ACT.Exp).then_inc(expd, 1)
            for n in range(NAB):
                p = wait_full(act, ("b1", n))
                e = n % EB
                if n >= 2:
                    wait_full(act, ("b2", n - 2))
                hb = h1 if n % 2 == 0 else h2
                for c in range(2):
                    o = LATE_AT["b1b"][0] + 2 * e + c
                    last = A(hb[:, c, :], p[:, c, :], ACT.Gelu, bias=late[:, o:o + 1])
                last.then_inc(taken[f"s{n % 2}"], 1)
            attention(1)
            act.wait_ge(gdiff, 1)
            A(gate[:, 1, :], gden[:, :], ACT.Exp).then_inc(gexp, 1)
            for q in range(1, NST // 4, 2):
                p = wait_full(act, ("pk", q))
                A(pkT[:, q * 512:(q + 1) * 512], p, ACT.Copy).then_inc(taken[filled_at[("pk", q)][0]], 1)
            for e in range(EC):
                p = wait_full(act, ("c1", e))
                if e >= 2:
                    wait_full(act, ("c2", e - 2))
                for c in range(FC):
                    o = LATE_AT["b1c"][0] + FC * e + c
                    last = A(hC[:, e % 2, c, :], p[:, c // 2, (c % 2) * CAP:(c % 2 + 1) * CAP], ACT.Gelu,
                             bias=late[:, o:o + 1])
                last.then_inc(taken[f"s{e % 2}"], 1)
            for q in range(1, NST // 4, 2):
                p = wait_full(act, ("eo", q))
                A(eo_tok[:, 4 * q:4 * q + 4, :].rearrange("p t d -> p (t d)"), p, ACT.Copy).then_inc(
                    taken[filled_at[("eo", q)][0]], 1)

        @block.vector
        def _(dve):
            V = nc.vector
            links = [0]

            def link(ins):
                links[0] += 1
                ins.then_inc(dve_chain, 1)
                dve.wait_ge(dve_chain, links[0])

            def wide(ap, n):
                return ap.unsqueeze(2).to_broadcast([ap.shape[0], ap.shape[1], n])

            def top2(E, p_or_l):
                for t in range(NT):
                    last = V.max(top8[:, t, :], p_or_l[:, t, 0:E])
                link(last)
                for t in range(NT):
                    last = V.max_index(idx8[:, t, :], top8[:, t, :], p_or_l[:, t, 0:E])
                link(last)
                link(V.tensor_copy(idxf[:, :, :], idx8[:, :, 0:2]))
                io = ea("iota")[:, 0:E].unsqueeze(1).to_broadcast([P, NT, E])
                for k in range(2):
                    last = V.tensor_tensor(oh[:, k, :, 0:E], io, wide(idxf[:, :, k], E), ALU.is_equal)
                link(last)

            def softmax8(nth):
                link(V.reduce_max(rmx[:, :], lg[:, :, 0:8], AX.X))
                V.tensor_tensor(lg[:, :, 0:8], lg[:, :, 0:8], wide(rmx[:, :], 8), ALU.subtract).then_inc(shifted, 1)
                dve.wait_ge(expd, nth)
                link(V.reduce_sum(rsm[:, :], pr[:, :, 0:8], AX.X))
                link(V.reciprocal(rsm[:, :], rsm[:, :]))
                link(V.tensor_tensor(pr[:, :, 0:8], pr[:, :, 0:8], wide(rsm[:, :], 8), ALU.mult))

            V.memset(Kp[:, :, :, :].rearrange("p a j s -> p (a j s)").bitcast(F32), 0.0).then_inc(clear0, 1)
            V.memset(MP[:, :, :, :].rearrange("p a j s -> p (a j s)").bitcast(F32), 0.0)
            V.memset(ao[:, :, :], 0.0).then_inc(zero_ready, 1)
            link(V.memset(vaug[:, :, :, :, :], 0.0))
            link(V.memset(vaug[:, :, :, :, HD[0]:HD[0] + 1], 1.0))
            dve.wait_ge(early_in, 16)
            V.tensor_copy(ident_r[:, :], ident).then_inc(consts_r, 1)
            V.tensor_scalar(wgs[:, :], ea("wg"), ea("rms"), None, ALU.mult).then_inc(gate_w_ready, 1)
            dve.wait_ge(ssq_done, 1)
            V.tensor_scalar(ssq[:, :], ssq[:, :], 1.0 / D, 1e-6, ALU.mult, ALU.add).then_inc(var_done, 1)
            p = wait_full(dve, "gb")
            pv = p[:, 0:B * EA].rearrange("p (b e) -> p b e", b=B)
            V.tensor_tensor(gbias[:, :, :], pv, ea("gg_b").unsqueeze(1).to_broadcast([P, B, EA]), ALU.add).then_inc(taken["mi"], 1)
            dve.wait_ge(taken["mi"], 1)
            link(V.tensor_tensor(gbias[:, :, :], gbias[:, :, :], ea("wg_b").unsqueeze(1).to_broadcast([P, B, EA]), ALU.add))
            dve.wait_ge(sd_done, 1)
            link(V.reciprocal(rstd[:, :], rstd[:, :]))
            p = wait_full(dve, "gl")
            pv = p[:, 0:NT * EA].rearrange("p (t e) -> p t e", e=EA)
            V.tensor_tensor(lg[:, :, 0:EA], pv, wide(rstd[:, :], EA), ALU.mult).then_inc(taken["m0"], 1)
            dve.wait_ge(taken["m0"], 1)
            for b in range(B):
                last = V.tensor_tensor(lg[:, b * TPB:(b + 1) * TPB, 0:EA], lg[:, b * TPB:(b + 1) * TPB, 0:EA],
                                       gbias[:, b, :].unsqueeze(1).to_broadcast([P, TPB, EA]), ALU.add)
            link(last)
            softmax8(1)
            top2(EA, pr)
            link(V.tensor_tensor(cw[:, :, :], oh[:, 0, :, 0:EA], oh[:, 1, :, 0:EA], ALU.add))
            V.tensor_tensor(cw[:, :, :], cw[:, :, :], pr[:, :, 0:EA], ALU.mult).then_inc(cw_ready, 1)

            def h2_out(n):
                p = wait_full(dve, ("a2", n))
                e = n % EA
                for c in range(2):
                    o = EARLY_AT["b2a"][0] + 2 * e + c
                    last = V.tensor_scalar(h2[:, c, :], p[:, c, :], early[:, o:o + 1], 0.0, ALU.add, ALU.max)
                last.then_inc(taken["s1"], 1)

            acc_at = {}

            def combine(kind, n, acc):
                b, e = divmod(n, 8)
                key = ("a3" if kind == "a" else "b2", n)
                p = wait_full(dve, key)
                if e:
                    dve.wait_ge(*acc_at[kind, n - 1])
                for t in range(TPB):
                    T = b * TPB + t
                    last = V.scalar_tensor_tensor(acc[:, T, :], p[:, t * P:(t + 1) * P], cw[:, T, e:e + 1], acc[:, T, :],
                                                  ALU.mult, ALU.add)
                last.then_inc(taken[filled_at[key][0]], 1)
                s, k = filled_at[key]
                acc_at[kind, n] = (taken[s], k)

            def bias_rows(kind, acc, done):
                p = wait_full(dve, (kind, "cwT"))
                V.tensor_copy(cwT[:, 0:S], p[0:EA, :]).then_inc(taken["pv"], 1)
                p = wait_full(dve, (kind, "cwT2"))
                V.tensor_copy(cwT[:, S:2 * S], p[0:EA, :]).then_inc(taken["mi"], 1)
                for b, s in enumerate(("pv", "mi")):
                    p = wait_full(dve, (kind, "bias", b))
                    V.tensor_copy(acc[:, b * TPB:(b + 1) * TPB, :].rearrange("p t d -> p (t d)"), p).then_inc(taken[s], 1)
                    dve.wait_ge(taken[s], filled_at[(kind, "bias", b)][1])

            def field(step):
                if step == 1:
                    p = wait_full(dve, "field1")
                    V.tensor_tensor(fz[:, :], p[0:B, 0:P], la("be2")[0:B, :], ALU.add).then_inc(taken["mi"], 1)
                    wait_taken(dve, "field1")
                    link(V.bn_stats(fst[:, :], fz[:, :]))
                    link(V.bn_aggr(fag[:, :], fst[:, :]))
                    V.tensor_scalar(fsd[:, 0:1], fag[:, 1:2], 1e-5, None, ALU.add).then_inc(field_var, 1)
                elif step == 2:
                    dve.wait_ge(field_sd, 1)
                    link(V.reciprocal(fsd[:, 2:3], fsd[:, 1:2]))
                    link(V.tensor_scalar(fz[:, :], fz[:, :], fag[:, 0:1], fsd[:, 2:3], ALU.subtract, ALU.mult))
                    link(V.tensor_tensor(fz[:, :], fz[:, :], la("ln_g")[0:B, :], ALU.mult))
                    V.tensor_tensor(fz[:, :], fz[:, :], la("ln_b")[0:B, :], ALU.add).then_inc(field_fp, 1)
                    p = wait_full(dve, "field2")
                    V.tensor_copy(fpT[:, :], p[:, 0:B]).then_inc(taken["mi"], 1)
                elif step == 3:
                    p = wait_full(dve, "field3")
                    V.tensor_reduce(fsd[:, 2:3], p[0:B, :], AX.X, ALU.max, negate=True).then_inc(field_mx, 1)
                    dve.wait_ge(field_exp, 1)
                    link(V.reciprocal(fsd[:, 3:4], fsd[:, 3:4]))
                    V.tensor_scalar(fe[:, :], fe[:, :], fsd[:, 3:4], FI, ALU.mult, ALU.mult).then_inc(taken["mi"], 1)
                elif step == 4:
                    p = wait_full(dve, "field4")
                    V.tensor_copy(faT[:, :, :], p[:, 0:TPB * B].rearrange("p (t b) -> p t b", b=B)).then_inc(taken["mi"], 1)

            h2_out(0)
            bias_rows("a", c0, c0_set)
            for n in range(1, NAB):
                combine("a", n - 1, c0)
                if n == EA + 1:
                    pass
                h2_out(n)
                if 3 <= n < 8:
                    field(n - 3)
            combine("a", NAB - 1, c0)
            dve.wait_ge(late_in, 16)
            V.tensor_copy(before_b[:, :], la("before")).then_inc(consts_b, 1)
            V.tensor_copy(ones_b[:, :], la("ones")).then_inc(consts_b, 1)

            def attention(L):
                hd = HD[L]

                def qk(b, i):
                    p = wait_full(dve, (L, "qk", b, i))
                    dve.wait_ge(H_done, (b + 1) if L == 0 else B + 2 * b + i + 1)
                    hi, lo = (kH, kL) if i else (qH, qL)
                    bias = la("bqk0" if L == 0 else ("bq1", "bk1")[i])
                    V.scalar_tensor_tensor(lo[:, :], p, bias, hi[:, :], ALU.add, ALU.subtract).then_inc(taken["mi"], 1)

                def v(b):
                    p = wait_full(dve, (L, "v", b))
                    pvv = p.rearrange("p (t c) -> p t c", t=TPB)[:, :, 0:H * hd]
                    for t in range(TPB):
                        last = V.tensor_tensor(vaug[:, b, t, :, 0:hd], pvv[:, t, :].rearrange("p (h d) -> p h d", d=hd),
                                               la("bv0" if L == 0 else "bv1").rearrange("p (h d) -> p h d", d=hd), ALU.add)
                    last.then_inc(taken["mi"], 1)

                def coh_(b):
                    p = wait_full(dve, ("coh", b))
                    V.tensor_tensor(coh2[:, b, :, :], p[:, 0:TPB * H].rearrange("p (t h) -> p t h", h=H),
                                    la("bc2").unsqueeze(1).to_broadcast([P, TPB, H]), ALU.add).then_inc(taken["mi"], 1)

                def vsum_(b):
                    p = wait_full(dve, ("vsum", b))
                    V.tensor_copy(vsum[:, b, :], p[:, 0:P]).then_inc(taken["mi"], 1)
                    dve.wait_ge(coh_e, b + 1)
                    link(V.tensor_scalar(coh[:, :, :], coh[:, :, :], 1.0, None, ALU.add))
                    link(V.reciprocal(coh[:, :, :], coh[:, :, :]))
                    link(V.tensor_scalar(coh2[:, b, :, :], coh[:, :, :], 1e-8, None, ALU.add))
                    link(V.reciprocal(coh2[:, b, :, :], coh2[:, b, :, :]))
                    link(V.scalar_tensor_tensor(coh2[:, b, :, :], coh[:, :, :], 1.0 - FI, coh2[:, b, :, :], ALU.mult, ALU.mult))

                def maxima(m, half):
                    G, qt = divmod(m, TPB)
                    if G >= NGB:
                        return
                    for j in (2 * half, 2 * half + 1):
                        key = (L, "max", G, qt, j)
                        p = wait_full(dve, key)
                        V.reduce_max(mx[:, G % 2, qt, j:j + 1], p, AX.X).then_inc(taken[filled_at[key][0]], 1)

                def place(G):
                    for j in (HPG - 2, HPG - 1):
                        wait_taken(dve, (L, "max", G, TPB - 1, j))
                    link(V.tensor_copy(MP[:, :, :, 0], mx[:, G % 2, :, :]))
                    V.tensor_tensor(MP[:, :, :, 1], mx[:, G % 2, :, :], MP[:, :, :, 0], ALU.subtract).then_inc(MP_ready, 1)

                def put_maxima(G):
                    p = wait_full(dve, (L, "mT", G))
                    V.tensor_tensor(Qm[:, G % 2, :], p, Qs[:, G % 3, :], ALU.add).then_inc(taken["mi"], 1)

                def norm(G):
                    b, g = divmod(G, NG)
                    p = wait_full(dve, (L, "o", G))
                    o = p.rearrange("p (t j s) -> p t j s", t=TPB, j=HPG)
                    link(V.reciprocal(rden[:, :, :], o[:, :, :, hd]))
                    if L == 1:
                        link(V.tensor_tensor(rden[:, :, :], rden[:, :, :], coh2[:, b, :, g * HPG:(g + 1) * HPG], ALU.mult))
                    if L == 0 and G == 0:
                        dve.wait_ge(zeroed, 16)
                    a = ao[:, :, :].rearrange("p t (h d) -> p t h d", d=hd)
                    for t in range(TPB):
                        last = V.tensor_tensor(a[:, t, g * HPG:(g + 1) * HPG, :], o[:, t, :, 0:hd], wide(rden[:, t, :], hd),
                                               ALU.mult)
                    last.then_inc(taken["mi"], 1)

                def aoT_(b):
                    if L == 1:
                        wait_taken(dve, (L, "o", (b + 1) * NG - 1))
                        for t in range(TPB):
                            last = V.scalar_tensor_tensor(ao[:, t, :], vsum[:, b, :], faT[:, t, b:b + 1], ao[:, t, :],
                                                          ALU.mult, ALU.add)
                        last.then_inc(ao_ready, 1)

                def proj(b):
                    if L == 1:
                        p = wait_full(dve, ("y", b))
                        V.tensor_tensor(y[:, b * TPB:(b + 1) * TPB, :], p.rearrange("p (t d) -> p t d", t=TPB),
                                        la("bout").unsqueeze(1).to_broadcast([P, TPB, D]), ALU.add).then_inc(taken["mi"], 1)

                def job(name, *at):
                    if name in ("qk", "v", "coh", "vsum", "turn", "maxT", "aoT", "proj"):
                        {"qk": qk, "v": v, "coh": coh_, "vsum": vsum_, "turn": norm, "maxT": put_maxima, "aoT": aoT_,
                         "proj": proj}[name](*at)

                for k in first_jobs(L):
                    job(*k)
                for m in range(TPB):
                    maxima(m, 0)
                    maxima(m, 1)
                place(0)
                maxima(TPB, 0)
                put_maxima(0)
                maxima(TPB, 1)
                for i in range(STEPS):
                    G, kt = divmod(i, TPB)
                    if kt == TPB - 1 and G + 1 < NGB:
                        place(G + 1)
                    maxima(i + TPB + 1, 0)
                    for k in jobs(L, i):
                        job(*k)
                    maxima(i + TPB + 1, 1)
                norm(NGB - 1)
                aoT_(B - 1)
                proj(B - 1)

            attention(0)
            p = wait_full(dve, "bl")
            V.tensor_tensor(lg[:, :, 0:EB], p[:, 0:NT * EB].rearrange("p (t e) -> p t e", e=EB),
                            la("rb_b").unsqueeze(1).to_broadcast([P, NT, EB]), ALU.add).then_inc(taken["m0"], 1)
            wait_taken(dve, "bl")
            softmax8(2)
            top2(EB, pr)
            link(V.tensor_tensor(rsm[:, :], top8[:, :, 0], top8[:, :, 1], ALU.add))
            link(V.tensor_scalar(rsm[:, :], rsm[:, :], 1e-8, None, ALU.add))
            link(V.reciprocal(rsm[:, :], rsm[:, :]))
            link(V.tensor_tensor(cw[:, :, :], oh[:, 0, :, 0:EB], oh[:, 1, :, 0:EB], ALU.add))
            link(V.tensor_tensor(cw[:, :, :], cw[:, :, :], pr[:, :, 0:EB], ALU.mult))
            V.tensor_tensor(cw[:, :, :], cw[:, :, :], wide(rsm[:, :], EB), ALU.mult).then_inc(cw_ready, 1)
            bias_rows("b", moe, moe_set)
            for n in range(NAB):
                combine("b", n, moe)
            for n in (EB - 1, NAB - 1):
                dve.wait_ge(*acc_at["b", n])
            link(V.scalar_tensor_tensor(moe[:, :, :], moe[:, :, :], 0.3, c0[:, :, :], ALU.mult, ALU.add))
            V.tensor_tensor(x1[:, :, :], moe[:, :, :], x_tok[:, :, :], ALU.add).then_inc(x1_ready, 1)
            V.memset(vaug[:, :, :, :, HD[1]:HD[1] + 1], 1.0)
            attention(1)

            p = wait_full(dve, "cl")
            V.tensor_tensor(lg[:, :, :], p[:, 0:NT * EC].rearrange("p (t e) -> p t e", e=EC),
                            la("rc_b").unsqueeze(1).to_broadcast([P, NT, EC]), ALU.add).then_inc(taken["m0"], 1)
            wait_taken(dve, "cl")
            top2(EC, lg)
            V.tensor_tensor(ohb[:, :, :], oh[:, 0, :, :], oh[:, 1, :, :], ALU.add).then_inc(ohb_ready, 1)
            V.tensor_tensor(gden[:, :], top8[:, :, 1], top8[:, :, 0], ALU.subtract).then_inc(gdiff, 1)
            p = wait_full(dve, "count").rearrange("p (t e) -> p t e", e=EC)[:, 0:NT, :]
            link(V.tensor_tensor(lg[:, :, :], oh[:, 0, :, :], p, ALU.mult))
            V.tensor_tensor(pr[:, :, :], oh[:, 1, :, :], p, ALU.mult).then_inc(taken["m1"], 1)
            wait_taken(dve, "count")
            V.reduce_sum(pos[:, 0, :], lg[:, :, :], AX.X)
            link(V.reduce_sum(pos[:, 1, :], pr[:, :, :], AX.X))
            for k in range(2):
                last = V.scalar_tensor_tensor(slot[:, k, :], idxf[:, :, k], float(CAP), pos[:, k, :], ALU.mult, ALU.add)
            link(last)
            link(V.tensor_scalar(kept[:, :, :], pos[:, :, :], float(CAP), None, ALU.is_lt))
            link(V.tensor_scalar(pos[:, :, :], kept[:, :, :], -2.0 * NSLOT, 2.0 * NSLOT, ALU.mult, ALU.add))
            link(V.tensor_tensor(pos[:, :, :], pos[:, :, :], slot[:, :, :], ALU.add))
            V.tensor_copy(put_at[:, :, :], pos[:, :, :]).then_inc(put_ready, 1)
            link(V.tensor_scalar(slot[:, :, :], slot[:, :, :], float(NSLOT - 1), None, ALU.min))
            V.tensor_copy(get_at[:, :, :], slot[:, :, :]).then_inc(get_ready, 1)
            dve.wait_ge(gexp, 1)
            link(V.tensor_scalar(gden[:, :], gate[:, 1, :], 1.0, None, ALU.add))
            link(V.reciprocal(gate[:, 0, :], gden[:, :]))
            link(V.tensor_tensor(gate[:, 1, :], gate[:, 1, :], gate[:, 0, :], ALU.mult))
            link(V.tensor_tensor(gate[:, :, :], gate[:, :, :], kept[:, :, :], ALU.mult))
            link(V.tensor_tensor(gden[:, :], gate[:, 0, :], gate[:, 1, :], ALU.add))
            link(V.tensor_scalar(gden[:, :], gden[:, :], 1e-9, None, ALU.add))
            link(V.reciprocal(gden[:, :], gden[:, :]))
            for k in range(2):
                last = V.tensor_tensor(gate[:, k, :], gate[:, k, :], gden[:, :], ALU.mult)
            link(last)
            for q in range(0, NST // 4, 2):
                p = wait_full(dve, ("pk", q))
                V.tensor_copy(pkT[:, q * 512:(q + 1) * 512], p).then_inc(taken[filled_at[("pk", q)][0]], 1)
            for e in range(EC):
                p = wait_full(dve, ("c2", e))
                o = LATE_AT["b2c"][0] + e
                V.tensor_scalar(eoT[:, e * CAP:(e + 1) * CAP], p[:, 0:CAP], late[:, o:o + 1], None, ALU.add).then_inc(
                    taken[filled_at[("c2", e)][0]], 1)
            for q in range(0, NST // 4, 2):
                p = wait_full(dve, ("eo", q))
                V.tensor_copy(eo_tok[:, 4 * q:4 * q + 4, :].rearrange("p t d -> p (t d)"), p).then_inc(
                    taken[filled_at[("eo", q)][0]], 1)
            for t in range(NT):
                dve.wait_ge(got_in, 16 * 2 * NT) if t == 0 else None
                link(V.scalar_tensor_tensor(x1[:, t, :], got[:, 0, t, :], gate[:, 0, t:t + 1], x1[:, t, :], ALU.mult, ALU.add))
                last = V.scalar_tensor_tensor(x1[:, t, :], got[:, 1, t, :], gate[:, 1, t:t + 1], x1[:, t, :], ALU.mult, ALU.add)
            last.then_inc(out_ready, 1)

        @block.sync
        def _(sp):
            sp.dma_start(early[:, :], early_d).then_inc(early_in, 16)
            sp.dma_start(x_tok[:, :, :], x_tok_d).then_inc(x_in, 16)
            sp.dma_start(xT[:, :], xT_d).then_inc(xT_in, 16)
            for e in range(EA):
                sp.dma_start(wa[:, e, :], wa_d[:, e, :]).then_inc(wa_in[e], 16)
            sp.dma_start(late[:, :], late_d).then_inc(late_in, 16)
            sp.wait_ge(zero_ready, 1)
            sp.dma_start(packed_d.rearrange("(p r) d -> p (r d)", p=P).rearrange("p (a n) -> p a n", n=512),
                         ao[:, :, :].rearrange("p t d -> p (t d)").unsqueeze(1).to_broadcast([P, NSLOT // P * D // 512, 512])).then_inc(zeroed, 16)
            sp.dma_start(wb[:, :, :], wb_d).then_inc(wb_in, 16)
            wait_taken(sp, ("a3", NAB - 1))
            for q in (0, 1):
                sp.dma_start(wa[:, 4 * q:4 * q + 4, :], wc_d[:, 4 * q:4 * q + 4, :]).then_inc(wc_in[q], 16)
            wait_taken(sp, (1, "pv", B * NG - 1))
            for q in (2, 3):
                sp.dma_start(wc_late[:, 4 * q - 8:4 * q - 4, :], wc_d[:, 4 * q:4 * q + 4, :]).then_inc(wc_in[q], 16)
            sp.wait_ge(putted, 16 * 2 * NT)
            sp.dma_start(pk_tok, packed_d.rearrange("(t p) d -> p t d", p=P)).then_inc(pk_in, 16)
            for q in range(NST // 4):
                wait_taken(sp, ("eo", q))
            sp.dma_start(expert_d.rearrange("(t p) d -> p t d", p=P), eo_tok).then_inc(eo_out, 16)
            sp.wait_ge(out_ready, 1)
            sp.dma_start(out_d, x1[:, :, :]).then_inc(out_done, 16)
            sp.wait_ge(out_done, 16)

        @block.gpsimd
        def _(pool):
            pool.dma_start(sel[:, :, :, :].rearrange("p g w s -> p (g w s)"), sel_d[:, 0, :]).then_inc(sel_in, 16)
            wait_full(pool, (0, "stack", B * NG - 1, 1))
            pool.dma_start(sel[:, :, :, :].rearrange("p g w s -> p (g w s)"), sel_d[:, 1, :]).then_inc(sel_in, 16)
            pool.wait_ge(zeroed, 16)
            pool.wait_ge(put_ready, 1)
            for t in range(NT):
                for k in range(2):
                    pool.indirect_dma_start(out=packed_d, out_offset=bass.IndirectOffsetOnAxis(ap=put_at[:, k, t:t + 1], axis=0),
                                            in_=y[:, t, :], in_offset=None, bounds_check=NSLOT - 1,
                                            oob_is_err=False).then_inc(putted, 16)
            pool.wait_ge(get_ready, 1)
            pool.wait_ge(eo_out, 16)
            for t in range(NT):
                for k in range(2):
                    pool.indirect_dma_start(out=got[:, k, t, :], out_offset=None, in_=expert_d,
                                            in_offset=bass.IndirectOffsetOnAxis(ap=get_at[:, k, t:t + 1], axis=0)
                                            ).then_inc(got_in, 16)


def kernel(**inputs):
    import numpy as np
    import concourse.bacc as bacc
    from concourse.bass_utils import run_bass_kernel_spmd

    a = {k: np.asarray(v) for k, v in inputs.items()}
    f4 = np.float32

    def rows(m):
        m = np.asarray(m, f4)
        out = np.zeros((P, m.shape[1]), f4)
        out[:m.shape[0]] = m
        return out

    def rep(v):
        return np.broadcast_to(np.asarray(v, f4).reshape(1, -1), (P, v.size))

    def cols(v):
        return np.asarray(v, f4).reshape(-1, P).T

    x = a["x"].reshape(B * S, D)
    cond = a["cond_256"]
    q_w = a["L0_ffn_q_w"].reshape(D, H, D // H)[:, :, :HD[0]].reshape(D, H * HD[0])
    q_b = a["L0_ffn_q_b"].reshape(H, D // H)[:, :HD[0]].reshape(-1)
    wqkv, bqkv = a["L1_cond_Wqkv"], a["L1_cond_bqkv"]
    wc1 = a["L1_cond_Wc1"]
    s_, e_ = np.arange(S, dtype=f4), np.arange(0, D, 2, dtype=f4)
    inv = f4(10000.0) ** np.repeat(e_ / f4(D), 2)
    early = {
        "wg": a["L0_cond_wg_W"], "rms": cols(a["L0_cond_rms_w"]), "gg": rows(a["L0_cond_gg_W"]),
        "cond_rep": rows(np.repeat(cond.T[:, :, None], P, axis=2).reshape(CD, B * P)),
        "wg_b": rep(a["L0_cond_wg_b"]), "gg_b": rep(a["L0_cond_gg_b"]),
        "b1a": cols(a["L0_cond_b1"]), "b2a": cols(a["L0_cond_b2"]), "b3a": rows(a["L0_cond_b3"]),
        "cond": rows(cond.T), "iota": rep(np.arange(EC, dtype=f4)), "ident": np.eye(P, dtype=f4),
    }
    minus = np.zeros((P, 1), f4)
    for j in range(HPG):
        minus[SL * j:SL * j + 2] = -1.0
    late = {
        "wqk0": np.concatenate([q_w, a["L0_ffn_k_w"]], 1), "bqk0": cols(np.concatenate([q_b, a["L0_ffn_k_b"]])),
        "wv0": a["L0_ffn_v_w"], "bv0": rep(a["L0_ffn_v_b"]), "wo0": a["L0_ffn_o_w"], "bo0": cols(a["L0_ffn_o_b"]),
        "rb_w": a["L0_ffn_router_w"], "rb_b": rep(a["L0_ffn_router_b"]), "b1b": cols(a["L0_ffn_b1"]),
        "b2b": rows(a["L0_ffn_b2"]),
        "wq1": wqkv[0:D].T, "wk1": wqkv[D:2 * D].T, "wv1": wqkv[2 * D:3 * D].T,
        "bq1": cols(bqkv[0:D]), "bk1": cols(bqkv[D:2 * D]), "bv1": rep(bqkv[2 * D:3 * D]),
        "wc1x": wc1[:, :D].T, "wc1c": rows(wc1[:, D:].T), "bc1": cols(a["L1_cond_bc1"]),
        "wc2": a["L1_cond_Wc2"].T, "bc2": rep(a["L1_cond_bc2"]),
        "we1": rows(a["L1_cond_We1"].T), "be1": cols(a["L1_cond_be1"]), "we2": a["L1_cond_We2"].T,
        "be2": rep(a["L1_cond_be2"]), "ln_g": rep(a["L1_cond_ln_g"]), "ln_b": rep(a["L1_cond_ln_b"]),
        "pe": np.sin(s_[:, None] / inv[None, :]).T,
        "wout": a["L1_cond_Wout"].T, "bout_col": cols(a["L1_cond_bout"]), "bout": rep(a["L1_cond_bout"]),
        "rc_w": a["L1_ffn_router_w"].T, "rc_b": rep(a["L1_ffn_router_b"]),
        "b1c": cols(a["L1_ffn_b1"]), "b2c": cols(a["L1_ffn_b2"]),
        "before": np.triu(np.ones((P, P), f4), 1), "ones": np.ones((P, P), f4), "minus": minus,
    }
    sel = np.zeros((P, 2, NG, 4, P), f4)
    for L in range(2):
        for g in range(NG):
            for j in range(HPG):
                for d in range(HD[L]):
                    q = (g * HPG + j) * HD[L] + d
                    k = q + (H * HD[0] if L == 0 else 0)
                    s0, s1, s2 = (SL * j + 2 + i * HD[L] + d for i in range(3))
                    sel[q, L, g, 0, [s0, s1]] = 1
                    sel[q, L, g, 1, s2] = 1
                    sel[k, L, g, 2, [s0, s2]] = 1
                    sel[k, L, g, 3, s1] = 1

    def chunks(w):
        e, k, n = w.shape
        return w.reshape(e, k // P, P, n).transpose(2, 0, 1, 3).reshape(P, e, -1)

    arrays = {
        "x_tok": x.reshape(NT, P, D).transpose(1, 0, 2), "xT": x.T,
        "early": np.concatenate([early[n] for n, _ in EARLY], 1),
        "late": np.concatenate([late[n] for n, _ in LATE], 1),
        "sel": sel.reshape(P, 2, -1),
        "wa": np.concatenate([chunks(a[f"L0_cond_W{i}"]) for i in (1, 2, 3)], 2),
        "wb": np.concatenate([chunks(a[f"L0_ffn_w{i}"]) for i in (1, 2)], 2),
        "wc": np.concatenate([chunks(a[f"L1_ffn_w{i}"]) for i in (1, 2)], 2),
    }
    arrays = {k + "_dram": np.ascontiguousarray(v) for k, v in arrays.items()}
    nc = bacc.Bacc("TRN2", target_bir_lowering=False, num_devices=1)
    args = [nc.dram_tensor(k, v.shape, mybir.dt.from_np(v.dtype), kind="ExternalInput").ap() for k, v in arrays.items()]
    out = nc.dram_tensor("out_dram", (P, NT, D), mybir.dt.float32, kind="ExternalOutput").ap()
    build(nc, *args, out)
    r = run_bass_kernel_spmd(nc, [arrays], core_ids=[0])
    got = r.results[0]["out_dram"]
    return np.ascontiguousarray(got.transpose(1, 0, 2)).reshape(B, S, D)
```

```python
import concourse.bass as bass
from concourse import mybir
from contextlib import ExitStack

P = 128
B, S, D = 2, 512, 128
TPB = S // P
NT = B * TPB
EA, MA = 8, 256
EB, MB = 8, 256
EC, MC = 16, 512
CAP = 160
NSLOT = EC * CAP
NST = NSLOT // P
ROW = D + 1
NPAIR = 2 * B * S
H = 16
HPG = 4
NG = H // HPG
SL = 32
VW = 16
HD = (4, 8)
FC = MC // P
CD = 32
FI = 0.3 * 0.7

EARLY = [("wg", EA), ("rms", 1), ("gg", EA), ("cond_rep", B * P), ("wg_b", EA), ("gg_b", EA),
         ("b1a", 2 * EA), ("b2a", 2 * EA), ("b3a", P), ("cond", B), ("iota", EC), ("ident", P)]
LATE = [("wqk0", P), ("bqk0", 1), ("wv0", H * HD[0]), ("bv0", H * HD[0]), ("wo0", P), ("bo0", 1),
        ("rb_w", EB), ("rb_b", EB), ("b1b", 2 * EB), ("b2b", P),
        ("wq1", P), ("wk1", P), ("wv1", P), ("bq1", 1), ("bk1", 1), ("bv1", P),
        ("wc1x", P), ("wc1c", P), ("bc1", 1), ("wc2", H), ("bc2", H),
        ("we1", P), ("be1", 1), ("we2", P), ("be2", P), ("ln_g", P), ("ln_b", P), ("pe", S),
        ("wout", P), ("bout_col", 1), ("bout", P), ("rc_w", EC), ("rc_b", EC),
        ("b1c", EC * FC), ("b2c", EC), ("before", P), ("ones", P), ("minus", 1), ("pair", 2 * NT)]


def places(fields):
    at, out = 0, {}
    for name, n in fields:
        out[name] = (at, at + n)
        at += n
    return out, at


EARLY_AT, EARLY_N = places(EARLY)
LATE_AT, LATE_N = places(LATE)


def build(nc, x_tok_d, xT_d, early_d, late_d, sel_d, wa_d, wb_d, wc_d, out_d):
    F32, F32R, BF16, U32 = mybir.dt.float32, mybir.dt.float32r, mybir.dt.bfloat16, mybir.dt.uint32
    ALU, ACT, AX = mybir.AluOpType, mybir.ActivationFunctionType, mybir.AxisListType
    ctx = ExitStack()
    with ctx:
        def sb(name, shape, dt=F32):
            return ctx.enter_context(nc.sbuf_tensor(name, shape, dt))

        def sem(name):
            return ctx.enter_context(nc.semaphore(name))

        packed_d = nc.dram_tensor("packed_rows", [NSLOT, ROW], F32, kind="Internal").ap()
        pair_d = nc.dram_tensor("result_pairs", [NPAIR, D], F32, kind="Internal").ap()

        REGIONS = (("xT_yT", 2 * B * S), ("wa", EA * 4 * MA), ("wb", EB * 2 * MB), ("wc_late", EC // 2 * 2 * MC),
                   ("work", 4608))
        with ExitStack() as once:
            f32_at = {name: once.enter_context(nc.sbuf_tensor(name, [P, n], F32)) for name, n in REGIONS}
        f32r_at = {name: sb(name + "_r", [P, n], F32R) for name, n in REGIONS}
        x_tok = sb("x_tok", [P, NT, D])
        xT_yT = f32_at["xT_yT"][:, :].rearrange("p (k s) -> p k s", k=2)
        xT, yT = xT_yT[:, 0, :], xT_yT[:, 1, :]
        mlaT = xT
        early = sb("early", [P, EARLY_N])
        late = sb("late", [P, LATE_N])
        sel = sb("sel", [P, NG, 4, P], F32R)
        wa = f32_at["wa"][:, :].rearrange("p (e n) -> p e n", e=EA)
        wb = f32_at["wb"][:, :].rearrange("p (e n) -> p e n", e=EB)
        wc_late = f32_at["wc_late"][:, :].rearrange("p (e n) -> p e n", e=EC // 2)
        wc = [wa[:, e, :] if e < EC // 2 else wc_late[:, e - EC // 2, :] for e in range(EC)]
        ident_r = sb("ident_r", [P, P], F32R)
        wgs = sb("wgs", [P, EA])
        gbias = sb("gbias", [P, B, EA])
        ssq = sb("ssq", [P, NT])
        rstd = sb("rstd", [P, NT])
        lg = sb("lg", [P, NT, EC])
        pr = sb("pr", [P, NT, EC])
        rmx = sb("rmx", [P, NT])
        rsm = sb("rsm", [P, NT])
        top8 = sb("top8", [P, NT, 8])
        idx8 = sb("idx8", [P, NT, 8], U32)
        idxf = sb("idxf", [P, NT, 2])
        oh = sb("oh", [P, 2, NT, EC])
        cw = sb("cw", [P, NT, EA])
        c0 = sb("c0", [P, NT, D])
        work = f32_at["work"]
        to_pack = work[:, 0:2 * NT * ROW].rearrange("p (k t c) -> p k t c", k=2, t=NT)
        y = to_pack[:, 0, :, 0:D]
        squares = work[:, 0:NT * D].rearrange("p (t d) -> p t d", d=D)
        h1 = work[:, 1024:2048].rearrange("p (c s) -> p c s", c=2)
        h2 = work[:, 2048:3072].rearrange("p (c s) -> p c s", c=2)
        cwT = work[0:EA, 4096:4608]
        OT, aoT, tT = work[:, 3072:3584], work[:, 3584:4096], work[:, 4096:4608]
        h1_whole = [h1, work[:, 3072:4096].rearrange("p (c s) -> p c s", c=2)]
        qH = sb("qH", [P, S], F32R)
        qL = sb("qL", [P, S], F32R)
        kH = sb("kH", [P, S], F32R)
        kL = sb("kL", [P, S], F32R)
        NV = B * TPB * H * VW
        v_c = sb("v_c", [P, NV + S])
        vaug = v_c[:, 0:NV].rearrange("p (b t h v) -> p b t h v", b=B, t=TPB, h=H)
        cT = v_c[:, NV:NV + S]
        Kp = sb("Kp", [P, 3, HPG, S], F32R)
        Ks = sb("Ks", [P, 2, S])
        Qs = sb("Qs", [P, 3, S], F32R)
        Qm = sb("Qm", [P, 2, S], F32R)
        mx = sb("mx", [P, 2, TPB, HPG])
        MP = sb("MP", [P, TPB, HPG, SL], F32R)
        E4 = wc_late[:, 0:4, :].rearrange("p a (b c) -> p a b c", b=2)
        spare, wa_r, wb_r = f32r_at["wc_late"], f32r_at["wa"], f32r_at["wb"]
        wa_high = [spare[:, e * 3 * MA:(e + 1) * 3 * MA] for e in range(EA)]
        wa_low = [wa_r[:, e * 4 * MA:e * 4 * MA + 3 * MA] for e in range(EA)]
        h1_high = [spare[:, 6144 + 1024 * i:7168 + 1024 * i].rearrange("p (c s) -> p c s", c=2) for i in range(2)]
        h1_low = [t.rearrange("p (c s) -> p c s", c=2)
                  for t in (f32r_at["work"][:, 0:2 * S], f32r_at["xT_yT"][:, B * S:])]
        x_high, x_low = (Qs[:, 0, :], Qs[:, 2, :]), (Qs[:, 1, :], Qm[:, 1, :])
        wb_high = [spare[:, 6144 + e * MB:6144 + (e + 1) * MB] for e in range(EB)]
        wb_low = [wb_r[:, e * 2 * MB:e * 2 * MB + MB] for e in range(EB)]
        mla_high, mla_low = (spare[:, 4096 + 1024 * i:5120 + 1024 * i] for i in range(2))
        rden = sb("rden", [P, TPB, HPG])
        ao = sb("ao", [P, TPB, P])
        x1 = x_tok
        rT = sb("rT", [P, B])
        bc1c = sb("bc1c", [P, B])
        fz = sb("fz", [B, D])
        fst = sb("fst", [B, 6])
        fag = sb("fag", [B, 2])
        fsd = sb("fsd", [B, 4])
        fpT = sb("fpT", [P, B])
        fe = sb("fe", [B, S])
        coh = sb("coh", [P, TPB, H])
        coh2 = sb("coh2", [P, B, TPB, H])
        vsum = sb("vsum", [B, B, P])
        ohb = sb("ohb", [P, NT, EC], BF16)
        before_b = sb("before_b", [P, P], BF16)
        ones_b = sb("ones_b", [P, P], BF16)
        pos = sb("pos", [P, 2, NT])
        slot = sb("slot", [P, 2, NT])
        kept = sb("kept", [P, 2, NT])
        gate = sb("gate", [P, 2, NT])
        gden = sb("gden", [P, NT])
        put_at = sb("put_at", [P, 2, NT], U32)
        back_at = sb("back_at", [P, NST], U32)
        pk_tok = wb[:, :, :].rearrange("p e n -> p (e n)")[:, 0:NST * ROW].rearrange("p (t c) -> p t c", c=ROW)
        eoT = v_c[:, :]
        pkT = work[:, 0:NSLOT]
        hC = work[:, NSLOT:NSLOT + 2 * FC * CAP].rearrange("p (a c n) -> p a c n", a=2, c=FC)
        eo_tok = wb[:, :, :].rearrange("p e n -> p (e n)")[:, 0:NST * D].rearrange("p (t d) -> p t d", d=D)
        got = f32_at["xT_yT"][:, :].rearrange("p (t k d) -> p t k d", k=2, d=D)

        PS = ctx.enter_context(nc.psum_tensor("PS", [P, 8, 512], F32))
        SLOTS = {"m0": (0, 1), "m1": (1, 2), "s0": (2, 4), "s1": (4, 6), "pv": (6, 7), "mi": (7, 8)}
        full = {s: sem("full_" + s) for s in SLOTS}
        taken = {s: sem("taken_" + s) for s in SLOTS}

        def ps(s):
            a, b = SLOTS[s]
            return PS[:, a, :] if b == a + 1 else PS[:, a:b, :]

        x_in, xT_in, early_in, late_in, sel_in = (sem(n) for n in ("x_in", "xT_in", "early_in", "late_in", "sel_in"))
        wa_in = [sem(f"wa_in{e}") for e in range(EA)]
        wb_in = sem("wb_in")
        wc_in = [sem(f"wc_in{q}") for q in range(4)]
        consts_r, consts_b = sem("ident_r_ready"), sem("bf16_consts")
        zero_ready, pool_clear, clear0 = sem("zero_ready"), sem("pool_clear"), sem("cleared")
        ssq_done, var_done, sd_done = sem("ssq_done"), sem("var_done"), sem("sd_done")
        gate_w_ready = sem("gate_w_ready")
        shifted, expd, cw_ready = sem("logits_shifted"), sem("logits_expd"), sem("cw_ready")
        dve_chain = sem("dve_chain")
        x_high_set, x_low_set = sem("x_high_set"), sem("x_low_set")
        h1_high_set, h1_low_set = sem("h1_high_set"), sem("h1_low_set")
        wa_high_set, wa_split, wa_split0 = sem("wa_high_set"), sem("wa_split"), sem("wa_split0")
        wb_high_set, wb_split = sem("wb_high_set"), sem("wb_split")
        mla_high_set, mla_split = sem("mla_high_set"), sem("mla_split")
        field_rT, field_var, field_sd, field_fp = sem("field_rT"), sem("field_var"), sem("field_sd"), sem("field_fp")
        field_mx, field_exp = sem("field_mx"), sem("field_exp")
        H_done, Kp_set, MP_ready, pv_read = sem("high_parts"), sem("Kp_set"), sem("maxima_placed"), sem("exps_used")
        coh_e, x_cond_set = sem("coh_expd"), sem("x_plus_cond")
        ohb_ready = sem("ohb_ready")
        gdiff, gexp = sem("gate_difference"), sem("gate_exp")
        put_ready, back_ready, pack_ready = sem("put_ready"), sem("back_ready"), sem("rows_to_pack")
        zeroed, putted, pk_in = sem("packed_zeroed"), sem("rows_put"), [sem(f"packed_in{q}") for q in range(NST // 4)]
        eo_out, got_in = sem("results_out"), [sem(f"results_in{c}") for c in range(NT // 2)]
        out_ready, out_done = sem("out_ready"), sem("out_done")

        def ea(name):
            a, b = EARLY_AT[name]
            return early[:, a:b]

        def la(name):
            a, b = LATE_AT[name]
            return late[:, a:b]

        ident = ea("ident")

        filled_at = {}

        def wait_full(eng, key):
            s, n = filled_at[key]
            eng.wait_ge(full[s], n)
            return ps(s)

        def wait_taken(eng, key):
            s, n = filled_at[key]
            eng.wait_ge(taken[s], n)

        NAB = B * EA
        NGB = B * NG
        STEPS = NGB * TPB

        def maxima_at(i, place):
            n = 3 if i in (TPB - 1, TPB) else 2
            first = 2 * (i + TPB + 1) + (0 if i < TPB else 1 if i == TPB else 2)
            return [divmod(h, 2) for h in (range(first, first + 1) if place == 0 else range(first + 1, first + n))]

        KEYS = NGB - 3

        def jobs(L, i, place):
            G, kt = divmod(i, TPB)
            more = G + 2 < NGB
            if place == 0:
                return {0: [("stackK2", G + 2)] * (more and G > 0), 1: [("stackQ", G + 2)] * more,
                        2: [("turn", G - 1)] * (G > 0),
                        3: [("maxT", G + 1)] * (G + 1 < NGB)}[kt]
            out = ({2: [("cT", 1)], 6: [("qk", 1, 0)], 9: [("v", 1)]},
                   {1: [("vsum", 0)], 2: [("cT", 1)], 5: [("qk", 1, 0)], 6: [("qk", 1, 1)], 9: [("tanh", 1)],
                    10: [("coh", 1)], 13: [("v", 1)], 14: [("vsum", 1)]})[L].get(i, [])
            out += {NG * TPB + 5: [("aoT", 0)], NG * TPB + 6: [("proj", 0)],
                    NG * TPB + 9: [("y", 0)] * L,
                    **({STEPS - 6: [("logits", 0)], STEPS - 4: [("count", 0)]} if L else
                       {STEPS - 4: [("logits", 0)], STEPS - 2: [("weightsT", 0)], STEPS - 1: [("bias", 0)]})}.get(i, [])
            return out + [("stackK", G + 3)] * (kt == TPB - 1 and G + 3 < NGB)

        halves = [("max", m, half) for m in range(TPB) for half in range(2)]
        early_jobs = [{(8, 1): [("cT", 0)], (9, 0): [("qk", 0, 0)], (9, 1): [("v", 0)],
                       (10, 0): [("stackK", 0), ("stackK2", 0)], (10, 1): [("stackQ", 0)],
                       (12, 1): [("stackK", 1), ("stackK2", 1)], (13, 1): [("stackQ", 1)],
                       (14, 1): [("stackK", 2), ("stackK2", 2), ("place", 0)],
                       (15, 0): [("maxT", 0), ("max", TPB, 0)], (15, 1): [("max", TPB, 1)]},
                      {(8, 0): [("cT", 0)], (8, 1): [("qk", 0, 0)], (9, 0): [("qk", 0, 1)],
                       (9, 1): [("stackK", 0), ("stackK2", 0)], (10, 1): [("stackQ", 0)], (11, 0): [("v", 0)],
                       (11, 1): [("stackK", 1), ("stackK2", 1)], (12, 1): [("stackQ", 1)], (13, 0): [("tanh", 0)],
                       (13, 1): [("stackK", 2), ("stackK2", 2)], (14, 1): [("place", 0), ("coh", 0)],
                       (15, 0): [("maxT", 0), ("max", TPB, 0)], (15, 1): [("max", TPB, 1)]}]
        for L in range(2):
            for k, half in enumerate(halves):
                at = (11 + k // 2, k % 2)
                early_jobs[L][at] = [half] + early_jobs[L].get(at, [])

        late_jobs = {0: [("turn", NGB - 1)], 1: [("aoT", B - 1)], 2: [("proj", B - 1)], 3: [("logits", B - 1)],
                     5: [("weightsT", B - 1)], 6: [("bias", B - 1)]}

        NQ = NST // 4
        ROWS, EO_ROWS = 4 * P, 2 * P
        c_steps, pks, eos = [], 0, 0
        for e in range(-1, EC):
            while pks * ROWS < min(e + 3, EC) * CAP and (pks * ROWS < (e + 2) * CAP or e >= 0):
                c_steps.append(("pk", pks))
                pks += 1
            if e + 1 < EC:
                c_steps.append(("h1", e + 1))
            while (eos + 1) * EO_ROWS <= e * CAP:
                c_steps.append(("eo", eos))
                eos += 1
            if e >= 0:
                c_steps.append(("out", e))
        c_steps += [("eo", k) for k in range(eos, 2 * NQ)]

        block = ctx.enter_context(nc.Block())

        @block.tensor
        def _(pe):
            fills = {s: 0 for s in SLOTS}
            mm = nc.tensor.matmul

            def claim(key, s):
                if fills[s]:
                    pe.wait_ge(taken[s], fills[s])
                fills[s] += 1
                filled_at[key] = (s, fills[s])
                return ps(s)

            def filled(last, key):
                last.then_inc(full[filled_at[key][0]], 1)

            def transposes(key, s, tiles, n=P, k=P):
                p = claim(key, s)
                for i, t in enumerate(tiles):
                    last = nc.tensor.transpose(p[0:n, i * P:i * P + k] if k == P else p[0:n, i * k:(i + 1) * k],
                                               t, ident[0:k, 0:k])
                filled(last, key)

            def keep_warm(n):
                pe.wait_ge(taken["m0"], fills["m0"])
                for _ in range(n):
                    mm(ps("m0"), Qs[:, 0, 0:P], Kp[:, 0, 0, :], start=True, stop=True)

            def field(step):
                if step == 0:
                    pe.wait_ge(late_in, 16)
                    p = claim("field0", "mi")
                    mm(p[:, 0:B], la("we1"), ea("cond"), start=True, stop=True)
                    filled(mm(p[:, B:2 * B], la("wc1c"), ea("cond"), start=True, stop=True), "field0")
                elif step == 1:
                    pe.wait_ge(field_rT, 1)
                    p = claim("field1", "mi")
                    filled(mm(p[0:B, 0:P], rT[:, :], la("we2"), start=True, stop=True), "field1")
                elif step == 2:
                    pe.wait_ge(field_fp, 1)
                    p = claim("field2", "mi")
                    filled(nc.tensor.transpose(p[:, 0:B], fz[:, :], ident[0:B, 0:B]), "field2")
                elif step == 3:
                    wait_taken(pe, "field2")
                    p = claim("field3", "mi")
                    filled(mm(p[0:B, :], fpT[:, :], la("pe"), start=True, stop=True), "field3")

            def attention(L):
                hd = HD[L]
                src = c0 if L == 0 else x1

                def cT_(b):
                    wait_taken(pe, ("b2" if L else "a3", (b + 1) * EA - 1))
                    transposes((L, "cT", b), "mi", [src[:, b * TPB + t, :] for t in range(TPB)])

                def qk(b, i):
                    wait_taken(pe, (L, "cT", b))
                    w = la("wqk0") if L == 0 else la(("wq1", "wk1")[i])
                    filled(mm(claim((L, "qk", b, i), "mi"), w, cT, start=True, stop=True), (L, "qk", b, i))

                def v(b):
                    wait_taken(pe, (L, "cT", b))
                    p = claim((L, "v", b), "mi")
                    for t in range(TPB):
                        last = mm(p[:, t * P:t * P + H * hd], cT[:, t * P:(t + 1) * P], la("wv0" if L == 0 else "wv1"),
                                  start=True, stop=True)
                    filled(last, (L, "v", b))

                def tanh(b):
                    filled(mm(claim(("tanh", b), "mi"), la("wc1x"), cT, start=True, stop=True), ("tanh", b))

                def coh_(b):
                    wait_taken(pe, ("tanh", b))
                    p = claim(("coh", b), "mi")
                    for t in range(TPB):
                        last = mm(p[:, t * H:(t + 1) * H], tT[:, t * P:(t + 1) * P], la("wc2"), start=True, stop=True)
                    filled(last, ("coh", b))

                def vsum_(b):
                    wait_taken(pe, (L, "v", b))
                    p = claim(("vsum", b), "mi")
                    for t in range(TPB):
                        last = mm(p[:, 0:P], la("ones"), vaug[:, b, t, :, 0:hd], start=(t == 0), stop=(t == TPB - 1))
                    filled(last, ("vsum", b))

                def stack(G, i):
                    b, g = divmod(G, NG)
                    if G == 0:
                        pe.wait_ge(sel_in, 16 * (L + 1))
                    wait_taken(pe, (L, "qk", b, L))
                    hi, lo = ((kH, kL), (qH, qL))[i] if L else (qH, qL)
                    w = (2, 0)[i]
                    key = (L, "stack", G, i)
                    p = claim(key, "mi")
                    mm(p, sel[:, g, w, :], hi[:, :], start=True, stop=False)
                    filled(mm(p, sel[:, g, w + 1, :], lo[:, :], start=False, stop=True), key)

                def maxima(m, half, slots=("m0", "m1")):
                    G, qt = divmod(m, TPB)
                    if G >= NGB:
                        return
                    if qt == 0 and half == 0:
                        wait_taken(pe, (L, "stack", G, 1))
                    if qt == 0 and G >= 3:
                        pe.wait_ge(Kp_set, HPG * (L * KEYS + G - 3) + 2 * (half + 1))
                    for j in (2 * half, 2 * half + 1):
                        p = claim((L, "max", G, qt, j), slots[j % 2])
                        filled(mm(p, Qs[:, G % 3, qt * P:(qt + 1) * P], Kp[:, G % 3, j, :], start=True, stop=True),
                               (L, "max", G, qt, j))

                def place_maxima(G):
                    pe.wait_ge(MP_ready, L * NGB + G + 1)
                    p = claim((L, "mT", G), "mi")
                    for qt in range(TPB):
                        last = mm(p[:, qt * P:(qt + 1) * P], MP[:, qt, :, :].rearrange("p j s -> p (j s)"), ident_r[:, :],
                                  start=True, stop=True)
                    filled(last, (L, "mT", G))

                def scores(i, jp):
                    G, kt = divmod(i, TPB)
                    if kt == 0 and jp == 0:
                        wait_taken(pe, (L, "mT", G))
                    p = claim((L, "s", i, jp), f"s{jp}")
                    for j in range(2):
                        last = mm(p[:, j, :], Kp[:, G % 3, 2 * jp + j, kt * P:(kt + 1) * P], Qm[:, G % 2, :],
                                  start=True, stop=True)
                    filled(last, (L, "s", i, jp))

                def values(i):
                    G, kt = divmod(i, TPB)
                    b, g = divmod(G, NG)
                    if kt == 0:
                        claim((L, "pv", G), "pv")
                        wait_taken(pe, (L, "v", b))
                    p = ps("pv")
                    for jp in range(2):
                        wait_taken(pe, (L, "s", i, jp))
                    for j in range(HPG):
                        r = 2 * (i % 2) + j // 2
                        last = mm(p[SL * j:SL * j + VW, :], vaug[:, b, kt, g * HPG + j, :], E4[:, r, j % 2, :],
                                  start=(kt == 0), stop=(kt == TPB - 1), tile_position=(0, SL * j))
                    if kt < TPB - 1:
                        last.then_inc(pv_read, 1)
                    else:
                        filled(last, (L, "pv", G))

                def turn(G):
                    wait_taken(pe, (L, "pv", G))
                    transposes((L, "o", G), "mi", [OT[:, q * P:(q + 1) * P] for q in range(TPB)])

                def aoT_(b):
                    key = (L, "aoT", b)
                    p = claim(key, "m1" if L and b else "mi")
                    if L == 1:
                        mm(p, vsum[:, b, :], fe[:, :], start=True, stop=False)
                    wait_taken(pe, (L, "o", (b + 1) * NG - 1))
                    for q in range(TPB):
                        last = mm(p[:, q * P:(q + 1) * P], ao[:, q, :], ident,
                                  start=(L == 0), stop=(L == 0 or q == TPB - 1))
                    filled(last, key)

                def proj(b):
                    wait_taken(pe, (L, "aoT", b))
                    if L == 0:
                        filled(mm(claim(("mla", b), "mi"), la("wo0"), aoT, start=True, stop=True), ("mla", b))
                    else:
                        filled(mm(claim(("yT", b), "mi"), la("wout"), aoT, start=True, stop=True), ("yT", b))

                def y_(b):
                    p = claim(("y", b), "m0" if b else "mi")
                    for t in range(TPB):
                        last = mm(p[:, t * P:(t + 1) * P], aoT[:, t * P:(t + 1) * P], la("wout"), start=True, stop=True)
                    filled(last, ("y", b))

                def logits(b):
                    wait_taken(pe, ("mla" if L == 0 else "yT", b))
                    p = claim((L, "logits", b), "mi")
                    n, src, w = (EB, mlaT, "rb_w") if L == 0 else (EC, yT, "rc_w")
                    for t in range(TPB):
                        T = b * TPB + t
                        last = mm(p[:, t * n:(t + 1) * n], src[:, T * P:(T + 1) * P], la(w), start=True, stop=True)
                    filled(last, (L, "logits", b))
                    if L == 1 and b:
                        y_(b)

                def count(b):
                    pe.wait_ge(ohb_ready, b + 1)
                    pe.wait_ge(consts_b, 2)
                    p = claim(("count", b), "mi")
                    for t in range(TPB):
                        T = b * TPB + t
                        for u in range(T + 1):
                            last = mm(p[:, t * EC:(t + 1) * EC], before_b[:, :] if u == T else ones_b[:, :],
                                      ohb[:, u, :], start=(u == 0), stop=(u == T))
                    filled(last, ("count", b))

                def job(name, *at):
                    if name == "stackK":
                        stack(at[0], 0)
                    elif name == "stackQ":
                        stack(at[0], 1)
                    elif name == "max":
                        maxima(*at)
                    elif name not in ("stackK2", "place"):
                        {"y": y_, "logits": logits, "count": count, "weightsT": lambda b: weightsT("b", b),
                         "bias": lambda b: bias("b", b, la("b2b")), "cT": cT_, "qk": qk, "v": v, "tanh": tanh,
                         "coh": coh_, "vsum": vsum_, "turn": turn,
                         "maxT": place_maxima, "aoT": aoT_, "proj": proj}[name](*at)

                def main():
                    for i in range(STEPS):
                        scores(i, 0)
                        scores(i, 1)
                        for m in maxima_at(i, 0):
                            maxima(*m)
                        for k in jobs(L, i, 0):
                            job(*k)
                        if i:
                            values(i - 1)
                        for m in maxima_at(i, 1):
                            maxima(*m)
                        for k in jobs(L, i, 1):
                            job(*k)
                    if L == 1:
                        values(STEPS - 1)
                        keep_warm(3)
                        turn(NGB - 1)
                        keep_warm(4)
                        aoT_(B - 1)
                        keep_warm(3)
                        proj(B - 1)
                        keep_warm(3)

                return {"job": job, "main": main, "values": values}

            pe.wait_ge(early_in, 16)
            p = claim("gb", "mi")
            for b in range(B):
                a0 = EARLY_AT["cond_rep"][0] + b * P
                last = mm(p[:, b * EA:(b + 1) * EA], early[:, a0:a0 + P], ea("gg"), start=True, stop=True)
            filled(last, "gb")
            pe.wait_ge(xT_in, 16)

            def split(p, terms):
                for i, (wH, wL, cols, mH, mL) in enumerate(terms):
                    mm(p, wH[:, cols], mH, start=(i == 0), stop=False)
                    mm(p, wL[:, cols], mH, start=False, stop=False)
                    last = mm(p, wH[:, cols], mL, start=False, stop=(i == len(terms) - 1))
                return last

            def a_h1(n):
                b, e = divmod(n, EA)
                if e:
                    pe.wait_ge(wa_split, e)
                else:
                    pe.wait_ge(wa_split0, 1)
                pe.wait_ge(x_low_set, b + 1)
                p = claim(("a1", n), "s0")
                for c in range(2):
                    last = split(p[:, c, :], [(wa_high[e], wa_low[e], slice(c * P, (c + 1) * P), x_high[b], x_low[b])])
                filled(last, ("a1", n))

            def a_h2(n):
                e = n % EA
                pe.wait_ge(h1_low_set, n + 1)
                p = claim(("a2", n), "s1")
                for c in range(2):
                    o = MA + c * P
                    last = split(p[:, c, :], [(wa_high[e], wa_low[e], slice(o + k * MA, o + k * MA + P),
                                               h1_high[n % 2][:, k, :], h1_low[n % 2][:, k, :]) for k in range(2)])
                filled(last, ("a2", n))

            def a_out(n):
                e = n % EA
                wait_taken(pe, ("a2", n))
                p = claim(("a3", n), "m1" if n % 2 else "m0")
                for t in range(TPB):
                    for k in range(2):
                        o = 3 * MA + k * P
                        last = mm(p[:, t * P:(t + 1) * P], h2[:, k, t * P:(t + 1) * P], wa[:, e, o:o + P],
                                  start=(k == 0), stop=(k == 1))
                filled(last, ("a3", n))

            def weightsT(kind, b):
                pe.wait_ge(cw_ready, (b + 1) if kind == "a" else B + b + 1)
                transposes((kind, "cwT", b), "mi", [cw[:, b * TPB + t, :] for t in range(TPB)], n=EA)

            def bias(kind, b, rows):
                wait_taken(pe, (kind, "cwT", b))
                p = claim((kind, "bias", b), "pv" if kind == "a" else "mi")
                for t in range(TPB):
                    last = mm(p[:, t * P:(t + 1) * P], cwT[:, t * P:(t + 1) * P], rows[0:EA, :], start=True, stop=True)
                filled(last, (kind, "bias", b))

            def first_of(L, n, place, free):
                for name, *at in early_jobs[L].get((n, place), []):
                    if name == "max":
                        at.append(("m1" if free % 2 else "m0", "pv"))
                    (second if L else first)["job"](name, *at)

            pe.wait_ge(gate_w_ready, 1)
            p = claim("gl", "m0")
            for t in range(NT):
                last = mm(p[:, t * EA:(t + 1) * EA], xT[:, t * P:(t + 1) * P], wgs[:, :], start=True, stop=True)
            filled(last, "gl")
            a_h1(0)
            a_h1(1)
            a_h2(0)
            a_h1(2)
            a_out(0)
            a_h2(1)
            weightsT("a", 0)
            for n in range(2, NAB):
                if n == EA:
                    first = attention(0)
                if n + 1 < NAB:
                    a_h1(n + 1)
                if n < B + 2:
                    bias("a", n - 2, ea("b3a"))
                if 4 <= n < 9:
                    field(n - 4)
                a_out(n - 1)
                first_of(0, n, 0, n)
                a_h2(n)
                if n == 2:
                    weightsT("a", 1)
                first_of(0, n, 1, n + 1)
            a_out(NAB - 1)

            pe.wait_ge(consts_r, 1)
            first["main"]()

            pe.wait_ge(wb_split, EB)

            def b_h1(n):
                b, e = divmod(n, EB)
                pe.wait_ge(mla_split, b + 1)
                p = claim(("b1", n), f"s{n % 2}")
                m = slice(b * S, (b + 1) * S)
                for c in range(2):
                    last = split(p[:, c, :], [(wb_high[e], wb_low[e], slice(c * P, (c + 1) * P),
                                               mla_high[:, m], mla_low[:, m])])
                filled(last, ("b1", n))

            def b_out(n):
                e = n % EB
                wait_taken(pe, ("b1", n))
                hb = h1 if n % 2 == 0 else h2
                p = claim(("b2", n), "m1" if n % 2 else "m0")
                for t in range(TPB):
                    for k in range(2):
                        o = MB + k * P
                        last = mm(p[:, t * P:(t + 1) * P], hb[:, k, t * P:(t + 1) * P], wb[:, e, o:o + P],
                                  start=(k == 0), stop=(k == 1))
                filled(last, ("b2", n))

            second = attention(1)
            b_h1(0)
            first["values"](STEPS - 1)
            b_h1(1)
            for n in range(NAB):
                b_out(n)
                for k in late_jobs.get(n, []):
                    first["job"](*k)
                first_of(1, n, 0, n + 1)
                if n + 2 < NAB:
                    b_h1(n + 2)
                first_of(1, n, 1, n)
            second["main"]()
            second["job"]("logits", 1)
            second["job"]("count", 1)
            keep_warm(60)

            def turned(kind, q, src, n):
                tiles = 4 if kind == "pk" else 2
                transposes((kind, q), ("pv", "mi")[n % 2], [src[tiles * q + i] for i in range(tiles)])

            def c_h1(e):
                if e % 4 == 0:
                    pe.wait_ge(wc_in[e // 4], 16)
                wait_taken(pe, ("pk", ((e + 1) * CAP - 1) // ROWS))
                p = claim(("c1", e), f"s{e % 2}")
                for c in range(FC):
                    last = mm(p[:, c // 2, (c % 2) * CAP:(c % 2 + 1) * CAP], wc[e][:, c * P:(c + 1) * P],
                              pkT[:, e * CAP:(e + 1) * CAP], start=True, stop=True)
                filled(last, ("c1", e))

            def c_out(e):
                wait_taken(pe, ("c1", e))
                p = claim(("c2", e), "m1" if e % 2 else "m0")
                for c in range(FC):
                    o = MC + c * P
                    last = mm(p[:, 0:CAP], wc[e][:, o:o + P], hC[:, e % 2, c, :], start=(c == 0), stop=(c == FC - 1))
                filled(last, ("c2", e))

            turns = 0
            for kind, k in c_steps:
                if kind == "h1":
                    c_h1(k)
                elif kind == "out":
                    c_out(k)
                else:
                    if kind == "pk":
                        pe.wait_ge(pk_in[k], 16)
                        src = [pk_tok[:, t, 0:D] for t in range(NST)]
                    else:
                        e = ((k + 1) * EO_ROWS - 1) // CAP
                        wait_taken(pe, ("c2", e))
                        wait_taken(pe, ("c2", e - 1))
                        src = [eoT[:, t * P:(t + 1) * P] for t in range(NST)]
                    turned(kind, k, src, turns)
                    turns += 1

        @block.scalar
        def _(act):
            A = nc.scalar.activation

            def field(step):
                if step == 0:
                    p = wait_full(act, "field0")
                    A(rT[:, :], p[:, 0:B], ACT.Relu, bias=la("be1")).then_inc(field_rT, 1)
                    A(bc1c[:, :], p[:, B:2 * B], ACT.Identity, bias=la("bc1")).then_inc(taken["mi"], 1)
                elif step == 1:
                    act.wait_ge(field_var, 1)
                    A(fsd[:, 1:2], fsd[:, 0:1], ACT.Sqrt).then_inc(field_sd, 1)
                elif step == 3:
                    act.wait_ge(field_mx, 1)
                    p = wait_full(act, "field3")
                    A(fe[:, :], p[0:B, :], ACT.Exp, bias=fsd[:, 2:3], accum_out=fsd[:, 3:4]).then_inc(field_exp, 1)

            act.wait_ge(x_in, 16)
            for t in range(NT):
                last = A(squares[:, t, :], x_tok[:, t, :], ACT.Square, accum_out=ssq[:, t:t + 1])
            last.then_inc(ssq_done, 1)
            act.wait_ge(xT_in, 16)

            def x_high_(b):
                A(x_high[b], xT[:, b * S:(b + 1) * S], ACT.Copy).then_inc(x_high_set, 1)

            def wa_high_(e):
                act.wait_ge(wa_in[e], 16)
                A(wa_high[e], wa[:, e, 0:3 * MA], ACT.Copy).then_inc(wa_high_set, 1)

            x_high_(0)
            wa_high_(0)
            act.wait_ge(var_done, 1)
            A(rstd[:, :], ssq[:, :], ACT.Sqrt).then_inc(sd_done, 1)
            x_high_(1)
            wa_high_(1)
            act.wait_ge(shifted, 1)
            A(pr[:, :, 0:EA], lg[:, :, 0:EA], ACT.Exp).then_inc(expd, 1)
            def a_h1(n):
                p = wait_full(act, ("a1", n))
                e = n % EA
                if n >= 2:
                    act.wait_ge(h1_low_set, n - 1)
                for c in range(2):
                    o = EARLY_AT["b1a"][0] + 2 * e + c
                    last = A(h1_whole[n % 2][:, c, :], p[:, c, :], ACT.Relu, bias=early[:, o:o + 1])
                last.then_inc(taken["s0"], 1)
                wait_taken(act, ("a1", n))
                if n >= 2:
                    wait_full(act, ("a2", n - 2))
                A(h1_high[n % 2], h1_whole[n % 2][:, :, :], ACT.Copy).then_inc(h1_high_set, 1)

            def attention(L):
                def cT_(b):
                    p = wait_full(act, (L, "cT", b))
                    A(cT, p, ACT.Copy).then_inc(taken["mi"], 1)

                def qk(b, i):
                    p = wait_full(act, (L, "qk", b, i))
                    hi = kH if i else qH
                    A(hi[:, :], p, ACT.Identity, bias=la("bqk0" if L == 0 else ("bq1", "bk1")[i])).then_inc(H_done, 1)

                def tanh(b):
                    p = wait_full(act, ("tanh", b))
                    A(tT, p, ACT.Tanh, bias=bc1c[:, b:b + 1]).then_inc(taken["mi"], 1)

                def coh_(b):
                    wait_taken(act, ("coh", b))
                    A(coh[:, :, :], coh2[:, b, :, :], ACT.Exp, scale=-1.0).then_inc(coh_e, 1)

                def stackK(G, half):
                    if G >= 3:
                        if half == 0:
                            p = wait_full(act, (L, "stack", G, 0))
                            if L * KEYS + G > 4:
                                act.wait_ge(Kp_set, HPG * (L * KEYS + max(G - 4, 0)))
                            A(Ks[:, G % 2, :], p, ACT.Identity, bias=la("minus")).then_inc(taken["mi"], 1)
                        return
                    p = wait_full(act, (L, "stack", G, 0))
                    for j in (2 * half, 2 * half + 1):
                        r = slice(SL * j, SL * (j + 1))
                        last = A(Kp[r, G % 3, j, :], p[r, :], ACT.Identity, bias=la("minus")[r, :])
                    if half:
                        last.then_inc(taken["mi"], 1)

                def stackQ(G):
                    p = wait_full(act, (L, "stack", G, 1))
                    A(Qs[:, G % 3, :], p, ACT.Copy).then_inc(taken["mi"], 1)

                def exps(i, jp):
                    G, kt = divmod(i, TPB)
                    if jp == 0 and kt != 1 and i:
                        Gu, ku = divmod(i - 2, TPB)
                        act.wait_ge(pv_read, (L * NGB + Gu) * (TPB - 1) + ku + 1)
                    p = wait_full(act, (L, "s", i, jp))
                    A(E4[:, 2 * (i % 2) + jp, :, :], p, ACT.Exp, scale=float(HD[L]) ** -0.5).then_inc(taken[f"s{jp}"], 1)

                def take_values(G):
                    p = wait_full(act, (L, "pv", G))
                    A(OT, p, ACT.Copy).then_inc(taken["pv"], 1)

                def aoT_(b):
                    p = wait_full(act, (L, "aoT", b))
                    A(aoT, p, ACT.Copy).then_inc(taken[filled_at[(L, "aoT", b)][0]], 1)

                def proj(b):
                    if L == 0:
                        p = wait_full(act, ("mla", b))
                        A(mlaT[:, b * S:(b + 1) * S], p, ACT.Identity, bias=la("bo0")).then_inc(taken["mi"], 1)
                    else:
                        p = wait_full(act, ("yT", b))
                        A(yT[:, b * S:(b + 1) * S], p, ACT.Identity, bias=la("bout_col")).then_inc(taken["mi"], 1)

                def logits(b):
                    if L == 0:
                        act.wait_ge(shifted, 1 + b + 1)
                        T = slice(b * TPB, (b + 1) * TPB)
                        A(pr[:, T, 0:EB], lg[:, T, 0:EB], ACT.Exp).then_inc(expd, 1)

                def count(b):
                    act.wait_ge(gdiff, b + 1)
                    T = slice(b * TPB, (b + 1) * TPB)
                    A(gate[:, 1, T], gden[:, T], ACT.Exp).then_inc(gexp, 1)

                def job(name, *at):
                    if name in ("stackK", "stackK2"):
                        stackK(at[0], int(name == "stackK2"))
                    elif name in ("cT", "qk", "tanh", "coh", "stackQ", "aoT", "proj", "logits", "count"):
                        {"logits": logits, "count": count, "cT": cT_, "qk": qk, "tanh": tanh, "coh": coh_,
                         "stackQ": stackQ, "aoT": aoT_, "proj": proj}[name](*at)

                def main():
                    for i in range(STEPS):
                        exps(i, 0)
                        exps(i, 1)
                        for k in jobs(L, i, 0):
                            job(*k)
                        if i and i % TPB == 0:
                            take_values(i // TPB - 1)
                        for k in jobs(L, i, 1):
                            job(*k)
                    if L == 1:
                        take_values(NGB - 1)
                        aoT_(B - 1)
                        proj(B - 1)

                return {"job": job, "main": main, "take_values": take_values}

            first = attention(0)
            a_h1(0)
            wa_high_(2)
            for n in range(NAB):
                if n + 1 < NAB:
                    a_h1(n + 1)
                if n + 3 < EA:
                    wa_high_(n + 3)
                if 3 <= n < 8:
                    field(n - 3)
                for k in early_jobs[0].get((n, 0), []) + early_jobs[0].get((n, 1), []):
                    first["job"](*k)
            first["main"]()

            def b_h1(n):
                p = wait_full(act, ("b1", n))
                e = n % EB
                if n >= 2:
                    wait_full(act, ("b2", n - 2))
                hb = h1 if n % 2 == 0 else h2
                for c in range(2):
                    o = LATE_AT["b1b"][0] + 2 * e + c
                    last = A(hb[:, c, :], p[:, c, :], ACT.Gelu, bias=late[:, o:o + 1])
                last.then_inc(taken[f"s{n % 2}"], 1)

            second = attention(1)
            b_h1(0)
            first["take_values"](NGB - 1)
            b_h1(1)
            for n in range(NAB):
                for k in late_jobs.get(n, []):
                    first["job"](*k)
                for k in early_jobs[1].get((n, 0), []):
                    second["job"](*k)
                if n + 2 < NAB:
                    b_h1(n + 2)
                for k in early_jobs[1].get((n, 1), []):
                    second["job"](*k)
            second["main"]()
            second["job"]("logits", 1)
            second["job"]("count", 1)
            def c_h1(e):
                p = wait_full(act, ("c1", e))
                if e >= 2:
                    wait_full(act, ("c2", e - 2))
                for c in range(FC):
                    o = LATE_AT["b1c"][0] + FC * e + c
                    last = A(hC[:, e % 2, c, :], p[:, c // 2, (c % 2) * CAP:(c % 2 + 1) * CAP], ACT.Gelu,
                             bias=late[:, o:o + 1])
                last.then_inc(taken[f"s{e % 2}"], 1)

            for kind, k in c_steps:
                if kind == "h1":
                    c_h1(k)
                elif kind != "out" and k % 2:
                    p = wait_full(act, (kind, k))
                    if kind == "eo":
                        act.wait_ge(back_ready, k // 2 + 1)
                        p = p[:, 0:EO_ROWS]
                    to = pkT[:, k * ROWS:(k + 1) * ROWS] if kind == "pk" else \
                        eo_tok[:, 2 * k:2 * k + 2, :].rearrange("p t d -> p (t d)")
                    A(to, p, ACT.Copy).then_inc(taken[filled_at[(kind, k)][0]], 1)

        @block.vector
        def _(dve):
            V = nc.vector
            links = [0]

            def link(ins):
                links[0] += 1
                ins.then_inc(dve_chain, 1)
                dve.wait_ge(dve_chain, links[0])

            def wide(ap, n):
                return ap.unsqueeze(2).to_broadcast([ap.shape[0], ap.shape[1], n])

            def top2(E, p_or_l, tiles):
                T = slice(tiles[0], tiles[-1] + 1)
                for t in tiles:
                    last = V.max(top8[:, t, :], p_or_l[:, t, 0:E])
                link(last)
                for t in tiles:
                    last = V.max_index(idx8[:, t, :], top8[:, t, :], p_or_l[:, t, 0:E])
                link(last)
                link(V.tensor_copy(idxf[:, T, :], idx8[:, T, 0:2]))
                io = ea("iota")[:, 0:E].unsqueeze(1).to_broadcast([P, len(tiles), E])
                for k in range(2):
                    last = V.tensor_tensor(oh[:, k, T, 0:E], io, wide(idxf[:, T, k], E), ALU.is_equal)
                link(last)

            def softmax8(nth, tiles):
                T = slice(tiles[0], tiles[-1] + 1)
                link(V.reduce_max(rmx[:, T], lg[:, T, 0:8], AX.X))
                V.tensor_tensor(lg[:, T, 0:8], lg[:, T, 0:8], wide(rmx[:, T], 8), ALU.subtract).then_inc(shifted, 1)
                dve.wait_ge(expd, nth)
                link(V.reduce_sum(rsm[:, T], pr[:, T, 0:8], AX.X))
                link(V.reciprocal(rsm[:, T], rsm[:, T]))
                link(V.tensor_tensor(pr[:, T, 0:8], pr[:, T, 0:8], wide(rsm[:, T], 8), ALU.mult))

            dve.wait_ge(early_in, 16)
            V.tensor_copy(ident_r[:, :], ident).then_inc(consts_r, 1)
            V.tensor_scalar(wgs[:, :], ea("wg"), ea("rms"), None, ALU.mult).then_inc(gate_w_ready, 1)
            dve.wait_ge(ssq_done, 1)
            V.tensor_scalar(ssq[:, :], ssq[:, :], 1.0 / D, 1e-6, ALU.mult, ALU.add).then_inc(var_done, 1)
            p = wait_full(dve, "gb")
            pv = p[:, 0:B * EA].rearrange("p (b e) -> p b e", b=B)
            V.tensor_tensor(gbias[:, :, :], pv, ea("gg_b").unsqueeze(1).to_broadcast([P, B, EA]),
                            ALU.add).then_inc(taken["mi"], 1)
            dve.wait_ge(taken["mi"], 1)
            link(V.tensor_tensor(gbias[:, :, :], gbias[:, :, :], ea("wg_b").unsqueeze(1).to_broadcast([P, B, EA]),
                                 ALU.add))
            def x_low_(b):
                dve.wait_ge(x_high_set, b + 1)
                V.tensor_tensor(x_low[b], xT[:, b * S:(b + 1) * S], x_high[b], ALU.subtract).then_inc(x_low_set, 1)

            x_low_(0)
            dve.wait_ge(wa_high_set, 1)
            V.tensor_tensor(wa_low[0], wa[:, 0, 0:3 * MA], wa_high[0], ALU.subtract).then_inc(wa_split0, 1)
            dve.wait_ge(sd_done, 1)
            link(V.reciprocal(rstd[:, :], rstd[:, :]))
            p = wait_full(dve, "gl")
            pv = p[:, 0:NT * EA].rearrange("p (t e) -> p t e", e=EA)
            V.tensor_tensor(lg[:, :, 0:EA], pv, wide(rstd[:, :], EA), ALU.mult).then_inc(taken["m0"], 1)
            dve.wait_ge(taken["m0"], 1)
            for b in range(B):
                last = V.tensor_tensor(lg[:, b * TPB:(b + 1) * TPB, 0:EA], lg[:, b * TPB:(b + 1) * TPB, 0:EA],
                                       gbias[:, b, :].unsqueeze(1).to_broadcast([P, TPB, EA]), ALU.add)
            link(last)
            softmax8(1, range(NT))
            top2(EA, pr, range(NT))
            link(V.tensor_tensor(cw[:, :, :], oh[:, 0, :, 0:EA], oh[:, 1, :, 0:EA], ALU.add))
            V.tensor_tensor(cw[:, :, :], cw[:, :, :], pr[:, :, 0:EA], ALU.mult).then_inc(cw_ready, B)

            def h2_out(n):
                p = wait_full(dve, ("a2", n))
                e = n % EA
                for c in range(2):
                    o = EARLY_AT["b2a"][0] + 2 * e + c
                    last = V.tensor_scalar(h2[:, c, :], p[:, c, :], early[:, o:o + 1], 0.0, ALU.add, ALU.max)
                last.then_inc(taken["s1"], 1)

            acc_at = {}

            def combine(kind, n, acc):
                b, e = divmod(n, 8)
                key = ("a3" if kind == "a" else "b2", n)
                p = wait_full(dve, key)
                if e:
                    dve.wait_ge(*acc_at[kind, n - 1])
                for t in range(TPB):
                    T = b * TPB + t
                    last = V.scalar_tensor_tensor(acc[:, T, :], p[:, t * P:(t + 1) * P], cw[:, T, e:e + 1], acc[:, T, :],
                                                  ALU.mult, ALU.add)
                last.then_inc(taken[filled_at[key][0]], 1)
                s, k = filled_at[key]
                acc_at[kind, n] = (taken[s], k)

            def weightsT(kind, b):
                p = wait_full(dve, (kind, "cwT", b))
                V.tensor_copy(cwT[:, :], p[0:EA, :]).then_inc(taken["mi"], 1)

            def bias(kind, b, acc):
                p = wait_full(dve, (kind, "bias", b))
                a = acc[:, b * TPB:(b + 1) * TPB, :].rearrange("p t d -> p (t d)")
                if kind == "a":
                    V.tensor_copy(a, p).then_inc(taken[filled_at[(kind, "bias", b)][0]], 1)
                else:
                    dve.wait_ge(x_cond_set, 1)
                    V.tensor_tensor(a, a, p, ALU.add).then_inc(taken[filled_at[(kind, "bias", b)][0]], 1)
                wait_taken(dve, (kind, "bias", b))

            def field(step):
                if step == 1:
                    p = wait_full(dve, "field1")
                    V.tensor_tensor(fz[:, :], p[0:B, 0:P], la("be2")[0:B, :], ALU.add).then_inc(taken["mi"], 1)
                    wait_taken(dve, "field1")
                    link(V.bn_stats(fst[:, :], fz[:, :]))
                    link(V.bn_aggr(fag[:, :], fst[:, :]))
                    V.tensor_scalar(fsd[:, 0:1], fag[:, 1:2], 1e-5, None, ALU.add).then_inc(field_var, 1)
                elif step == 2:
                    dve.wait_ge(field_sd, 1)
                    link(V.reciprocal(fsd[:, 2:3], fsd[:, 1:2]))
                    link(V.tensor_scalar(fz[:, :], fz[:, :], fag[:, 0:1], fsd[:, 2:3], ALU.subtract, ALU.mult))
                    link(V.tensor_tensor(fz[:, :], fz[:, :], la("ln_g")[0:B, :], ALU.mult))
                    V.tensor_tensor(fz[:, :], fz[:, :], la("ln_b")[0:B, :], ALU.add).then_inc(field_fp, 1)
                    p = wait_full(dve, "field2")
                    V.tensor_copy(fpT[:, :], p[:, 0:B]).then_inc(taken["mi"], 1)
                elif step == 3:
                    p = wait_full(dve, "field3")
                    V.tensor_reduce(fsd[:, 2:3], p[0:B, :], AX.X, ALU.max, negate=True).then_inc(field_mx, 1)
                    dve.wait_ge(field_exp, 1)
                    link(V.reciprocal(fsd[:, 3:4], fsd[:, 3:4]))
                    V.tensor_scalar(fe[:, :], fe[:, :], fsd[:, 3:4], FI, ALU.mult, ALU.mult).then_inc(taken["mi"], 1)

            def attention(L):
                hd = HD[L]

                def qk(b, i):
                    p = wait_full(dve, (L, "qk", b, i))
                    dve.wait_ge(H_done, (b + 1) if L == 0 else B + 2 * b + i + 1)
                    hi, lo = (kH, kL) if i else (qH, qL)
                    bias = la("bqk0" if L == 0 else ("bq1", "bk1")[i])
                    V.scalar_tensor_tensor(lo[:, :], p, bias, hi[:, :], ALU.add, ALU.subtract).then_inc(taken["mi"], 1)

                def v(b):
                    p = wait_full(dve, (L, "v", b))
                    if L == 0 and b == 0:
                        dve.wait_ge(clear0, 1)
                    pvv = p.rearrange("p (t c) -> p t c", t=TPB)[:, :, 0:H * hd]
                    for t in range(TPB):
                        last = V.tensor_tensor(vaug[:, b, t, :, 0:hd], pvv[:, t, :].rearrange("p (h d) -> p h d", d=hd),
                                               la("bv0" if L == 0 else "bv1").rearrange("p (h d) -> p h d", d=hd), ALU.add)
                    last.then_inc(taken["mi"], 1)

                def coh_(b):
                    p = wait_full(dve, ("coh", b))
                    V.tensor_tensor(coh2[:, b, :, :], p[:, 0:TPB * H].rearrange("p (t h) -> p t h", h=H),
                                    la("bc2").unsqueeze(1).to_broadcast([P, TPB, H]), ALU.add).then_inc(taken["mi"], 1)

                def vsum_(b):
                    p = wait_full(dve, ("vsum", b))
                    V.tensor_scalar(vsum[:, b, :], p[0:B, 0:P], ident[0:B, b:b + 1], None,
                                    ALU.mult).then_inc(taken["mi"], 1)
                    dve.wait_ge(coh_e, b + 1)
                    link(V.tensor_scalar(coh[:, :, :], coh[:, :, :], 1e-8 / (1.0 - FI), (1.0 + 1e-8) / (1.0 - FI),
                                         ALU.mult, ALU.add))
                    link(V.reciprocal(coh2[:, b, :, :], coh[:, :, :]))

                def maxima(m, half):
                    G, qt = divmod(m, TPB)
                    if G >= NGB:
                        return
                    for j in (2 * half, 2 * half + 1):
                        key = (L, "max", G, qt, j)
                        p = wait_full(dve, key)
                        V.reduce_max(mx[:, G % 2, qt, j:j + 1], p, AX.X).then_inc(taken[filled_at[key][0]], 1)

                def place(G):
                    if L == 0 and G == 0:
                        dve.wait_ge(clear0, 1)
                    for j in (HPG - 2, HPG - 1):
                        wait_taken(dve, (L, "max", G, TPB - 1, j))
                    link(V.tensor_copy(MP[:, :, :, 0], mx[:, G % 2, :, :]))
                    V.tensor_tensor(MP[:, :, :, 1], mx[:, G % 2, :, :], MP[:, :, :, 0], ALU.subtract).then_inc(MP_ready, 1)

                def put_maxima(G):
                    p = wait_full(dve, (L, "mT", G))
                    V.tensor_tensor(Qm[:, G % 2, :], p, Qs[:, G % 3, :], ALU.add).then_inc(taken["mi"], 1)

                def norm(G):
                    b, g = divmod(G, NG)
                    p = wait_full(dve, (L, "o", G))
                    o = p.rearrange("p (t j s) -> p t j s", t=TPB, j=HPG)
                    link(V.reciprocal(rden[:, :, :], o[:, :, :, hd]))
                    if L == 1:
                        link(V.tensor_tensor(rden[:, :, :], rden[:, :, :], coh2[:, b, :, g * HPG:(g + 1) * HPG], ALU.mult))
                    if L == 0 and G == 0:
                        dve.wait_ge(zeroed, 32)
                    a = ao[:, :, :].rearrange("p t (h d) -> p t h d", d=hd)
                    for t in range(TPB):
                        last = V.tensor_tensor(a[:, t, g * HPG:(g + 1) * HPG, :], o[:, t, :, 0:hd], wide(rden[:, t, :], hd),
                                               ALU.mult)
                    last.then_inc(taken["mi"], 1)

                def y_(b):
                    p = wait_full(dve, ("y", b))
                    V.tensor_tensor(y[:, b * TPB:(b + 1) * TPB, :], p.rearrange("p (t d) -> p t d", t=TPB),
                                    la("bout").unsqueeze(1).to_broadcast([P, TPB, D]), ALU.add).then_inc(
                        taken[filled_at[("y", b)][0]], 1)

                def logits(b):
                    tiles = range(b * TPB, (b + 1) * TPB)
                    T = slice(b * TPB, (b + 1) * TPB)
                    n, rb = ((EB, "rb_b"), (EC, "rc_b"))[L]
                    p = wait_full(dve, (L, "logits", b))
                    V.tensor_tensor(lg[:, T, 0:n], p[:, 0:TPB * n].rearrange("p (t e) -> p t e", e=n),
                                    la(rb).unsqueeze(1).to_broadcast([P, TPB, n]), ALU.add).then_inc(taken["mi"], 1)
                    wait_taken(dve, (L, "logits", b))
                    if L == 0:
                        softmax8(2 + b, tiles)
                        top2(EB, pr, tiles)
                        link(V.tensor_tensor(rsm[:, T], top8[:, T, 0], top8[:, T, 1], ALU.add))
                        link(V.tensor_scalar(rsm[:, T], rsm[:, T], 1e-8, 1.0 / 0.3, ALU.add, ALU.mult))
                        link(V.reciprocal(rsm[:, T], rsm[:, T]))
                        link(V.tensor_tensor(cw[:, T, :], oh[:, 0, T, 0:EB], oh[:, 1, T, 0:EB], ALU.add))
                        link(V.tensor_tensor(cw[:, T, :], cw[:, T, :], pr[:, T, 0:EB], ALU.mult))
                        V.tensor_tensor(cw[:, T, :], cw[:, T, :], wide(rsm[:, T], EB), ALU.mult).then_inc(cw_ready, 1)
                    else:
                        top2(EC, lg, tiles)
                        V.tensor_tensor(ohb[:, T, :], oh[:, 0, T, :], oh[:, 1, T, :], ALU.add).then_inc(ohb_ready, 1)
                        V.tensor_tensor(gden[:, T], top8[:, T, 1], top8[:, T, 0], ALU.subtract).then_inc(gdiff, 1)
                        if b:
                            y_(b)

                def count(b):
                    T = slice(b * TPB, (b + 1) * TPB)
                    p = wait_full(dve, ("count", b))[:, 0:TPB * EC].rearrange("p (t e) -> p t e", e=EC)
                    V.tensor_tensor(lg[:, T, :], oh[:, 0, T, :], p, ALU.mult)
                    V.tensor_tensor(pr[:, T, :], oh[:, 1, T, :], p, ALU.mult).then_inc(taken["mi"], 1)
                    wait_taken(dve, ("count", b))
                    V.reduce_sum(pos[:, 0, T], lg[:, T, :], AX.X)
                    link(V.reduce_sum(pos[:, 1, T], pr[:, T, :], AX.X))
                    for k in range(2):
                        last = V.scalar_tensor_tensor(slot[:, k, T], idxf[:, T, k], float(CAP), pos[:, k, T],
                                                      ALU.mult, ALU.add)
                    link(last)
                    link(V.tensor_scalar(kept[:, :, T], pos[:, :, T], float(CAP), None, ALU.is_lt))
                    link(V.tensor_scalar(pos[:, :, T], kept[:, :, T], -2.0 * NSLOT, 2.0 * NSLOT, ALU.mult, ALU.add))
                    link(V.tensor_tensor(pos[:, :, T], pos[:, :, T], slot[:, :, T], ALU.add))
                    V.tensor_copy(put_at[:, :, T], pos[:, :, T]).then_inc(put_ready, 1)
                    dve.wait_ge(gexp, b + 1)
                    link(V.tensor_scalar(gden[:, T], gate[:, 1, T], 1.0, None, ALU.add))
                    link(V.reciprocal(gate[:, 0, T], gden[:, T]))
                    link(V.tensor_tensor(gate[:, 1, T], gate[:, 1, T], gate[:, 0, T], ALU.mult))
                    link(V.tensor_tensor(gate[:, :, T], gate[:, :, T], kept[:, :, T], ALU.mult))
                    link(V.tensor_tensor(gden[:, T], gate[:, 0, T], gate[:, 1, T], ALU.add))
                    link(V.tensor_scalar(gden[:, T], gden[:, T], 1e-9, None, ALU.add))
                    link(V.reciprocal(gden[:, T], gden[:, T]))
                    for k in range(2):
                        last = V.tensor_tensor(gate[:, k, T], gate[:, k, T], gden[:, T], ALU.mult)
                    link(last)

                def job(name, *at):
                    if name == "max":
                        maxima(*at)
                    elif name == "place":
                        place(*at)
                    elif name in ("logits", "count", "weightsT", "bias", "qk", "v", "coh", "vsum", "turn", "maxT", "y"):
                        {"y": y_, "logits": logits, "count": count, "weightsT": lambda b: weightsT("b", b),
                         "bias": lambda b: bias("b", b, x1), "qk": qk, "v": v, "coh": coh_, "vsum": vsum_,
                         "turn": norm, "maxT": put_maxima}[name](*at)

                def main():
                    for i in range(STEPS):
                        G, kt = divmod(i, TPB)
                        if kt == (TPB - 2 if G else TPB - 1) and G + 1 < NGB:
                            place(G + 1)
                        for m in maxima_at(i, 0):
                            maxima(*m)
                        for k in jobs(L, i, 0):
                            job(*k)
                        for m in maxima_at(i, 1):
                            maxima(*m)
                        for k in jobs(L, i, 1):
                            job(*k)
                    if L == 1:
                        norm(NGB - 1)

                return {"job": job, "main": main}

            first = attention(0)
            x_low_(1)
            h2_out(0)
            h2_out(1)
            weightsT("a", 0)
            for n in range(2, NAB):
                if n < B + 2:
                    bias("a", n - 2, c0)
                if n == 2:
                    combine("a", 0, c0)
                combine("a", n - 1, c0)
                for k in early_jobs[0].get((n, 0), []):
                    first["job"](*k)
                h2_out(n)
                if n == 2:
                    weightsT("a", 1)
                if 3 <= n < 8:
                    field(n - 3)
                for k in early_jobs[0].get((n, 1), []):
                    first["job"](*k)
            combine("a", NAB - 1, c0)
            V.tensor_copy(before_b[:, :], la("before")).then_inc(consts_b, 1)
            V.tensor_copy(ones_b[:, :], la("ones")).then_inc(consts_b, 1)
            first["main"]()

            second = attention(1)
            for n in range(NAB):
                combine("b", n, x1)
                for k in late_jobs.get(n, []):
                    first["job"](*k)
                if n == 7:
                    V.memset(vaug[:, :, :, :, HD[1]:HD[1] + 1], 1.0)
                for k in early_jobs[1].get((n, 0), []) + early_jobs[1].get((n, 1), []):
                    second["job"](*k)
            second["main"]()
            second["job"]("logits", 1)
            second["job"]("count", 1)
            for kind, k in c_steps:
                if kind == "out":
                    p = wait_full(dve, ("c2", k))
                    o = LATE_AT["b2c"][0] + k
                    V.tensor_scalar(eoT[:, k * CAP:(k + 1) * CAP], p[:, 0:CAP], late[:, o:o + 1], None, ALU.add).then_inc(
                        taken[filled_at[("c2", k)][0]], 1)
                if kind == "pk":
                    dve.wait_ge(pk_in[k], 16)
                    V.tensor_copy(back_at[:, 4 * k:4 * k + 4], pk_tok[:, 4 * k:4 * k + 4, D]).then_inc(back_ready, 1)
                if kind in ("pk", "eo") and k % 2 == 0:
                    p = wait_full(dve, (kind, k))
                    if kind == "eo":
                        dve.wait_ge(back_ready, k // 2 + 1)
                        p = p[:, 0:EO_ROWS]
                    to = pkT[:, k * ROWS:(k + 1) * ROWS] if kind == "pk" else \
                        eo_tok[:, 2 * k:2 * k + 2, :].rearrange("p t d -> p (t d)")
                    V.tensor_copy(to, p).then_inc(taken[filled_at[(kind, k)][0]], 1)
            for c in range(NT // 2):
                dve.wait_ge(got_in[c], 16)
                for k in range(2):
                    for t in (2 * c, 2 * c + 1):
                        last = V.scalar_tensor_tensor(x1[:, t, :], got[:, t, k, :], gate[:, k, t:t + 1], x1[:, t, :],
                                                      ALU.mult, ALU.add)
                    if k == 0:
                        link(last)
                last.then_inc(out_ready, 1)

        @block.sync
        def _(sp):
            sp.dma_start(early[:, :], early_d).then_inc(early_in, 16)
            sp.dma_start(x_tok[:, :, :], x_tok_d).then_inc(x_in, 16)
            sp.dma_start(xT[:, :], xT_d).then_inc(xT_in, 16)
            for e in range(EA):
                sp.dma_start(wa[:, e, :], wa_d[:, e, :]).then_inc(wa_in[e], 16)
            sp.dma_start(late[:, :], late_d).then_inc(late_in, 16)
            sp.wait_ge(zero_ready, 3)
            blank = ao[:, :, :].rearrange("p t d -> p (t d)")
            sp.dma_start(packed_d.rearrange("(t p) c -> p t c", p=P),
                         blank[:, 0:ROW].unsqueeze(1).to_broadcast([P, NST, ROW])).then_inc(zeroed, 16)
            sp.dma_start(pair_d.rearrange("(r p) d -> p r d", p=P),
                         blank[:, 2 * D:3 * D].unsqueeze(1).to_broadcast([P, NPAIR // P, D])).then_inc(zeroed, 16)
            sp.dma_start(wb[:, :, :], wb_d).then_inc(wb_in, 16)
            wait_taken(sp, ("a3", NAB - 1))
            for q in (0, 1):
                sp.dma_start(wa[:, 4 * q:4 * q + 4, :], wc_d[:, 4 * q:4 * q + 4, :]).then_inc(wc_in[q], 16)
            wait_taken(sp, (1, "pv", B * NG - 1))
            for q in (2, 3):
                sp.dma_start(wc_late[:, 4 * q - 8:4 * q - 4, :], wc_d[:, 4 * q:4 * q + 4, :]).then_inc(wc_in[q], 16)
            sp.wait_ge(putted, 16 * 2 * NT)
            for q in range(NQ):
                sp.dma_start(pk_tok[:, 4 * q:4 * q + 4, :],
                             packed_d.rearrange("(t p) c -> p t c", p=P)[:, 4 * q:4 * q + 4, :]).then_inc(pk_in[q], 16)
            sp.wait_ge(eo_out, 16 * NST)
            for c in range(NT // 2):
                sp.dma_start(got[:, 2 * c:2 * c + 2, :, :].rearrange("p t k d -> p t (k d)"),
                             pair_d.rearrange("(t p k) d -> p t (k d)", p=P, k=2)[:, 2 * c:2 * c + 2, :]
                             ).then_inc(got_in[c], 16)
            for c in range(NT // 2):
                sp.wait_ge(out_ready, c + 1)
                sp.dma_start(out_d[:, 2 * c:2 * c + 2, :], x1[:, 2 * c:2 * c + 2, :]).then_inc(out_done, 16)
            sp.wait_ge(out_done, 16 * NT // 2)

        @block.gpsimd
        def _(pool):
            blank = ao[:, :, :].rearrange("p t d -> p (t d)")
            nc.gpsimd.memset(blank[:, 0:D], 0.0).then_inc(zero_ready, 1)
            nc.gpsimd.memset(blank[:, D:ROW], float(2 * NPAIR)).then_inc(zero_ready, 1)
            nc.gpsimd.memset(blank[:, ROW:], 0.0).then_inc(zero_ready, 1)
            nc.gpsimd.memset(Kp[:, :, :, :].rearrange("p a j s -> p (a j s)").bitcast(F32), 0.0)

            def part_wa(e):
                pool.wait_ge(wa_high_set, e + 1)
                nc.gpsimd.tensor_tensor(wa_low[e], wa[:, e, 0:3 * MA], wa_high[e], ALU.subtract).then_inc(wa_split, 1)

            part_wa(1)
            for n in range(NAB):
                pool.wait_ge(h1_high_set, n + 1)
                if n >= 2:
                    wait_full(pool, ("a2", n - 2))
                nc.gpsimd.tensor_tensor(h1_low[n % 2], h1_whole[n % 2][:, :, :], h1_high[n % 2],
                                        ALU.subtract).then_inc(h1_low_set, 1)
                if n == 0:
                    part_wa(2)
                if n + 3 < EA:
                    part_wa(n + 3)
                if n + 2 == EA:
                    nc.gpsimd.memset(MP[:, :, :, :].rearrange("p a j s -> p (a j s)").bitcast(F32), 0.0)
                    nc.gpsimd.memset(vaug[:, :, :, :, :], 0.0).then_inc(pool_clear, 1)
                    pool.wait_ge(pool_clear, 1)
                    nc.gpsimd.memset(vaug[:, :, :, :, HD[0]:HD[0] + 1], 1.0).then_inc(clear0, 1)
                    pool.dma_start(sel[:, :, :, :].rearrange("p g w s -> p (g w s)"), sel_d[:, 0, :]).then_inc(sel_in, 16)
            for n in (NAB - 2, NAB - 1):
                wait_taken(pool, ("a3", n))
            nc.gpsimd.tensor_tensor(x1[:, :, :], x_tok[:, :, :], c0[:, :, :], ALU.add).then_inc(x_cond_set, 1)
            wait_full(pool, ("a2", NAB - 1))
            pool.wait_ge(wb_in, 16)
            for e in range(EB):
                nc.gpsimd.tensor_copy(wb_high[e], wb[:, e, 0:MB]).then_inc(wb_high_set, 1)
            for e in range(EB):
                pool.wait_ge(wb_high_set, e + 1)
                nc.gpsimd.tensor_tensor(wb_low[e], wb[:, e, 0:MB], wb_high[e], ALU.subtract).then_inc(wb_split, 1)

            def part_mla(b):
                m = slice(b * S, (b + 1) * S)
                wait_taken(pool, ("mla", b))
                nc.gpsimd.tensor_copy(mla_high[:, m], mlaT[:, m]).then_inc(mla_high_set, 1)
                pool.wait_ge(mla_high_set, b + 1)
                nc.gpsimd.tensor_tensor(mla_low[:, m], mlaT[:, m], mla_high[:, m], ALU.subtract).then_inc(mla_split, 1)

            def place_keys(L):
                for G in range(3, NGB):
                    wait_taken(pool, (L, "stack", G, 0))
                    for j in range(HPG):
                        rows = slice(SL * j, SL * (j + 1))
                        nc.gpsimd.tensor_copy(Kp[rows, G % 3, j, :], Ks[rows, G % 2, :]).then_inc(Kp_set, 1)
                        pool.wait_ge(Kp_set, HPG * (L * KEYS + G - 3) + j + 1)

            pool.wait_ge(wb_split, EB)
            place_keys(0)
            part_mla(0)
            wait_full(pool, (0, "stack", B * NG - 1, 1))
            pool.dma_start(sel[:, :, :, :].rearrange("p g w s -> p (g w s)"), sel_d[:, 1, :]).then_inc(sel_in, 16)
            part_mla(1)
            pool.wait_ge(zeroed, 32)
            for n in (NAB - 2, NAB - 1):
                wait_taken(pool, ("b2", n))
            nc.gpsimd.tensor_copy(to_pack[:, :, :, D], la("pair").rearrange("p (k t) -> p k t", k=2)
                                  ).then_inc(pack_ready, 1)
            pool.wait_ge(pack_ready, 1)
            place_keys(1)
            for b in range(B):
                T = slice(b * TPB, (b + 1) * TPB)
                wait_taken(pool, ("y", b))
                nc.gpsimd.tensor_copy(to_pack[:, 1, T, 0:D], y[:, T, :]).then_inc(pack_ready, 1)
                pool.wait_ge(put_ready, b + 1)
                pool.wait_ge(pack_ready, b + 2)
                for t in range(b * TPB, (b + 1) * TPB):
                    for k in range(2):
                        pool.indirect_dma_start(out=packed_d,
                                                out_offset=bass.IndirectOffsetOnAxis(ap=put_at[:, k, t:t + 1], axis=0),
                                                in_=to_pack[:, k, t, :], in_offset=None, bounds_check=NSLOT - 1,
                                                oob_is_err=False).then_inc(putted, 16)
            for q in range(2 * NQ):
                pool.wait_ge(back_ready, q // 2 + 1)
                wait_taken(pool, ("eo", q))
                for t in (2 * q, 2 * q + 1):
                    pool.indirect_dma_start(out=pair_d,
                                            out_offset=bass.IndirectOffsetOnAxis(ap=back_at[:, t:t + 1], axis=0),
                                            in_=eo_tok[:, t, :], in_offset=None, bounds_check=NPAIR - 1,
                                            oob_is_err=False).then_inc(eo_out, 16)


def kernel(**inputs):
    import numpy as np
    import concourse.bacc as bacc
    from concourse.bass_utils import run_bass_kernel_spmd

    a = {k: np.asarray(v) for k, v in inputs.items()}
    f4 = np.float32

    def rows(m):
        m = np.asarray(m, f4)
        out = np.zeros((P, m.shape[1]), f4)
        out[:m.shape[0]] = m
        return out

    def rep(v):
        return np.broadcast_to(np.asarray(v, f4).reshape(1, -1), (P, v.size))

    def cols(v):
        return np.asarray(v, f4).reshape(-1, P).T

    x = a["x"].reshape(B * S, D)
    cond = a["cond_256"]
    q_w = a["L0_ffn_q_w"].reshape(D, H, D // H)[:, :, :HD[0]].reshape(D, H * HD[0])
    q_b = a["L0_ffn_q_b"].reshape(H, D // H)[:, :HD[0]].reshape(-1)
    wqkv, bqkv = a["L1_cond_Wqkv"], a["L1_cond_bqkv"]
    wc1 = a["L1_cond_Wc1"]
    s_, e_ = np.arange(S, dtype=f4), np.arange(0, D, 2, dtype=f4)
    inv = f4(10000.0) ** np.repeat(e_ / f4(D), 2)
    early = {
        "wg": a["L0_cond_wg_W"], "rms": cols(a["L0_cond_rms_w"]), "gg": rows(a["L0_cond_gg_W"]),
        "cond_rep": rows(np.repeat(cond.T[:, :, None], P, axis=2).reshape(CD, B * P)),
        "wg_b": rep(a["L0_cond_wg_b"]), "gg_b": rep(a["L0_cond_gg_b"]),
        "b1a": cols(a["L0_cond_b1"]), "b2a": cols(a["L0_cond_b2"]), "b3a": rows(a["L0_cond_b3"]),
        "cond": rows(cond.T), "iota": rep(np.arange(EC, dtype=f4)), "ident": np.eye(P, dtype=f4),
    }
    minus = np.zeros((P, 1), f4)
    for j in range(HPG):
        minus[SL * j:SL * j + 2] = -1.0
    late = {
        "wqk0": np.concatenate([q_w, a["L0_ffn_k_w"]], 1), "bqk0": cols(np.concatenate([q_b, a["L0_ffn_k_b"]])),
        "wv0": a["L0_ffn_v_w"], "bv0": rep(a["L0_ffn_v_b"]), "wo0": a["L0_ffn_o_w"], "bo0": cols(a["L0_ffn_o_b"]),
        "rb_w": a["L0_ffn_router_w"], "rb_b": rep(a["L0_ffn_router_b"]), "b1b": cols(a["L0_ffn_b1"]),
        "b2b": rows(a["L0_ffn_b2"]),
        "wq1": wqkv[0:D].T, "wk1": wqkv[D:2 * D].T, "wv1": wqkv[2 * D:3 * D].T,
        "bq1": cols(bqkv[0:D]), "bk1": cols(bqkv[D:2 * D]), "bv1": rep(bqkv[2 * D:3 * D]),
        "wc1x": wc1[:, :D].T, "wc1c": rows(wc1[:, D:].T), "bc1": cols(a["L1_cond_bc1"]),
        "wc2": a["L1_cond_Wc2"].T, "bc2": rep(a["L1_cond_bc2"]),
        "we1": rows(a["L1_cond_We1"].T), "be1": cols(a["L1_cond_be1"]), "we2": a["L1_cond_We2"].T,
        "be2": rep(a["L1_cond_be2"]), "ln_g": rep(a["L1_cond_ln_g"]), "ln_b": rep(a["L1_cond_ln_b"]),
        "pe": np.sin(s_[:, None] / inv[None, :]).T,
        "wout": a["L1_cond_Wout"].T, "bout_col": cols(a["L1_cond_bout"]), "bout": rep(a["L1_cond_bout"]),
        "rc_w": a["L1_ffn_router_w"].T, "rc_b": rep(a["L1_ffn_router_b"]),
        "b1c": cols(a["L1_ffn_b1"]), "b2c": cols(a["L1_ffn_b2"]),
        "before": np.triu(np.ones((P, P), f4), 1), "ones": np.ones((P, P), f4), "minus": minus,
        "pair": (2 * (np.arange(NT)[None, None, :] * P + np.arange(P)[:, None, None])
                 + np.arange(2)[None, :, None]).reshape(P, 2 * NT).astype(f4),
    }
    sel = np.zeros((P, 2, NG, 4, P), f4)
    for L in range(2):
        for g in range(NG):
            for j in range(HPG):
                for d in range(HD[L]):
                    q = (g * HPG + j) * HD[L] + d
                    k = q + (H * HD[0] if L == 0 else 0)
                    s0, s1, s2 = (SL * j + 2 + i * HD[L] + d for i in range(3))
                    sel[q, L, g, 0, [s0, s1]] = 1
                    sel[q, L, g, 1, s2] = 1
                    sel[k, L, g, 2, [s0, s2]] = 1
                    sel[k, L, g, 3, s1] = 1

    def chunks(w):
        e, k, n = w.shape
        return w.reshape(e, k // P, P, n).transpose(2, 0, 1, 3).reshape(P, e, -1)

    arrays = {
        "x_tok": x.reshape(NT, P, D).transpose(1, 0, 2), "xT": x.T,
        "early": np.concatenate([early[n] for n, _ in EARLY], 1),
        "late": np.concatenate([late[n] for n, _ in LATE], 1),
        "sel": sel.reshape(P, 2, -1),
        "wa": np.concatenate([chunks(a[f"L0_cond_W{i}"]) for i in (1, 2, 3)], 2),
        "wb": np.concatenate([chunks(a[f"L0_ffn_w{i}"]) for i in (1, 2)], 2),
        "wc": np.concatenate([chunks(a[f"L1_ffn_w{i}"]) for i in (1, 2)], 2),
    }
    arrays = {k + "_dram": np.ascontiguousarray(v) for k, v in arrays.items()}
    nc = bacc.Bacc("TRN2", target_bir_lowering=False, num_devices=1)
    args = [nc.dram_tensor(k, v.shape, mybir.dt.from_np(v.dtype), kind="ExternalInput").ap() for k, v in arrays.items()]
    out = nc.dram_tensor("out_dram", (P, NT, D), mybir.dt.float32, kind="ExternalOutput").ap()
    build(nc, *args, out)
    r = run_bass_kernel_spmd(nc, [arrays], core_ids=[0])
    got = r.results[0]["out_dram"]
    return np.ascontiguousarray(got.transpose(1, 0, 2)).reshape(B, S, D)
```
